# Optimizing a Trainium2 kernel written in Bass

```python
import numpy as np
import jax
import jax.numpy as jnp

def _softmax(x, axis=-1):
    return jax.nn.softmax(x, axis=axis)

def _gelu(x):
    return jax.nn.gelu(x, approximate=True)

def _silu(x):
    return jax.nn.silu(x)

def _sigmoid(x):
    return jax.nn.sigmoid(x)

def _layernorm(x, axis=-1, eps=1e-05):
    m = jnp.mean(x, axis=axis, keepdims=True)
    v = jnp.var(x, axis=axis, keepdims=True)
    return (x - m) / jnp.sqrt(v + eps)

def _scatter_add(tgt, idx, src, axis=0):
    return tgt.at[idx].add(src)

def _segment_sum(src, seg, n):
    return jax.ops.segment_sum(src, seg, n)
kernel_name = 'mk_gps_d2_gnn_r16_ea223b'

def setup_inputs(seed: int=0):
    np.random.seed(seed)
    _w = jnp.asarray

    def _rec_inputs():
        import jax
        import jax.numpy as jnp
        _gk = jax.random.key(seed)
        x = -0.0002117 + 1 * jax.random.normal(jax.random.fold_in(_gk, 1), (3125, 256), jnp.float32)
        src = jax.random.randint(jax.random.fold_in(_gk, 2), (100000,), 0, 3125, jnp.int32)
        dst = jax.random.randint(jax.random.fold_in(_gk, 3), (100000,), 0, 3125, jnp.int32)
        _o = jnp.argsort(dst, stable=True)
        src = src[_o]
        dst = dst[_o]
        edge_attr_64 = 1.36993e-05 + 0.999972 * jax.random.normal(jax.random.fold_in(_gk, 13), (100000, 64), jnp.float32)
        edge_weight = jax.random.uniform(jax.random.fold_in(_gk, 15), (100000,), jnp.float32, 0.0, 1)
        return (x, src, dst, edge_attr_64, edge_weight)
    x, src, dst, edge_attr_64, edge_weight = _rec_inputs()

    def _L0_gnn_setup():
        import jax, jax.numpy as jnp
        import numpy as np
        BN_EPS = 1e-05

        def _batchnorm(h, gamma, beta):
            mean = jnp.mean(h, axis=0, keepdims=True)
            var = jnp.var(h, axis=0, keepdims=True)
            return (h - mean) * jax.lax.rsqrt(var + BN_EPS) * gamma + beta
        key = jax.random.key(seed)
        ks = jax.random.split(key, 10)
        N, E, D = (6250, 200000, 256)
        x = jax.random.normal(ks[0], (N, D), dtype=jnp.float32)
        edge_src = jax.random.randint(ks[1], (E,), 0, N, dtype=jnp.int32)
        edge_dst = jax.random.randint(ks[2], (E,), 0, N, dtype=jnp.int32)
        edge_vals = jnp.ones((E,), dtype=jnp.float32)
        n_norm = jax.random.uniform(ks[3], (N, 1), dtype=jnp.float32)
        s = 1.0 / np.sqrt(D)
        w1 = jax.random.uniform(ks[4], (D, D), jnp.float32, -s, s)
        gamma1 = jnp.ones((D,), jnp.float32)
        beta1 = jnp.zeros((D,), jnp.float32)
        w2 = jax.random.uniform(ks[5], (D, D), jnp.float32, -s, s)
        eps_weight = jnp.zeros((1,), jnp.float32)
        gamma_h = jnp.ones((D,), jnp.float32)
        beta_h = jnp.zeros((D,), jnp.float32)
        return {'x': x, 'edge_src': edge_src, 'edge_dst': edge_dst, 'edge_vals': edge_vals, 'n_norm': n_norm, 'w1': w1, 'gamma1': gamma1, 'beta1': beta1, 'w2': w2, 'eps_weight': eps_weight, 'gamma_h': gamma_h, 'beta_h': beta_h}
    _L0_gnn_all = _L0_gnn_setup()
    _L0_gnn_in = {k: v for k, v in _L0_gnn_all.items() if k in ('w1', 'gamma1', 'beta1', 'w2', 'eps_weight', 'gamma_h', 'beta_h')}
    del _L0_gnn_all

    def _L0_mix_setup():
        import jax, jax.numpy as jnp
        import numpy as np
        HEADS = 4
        DIM_HEAD = 32
        key = jax.random.key(seed)
        k1, k2, k3 = jax.random.split(key, 3)
        B, L, D = (16, 512, 256)
        hidden = HEADS * DIM_HEAD
        x = jax.random.normal(k1, (B, L, D), dtype=jnp.float32)
        W_qkv = jax.random.normal(k2, (D, 3 * hidden), dtype=jnp.float32) * D ** (-0.5)
        W_out = jax.random.normal(k3, (hidden, D), dtype=jnp.float32) * hidden ** (-0.5)
        b_out = jnp.zeros((D,), dtype=jnp.float32)
        return {'x': x, 'W_qkv': W_qkv, 'W_out': W_out, 'b_out': b_out}
    _L0_mix_all = _L0_mix_setup()
    _L0_mix_in = {k: v for k, v in _L0_mix_all.items() if k in ('W_qkv', 'W_out', 'b_out')}
    del _L0_mix_all

    def _L0_ffn_setup():
        import jax, jax.numpy as jnp
        import numpy as np
        D_MODEL = 256
        EXPERT_DIM = 512
        NUM_EXPERTS = 8
        TOP_K = 2
        SEQ_LEN = 128
        BATCH = 2
        key = jax.random.key(seed)
        ks = jax.random.split(key, 8)
        s = 0.02
        x = jax.random.normal(ks[0], (SEQ_LEN, BATCH, D_MODEL), dtype=jnp.float32)
        Wg = jax.random.normal(ks[1], (D_MODEL, NUM_EXPERTS), dtype=jnp.float32) * s
        bg = jax.random.normal(ks[2], (NUM_EXPERTS,), dtype=jnp.float32) * s
        bias = jnp.zeros((NUM_EXPERTS,), dtype=jnp.float32)
        W1 = jax.random.normal(ks[3], (NUM_EXPERTS, D_MODEL, EXPERT_DIM), dtype=jnp.float32) * s
        b1 = jax.random.normal(ks[4], (NUM_EXPERTS, EXPERT_DIM), dtype=jnp.float32) * s
        W2 = jax.random.normal(ks[5], (NUM_EXPERTS, EXPERT_DIM, D_MODEL), dtype=jnp.float32) * s
        b2 = jax.random.normal(ks[6], (NUM_EXPERTS, D_MODEL), dtype=jnp.float32) * s
        return {'x': x, 'Wg': Wg, 'bg': bg, 'bias': bias, 'W1': W1, 'b1': b1, 'W2': W2, 'b2': b2}
    _L0_ffn_all = _L0_ffn_setup()
    _L0_ffn_in = {k: v for k, v in _L0_ffn_all.items() if k in ('Wg', 'bg', 'bias', 'W1', 'b1', 'W2', 'b2')}
    del _L0_ffn_all

    def _L1_gnn_setup():
        import jax, jax.numpy as jnp
        import numpy as np
        N = 1250
        E = 20000
        D = 256
        H = 8
        DH = D // H
        ED = 64
        FF = 4 * D
        EPS = 1e-05

        def _layernorm(x, g, b):
            m = jnp.mean(x, axis=-1, keepdims=True)
            v = jnp.var(x, axis=-1, keepdims=True)
            return (x - m) * jax.lax.rsqrt(v + EPS) * g + b

        def _edge_attention(xn, edge_index, ef, ew, Wq, bq, Wk, bk, Wv, bv, We, be, Wo, bo):
            n = xn.shape[0]
            scale = DH ** (-0.5)
            q = (xn @ Wq + bq).reshape(n, H, DH)
            k = (xn @ Wk + bk).reshape(n, H, DH)
            v = (xn @ Wv + bv).reshape(n, H, DH)
            src, dst = (edge_index[0], edge_index[1])
            ep = ef @ We + be
            scores = jnp.einsum('ehd,ehd->eh', q[dst], k[src] + ep[:, None, :]) * scale
            scores = scores * ew[:, None]
            m = jax.ops.segment_max(scores, dst, num_segments=n)
            m = jnp.where(jnp.isfinite(m), m, 0.0)
            ex = jnp.exp(scores - m[dst])
            s = jax.ops.segment_sum(ex, dst, num_segments=n)
            attn = ex / s[dst]
            out = jax.ops.segment_sum(attn[:, :, None] * v[src], dst, num_segments=n)
            out = out.reshape(n, D) @ Wo + bo
            return out
        key = jax.random.key(seed)
        ks = jax.random.split(key, 32)

        def lin_w(k, i, o):
            return (jax.random.normal(k, (i, o), jnp.float32) / np.sqrt(i)).astype(jnp.float32)
        return {'x': jax.random.normal(ks[0], (N, D), jnp.float32), 'edge_features': jax.random.normal(ks[1], (E, ED), jnp.float32), 'edge_weights': jax.random.uniform(ks[2], (E,), jnp.float32), 'edge_index': jax.random.randint(ks[3], (2, E), 0, N, dtype=jnp.int32), 'Wq': lin_w(ks[4], D, D), 'bq': jnp.zeros((D,), jnp.float32), 'Wk': lin_w(ks[5], D, D), 'bk': jnp.zeros((D,), jnp.float32), 'Wv': lin_w(ks[6], D, D), 'bv': jnp.zeros((D,), jnp.float32), 'We': lin_w(ks[7], ED, DH), 'be': jnp.zeros((DH,), jnp.float32), 'Wo': lin_w(ks[8], D, D), 'bo': jnp.zeros((D,), jnp.float32), 'ln1_g': jnp.ones((D,), jnp.float32), 'ln1_b': jnp.zeros((D,), jnp.float32), 'ln2_g': jnp.ones((D,), jnp.float32), 'ln2_b': jnp.zeros((D,), jnp.float32), 'W1': lin_w(ks[9], D, FF), 'b1': jnp.zeros((FF,), jnp.float32), 'W2': lin_w(ks[10], FF, D), 'b2': jnp.zeros((D,), jnp.float32), 'alpha': jnp.ones((1,), jnp.float32), 'beta': jnp.ones((1,), jnp.float32)}
    _L1_gnn_all = _L1_gnn_setup()
    _L1_gnn_in = {k: v for k, v in _L1_gnn_all.items() if k in ('Wq', 'bq', 'Wk', 'bk', 'Wv', 'bv', 'We', 'be', 'Wo', 'bo', 'ln1_g', 'ln1_b', 'ln2_g', 'ln2_b', 'W1', 'b1', 'W2', 'b2', 'alpha', 'beta')}
    del _L1_gnn_all

    def _L1_mix_setup():
        import jax, jax.numpy as jnp
        import numpy as np
        D_MODEL = 256
        NHEAD = 8
        D_HEAD = D_MODEL // NHEAD
        DIM_FF = 1024
        B, L = (4, 1024)
        LN_EPS = 1e-05

        def _layernorm(x, g, b):
            mu = jnp.mean(x, axis=-1, keepdims=True)
            var = jnp.mean((x - mu) ** 2, axis=-1, keepdims=True)
            return (x - mu) * jax.lax.rsqrt(var + LN_EPS) * g + b

        def _phi(x):
            return jnp.where(x > 0, x + 1.0, jnp.exp(x))
        key = jax.random.key(seed)
        ks = jax.random.split(key, 16)
        s_in = 1.0 / np.sqrt(D_MODEL)
        s_ff = 1.0 / np.sqrt(DIM_FF)
        inp = {'x': jax.random.normal(ks[0], (B, L, D_MODEL), dtype=jnp.float32), 'Wq': jax.random.normal(ks[1], (D_MODEL, D_MODEL), dtype=jnp.float32) * s_in, 'bq': jnp.zeros((D_MODEL,), jnp.float32), 'Wk': jax.random.normal(ks[2], (D_MODEL, D_MODEL), dtype=jnp.float32) * s_in, 'bk': jnp.zeros((D_MODEL,), jnp.float32), 'Wv': jax.random.normal(ks[3], (D_MODEL, D_MODEL), dtype=jnp.float32) * s_in, 'bv': jnp.zeros((D_MODEL,), jnp.float32), 'Wo': jax.random.normal(ks[4], (D_MODEL, D_MODEL), dtype=jnp.float32) * s_in, 'bo': jnp.zeros((D_MODEL,), jnp.float32), 'W1': jax.random.normal(ks[5], (D_MODEL, DIM_FF), dtype=jnp.float32) * s_in, 'b1': jnp.zeros((DIM_FF,), jnp.float32), 'W2': jax.random.normal(ks[6], (DIM_FF, D_MODEL), dtype=jnp.float32) * s_ff, 'b2': jnp.zeros((D_MODEL,), jnp.float32), 'ln1_g': jnp.ones((D_MODEL,), jnp.float32), 'ln1_b': jnp.zeros((D_MODEL,), jnp.float32), 'ln2_g': jnp.ones((D_MODEL,), jnp.float32), 'ln2_b': jnp.zeros((D_MODEL,), jnp.float32)}
        return inp
    _L1_mix_all = _L1_mix_setup()
    _L1_mix_in = {k: v for k, v in _L1_mix_all.items() if k in ('Wq', 'bq', 'Wk', 'bk', 'Wv', 'bv', 'Wo', 'bo', 'W1', 'b1', 'W2', 'b2', 'ln1_g', 'ln1_b', 'ln2_g', 'ln2_b')}
    del _L1_mix_all

    def _L1_ffn_setup():
        import math
        import jax, jax.numpy as jnp
        import numpy as np
        CAPACITY_FACTOR = 1.25
        TOP_K = 2
        LN_EPS = 1e-05

        def _layer_norm(x, gamma, beta):
            mu = jnp.mean(x, axis=-1, keepdims=True)
            var = jnp.var(x, axis=-1, keepdims=True)
            return (x - mu) * jax.lax.rsqrt(var + LN_EPS) * gamma + beta
        key = jax.random.key(seed)
        ks = jax.random.split(key, 4)
        B, S, D, F, E = (8, 256, 256, 512, 8)
        x = jax.random.normal(ks[0], (B, S, D), dtype=jnp.float32)
        Wr = jax.random.normal(ks[1], (D, E), dtype=jnp.float32) / np.sqrt(D)
        br = jnp.zeros((E,), jnp.float32)
        W1 = jax.random.normal(ks[2], (E, D, F), dtype=jnp.float32) / np.sqrt(D)
        b1 = jnp.zeros((E, F), jnp.float32)
        W2 = jax.random.normal(ks[3], (E, F, D), dtype=jnp.float32) / np.sqrt(F)
        b2 = jnp.zeros((E, D), jnp.float32)
        gamma = jnp.ones((D,), jnp.float32)
        beta = jnp.zeros((D,), jnp.float32)
        return {'x': x, 'Wr': Wr, 'br': br, 'W1': W1, 'b1': b1, 'W2': W2, 'b2': b2, 'gamma': gamma, 'beta': beta}
    _L1_ffn_all = _L1_ffn_setup()
    _L1_ffn_in = {k: v for k, v in _L1_ffn_all.items() if k in ('Wr', 'br', 'W1', 'b1', 'W2', 'b2', 'gamma', 'beta')}
    del _L1_ffn_all
    return {'x': x, 'src': src, 'dst': dst, 'edge_attr_64': edge_attr_64, 'edge_weight': edge_weight, 'L0_gnn_w1': _L0_gnn_in['w1'], 'L0_gnn_gamma1': _L0_gnn_in['gamma1'], 'L0_gnn_beta1': _L0_gnn_in['beta1'], 'L0_gnn_w2': _L0_gnn_in['w2'], 'L0_gnn_eps_weight': _L0_gnn_in['eps_weight'], 'L0_gnn_gamma_h': _L0_gnn_in['gamma_h'], 'L0_gnn_beta_h': _L0_gnn_in['beta_h'], 'L0_mix_W_qkv': _L0_mix_in['W_qkv'], 'L0_mix_W_out': _L0_mix_in['W_out'], 'L0_mix_b_out': _L0_mix_in['b_out'], 'L0_ffn_Wg': _L0_ffn_in['Wg'], 'L0_ffn_bg': _L0_ffn_in['bg'], 'L0_ffn_bias': _L0_ffn_in['bias'], 'L0_ffn_W1': _L0_ffn_in['W1'], 'L0_ffn_b1': _L0_ffn_in['b1'], 'L0_ffn_W2': _L0_ffn_in['W2'], 'L0_ffn_b2': _L0_ffn_in['b2'], 'L1_gnn_Wq': _L1_gnn_in['Wq'], 'L1_gnn_bq': _L1_gnn_in['bq'], 'L1_gnn_Wk': _L1_gnn_in['Wk'], 'L1_gnn_bk': _L1_gnn_in['bk'], 'L1_gnn_Wv': _L1_gnn_in['Wv'], 'L1_gnn_bv': _L1_gnn_in['bv'], 'L1_gnn_We': _L1_gnn_in['We'], 'L1_gnn_be': _L1_gnn_in['be'], 'L1_gnn_Wo': _L1_gnn_in['Wo'], 'L1_gnn_bo': _L1_gnn_in['bo'], 'L1_gnn_ln1_g': _L1_gnn_in['ln1_g'], 'L1_gnn_ln1_b': _L1_gnn_in['ln1_b'], 'L1_gnn_ln2_g': _L1_gnn_in['ln2_g'], 'L1_gnn_ln2_b': _L1_gnn_in['ln2_b'], 'L1_gnn_W1': _L1_gnn_in['W1'], 'L1_gnn_b1': _L1_gnn_in['b1'], 'L1_gnn_W2': _L1_gnn_in['W2'], 'L1_gnn_b2': _L1_gnn_in['b2'], 'L1_gnn_alpha': _L1_gnn_in['alpha'], 'L1_gnn_beta': _L1_gnn_in['beta'], 'L1_mix_Wq': _L1_mix_in['Wq'], 'L1_mix_bq': _L1_mix_in['bq'], 'L1_mix_Wk': _L1_mix_in['Wk'], 'L1_mix_bk': _L1_mix_in['bk'], 'L1_mix_Wv': _L1_mix_in['Wv'], 'L1_mix_bv': _L1_mix_in['bv'], 'L1_mix_Wo': _L1_mix_in['Wo'], 'L1_mix_bo': _L1_mix_in['bo'], 'L1_mix_W1': _L1_mix_in['W1'], 'L1_mix_b1': _L1_mix_in['b1'], 'L1_mix_W2': _L1_mix_in['W2'], 'L1_mix_b2': _L1_mix_in['b2'], 'L1_mix_ln1_g': _L1_mix_in['ln1_g'], 'L1_mix_ln1_b': _L1_mix_in['ln1_b'], 'L1_mix_ln2_g': _L1_mix_in['ln2_g'], 'L1_mix_ln2_b': _L1_mix_in['ln2_b'], 'L1_ffn_Wr': _L1_ffn_in['Wr'], 'L1_ffn_br': _L1_ffn_in['br'], 'L1_ffn_W1': _L1_ffn_in['W1'], 'L1_ffn_b1': _L1_ffn_in['b1'], 'L1_ffn_W2': _L1_ffn_in['W2'], 'L1_ffn_b2': _L1_ffn_in['b2'], 'L1_ffn_gamma': _L1_ffn_in['gamma'], 'L1_ffn_beta': _L1_ffn_in['beta']}

def reference(x, src, dst, edge_attr_64, edge_weight, L0_gnn_w1, L0_gnn_gamma1, L0_gnn_beta1, L0_gnn_w2, L0_gnn_eps_weight, L0_gnn_gamma_h, L0_gnn_beta_h, L0_mix_W_qkv, L0_mix_W_out, L0_mix_b_out, L0_ffn_Wg, L0_ffn_bg, L0_ffn_bias, L0_ffn_W1, L0_ffn_b1, L0_ffn_W2, L0_ffn_b2, L1_gnn_Wq, L1_gnn_bq, L1_gnn_Wk, L1_gnn_bk, L1_gnn_Wv, L1_gnn_bv, L1_gnn_We, L1_gnn_be, L1_gnn_Wo, L1_gnn_bo, L1_gnn_ln1_g, L1_gnn_ln1_b, L1_gnn_ln2_g, L1_gnn_ln2_b, L1_gnn_W1, L1_gnn_b1, L1_gnn_W2, L1_gnn_b2, L1_gnn_alpha, L1_gnn_beta, L1_mix_Wq, L1_mix_bq, L1_mix_Wk, L1_mix_bk, L1_mix_Wv, L1_mix_bv, L1_mix_Wo, L1_mix_bo, L1_mix_W1, L1_mix_b1, L1_mix_W2, L1_mix_b2, L1_mix_ln1_g, L1_mix_ln1_b, L1_mix_ln2_g, L1_mix_ln2_b, L1_ffn_Wr, L1_ffn_br, L1_ffn_W1, L1_ffn_b1, L1_ffn_W2, L1_ffn_b2, L1_ffn_gamma, L1_ffn_beta):
    import jax
    import jax.numpy as jnp

    def _L0_gnn_ref(x, edge_src, edge_dst, edge_vals, n_norm, w1, gamma1, beta1, w2, eps_weight, gamma_h, beta_h):
        import jax, jax.numpy as jnp
        import numpy as np
        BN_EPS = 1e-05

        def _batchnorm(h, gamma, beta):
            mean = jnp.mean(h, axis=0, keepdims=True)
            var = jnp.var(h, axis=0, keepdims=True)
            return (h - mean) * jax.lax.rsqrt(var + BN_EPS) * gamma + beta
        N = x.shape[0]
        msgs = edge_vals[:, None] * x[edge_src]
        agg = jax.ops.segment_sum(msgs, edge_dst, num_segments=N)
        y = agg + eps_weight * x
        h = jax.nn.relu(_batchnorm(y @ w1.T, gamma1, beta1))
        y = h @ w2.T
        y = y * n_norm
        y = _batchnorm(y, gamma_h, beta_h)
        y = jax.nn.relu(y)
        y = y + x
        return y

    def _L0_mix_ref(x, W_qkv, W_out, b_out):
        import jax, jax.numpy as jnp
        import numpy as np
        HEADS = 4
        DIM_HEAD = 32
        B, L, D = x.shape
        scale = DIM_HEAD ** (-0.5)
        qkv = jnp.einsum('bld,df->blf', x, W_qkv)
        qkv = qkv.reshape(B, L, 3, HEADS, DIM_HEAD)
        q = jnp.transpose(qkv[:, :, 0], (0, 2, 1, 3)) * scale
        k = jax.nn.softmax(jnp.transpose(qkv[:, :, 1], (0, 2, 1, 3)), axis=2)
        v = jnp.transpose(qkv[:, :, 2], (0, 2, 1, 3))
        context = jnp.einsum('bhld,bhle->bhde', k, v)
        out = jnp.einsum('bhde,bhld->bhle', context, q)
        out = jnp.transpose(out, (0, 2, 1, 3)).reshape(B, L, HEADS * DIM_HEAD)
        return jnp.einsum('blf,fd->bld', out, W_out) + b_out

    def _L0_ffn_ref(x, Wg, bg, bias, W1, b1, W2, b2):
        import jax, jax.numpy as jnp
        import numpy as np
        D_MODEL = 256
        EXPERT_DIM = 512
        NUM_EXPERTS = 8
        TOP_K = 2
        SEQ_LEN = 128
        BATCH = 2
        x_flat = x.reshape(-1, D_MODEL)
        gate_logits = x_flat @ Wg + bg + bias
        topk_vals, topk_idx = jax.lax.top_k(gate_logits, TOP_K)
        topk_w = jax.nn.softmax(topk_vals, axis=-1)
        combine = (jax.nn.one_hot(topk_idx, NUM_EXPERTS, dtype=x.dtype) * topk_w[..., None]).sum(axis=1)
        h = jax.nn.relu(jnp.einsum('td,edh->teh', x_flat, W1) + b1)
        y = jnp.einsum('teh,ehd->ted', h, W2) + b2
        out = jnp.einsum('ted,te->td', y, combine)
        return out.reshape(x.shape)

    def _L1_gnn_ref(x, edge_features, edge_weights, edge_index, Wq, bq, Wk, bk, Wv, bv, We, be, Wo, bo, ln1_g, ln1_b, ln2_g, ln2_b, W1, b1, W2, b2, alpha, beta):
        import jax, jax.numpy as jnp
        import numpy as np
        N = 1250
        E = 20000
        D = 256
        H = 8
        DH = D // H
        ED = 64
        FF = 4 * D
        EPS = 1e-05

        def _layernorm(x, g, b):
            m = jnp.mean(x, axis=-1, keepdims=True)
            v = jnp.var(x, axis=-1, keepdims=True)
            return (x - m) * jax.lax.rsqrt(v + EPS) * g + b

        def _edge_attention(xn, edge_index, ef, ew, Wq, bq, Wk, bk, Wv, bv, We, be, Wo, bo):
            n = xn.shape[0]
            scale = DH ** (-0.5)
            q = (xn @ Wq + bq).reshape(n, H, DH)
            k = (xn @ Wk + bk).reshape(n, H, DH)
            v = (xn @ Wv + bv).reshape(n, H, DH)
            src, dst = (edge_index[0], edge_index[1])
            ep = ef @ We + be
            scores = jnp.einsum('ehd,ehd->eh', q[dst], k[src] + ep[:, None, :]) * scale
            scores = scores * ew[:, None]
            m = jax.ops.segment_max(scores, dst, num_segments=n)
            m = jnp.where(jnp.isfinite(m), m, 0.0)
            ex = jnp.exp(scores - m[dst])
            s = jax.ops.segment_sum(ex, dst, num_segments=n)
            attn = ex / s[dst]
            out = jax.ops.segment_sum(attn[:, :, None] * v[src], dst, num_segments=n)
            out = out.reshape(n, D) @ Wo + bo
            return out
        xn = _layernorm(x, ln1_g, ln1_b)
        attn_out = _edge_attention(xn, edge_index, edge_features, edge_weights, Wq, bq, Wk, bk, Wv, bv, We, be, Wo, bo)
        x = x + alpha * attn_out
        xn = _layernorm(x, ln2_g, ln2_b)
        ff = jax.nn.gelu(xn @ W1 + b1, approximate=False) @ W2 + b2
        x = x + beta * ff
        return x

    def _L1_mix_ref(x, Wq, bq, Wk, bk, Wv, bv, Wo, bo, W1, b1, W2, b2, ln1_g, ln1_b, ln2_g, ln2_b):
        import jax, jax.numpy as jnp
        import numpy as np
        D_MODEL = 256
        NHEAD = 8
        D_HEAD = D_MODEL // NHEAD
        DIM_FF = 1024
        B, L = (4, 1024)
        LN_EPS = 1e-05

        def _layernorm(x, g, b):
            mu = jnp.mean(x, axis=-1, keepdims=True)
            var = jnp.mean((x - mu) ** 2, axis=-1, keepdims=True)
            return (x - mu) * jax.lax.rsqrt(var + LN_EPS) * g + b

        def _phi(x):
            return jnp.where(x > 0, x + 1.0, jnp.exp(x))
        Bq, Lq, _ = x.shape
        q = (x @ Wq + bq).reshape(Bq, Lq, NHEAD, D_HEAD)
        k = (x @ Wk + bk).reshape(Bq, Lq, NHEAD, D_HEAD)
        v = (x @ Wv + bv).reshape(Bq, Lq, NHEAD, D_HEAD)
        q_phi = _phi(q)
        k_phi = _phi(k)
        kv = jnp.einsum('blhd,blhe->bhde', k_phi, v)
        k_sum = k_phi.sum(axis=1)
        z = 1.0 / (jnp.einsum('blhd,bhd->blh', q_phi, k_sum) + 1e-06)
        out = jnp.einsum('blhd,bhde,blh->blhe', q_phi, kv, z)
        out = out.reshape(Bq, Lq, D_MODEL) @ Wo + bo
        x = _layernorm(x + out, ln1_g, ln1_b)
        ff = jax.nn.relu(x @ W1 + b1) @ W2 + b2
        x = _layernorm(x + ff, ln2_g, ln2_b)
        return x

    def _L1_ffn_ref(x, Wr, br, W1, b1, W2, b2, gamma, beta):
        import math
        import jax, jax.numpy as jnp
        import numpy as np
        CAPACITY_FACTOR = 1.25
        TOP_K = 2
        LN_EPS = 1e-05

        def _layer_norm(x, gamma, beta):
            mu = jnp.mean(x, axis=-1, keepdims=True)
            var = jnp.var(x, axis=-1, keepdims=True)
            return (x - mu) * jax.lax.rsqrt(var + LN_EPS) * gamma + beta
        B, S, D = x.shape
        E = Wr.shape[1]
        N = B * S
        K = TOP_K
        logits = jnp.mean(x, axis=1) @ Wr + br
        routing_weights = jax.nn.softmax(logits, axis=-1)
        capacity = float(math.ceil(N * CAPACITY_FACTOR / E))
        expected_loads = routing_weights.sum(axis=0) * (N / B)
        scale = jnp.where(expected_loads > capacity, capacity / expected_loads, 1.0)
        routing_weights = jax.nn.softmax(routing_weights * scale, axis=-1)
        rw_tok = jnp.broadcast_to(routing_weights[:, None, :], (B, S, E)).reshape(N, E)
        top_w, top_i = jax.lax.top_k(rw_tok, K)
        top_w = jax.nn.softmax(top_w, axis=-1)
        xf = x.reshape(N, D)
        h = jax.nn.gelu(jnp.einsum('nd,edf->enf', xf, W1) + b1[:, None, :], approximate=False)
        y = jnp.einsum('enf,efd->end', h, W2) + b2[:, None, :]
        w_dense = jnp.zeros((N, E), x.dtype).at[jnp.arange(N)[:, None], top_i].add(top_w)
        out = jnp.einsum('ne,end->nd', w_dense, y).reshape(B, S, D)
        out = _layer_norm(out + x, gamma, beta)
        return out
    edge_index = jnp.stack([src, dst])
    deg = jnp.maximum(jax.ops.segment_sum(jnp.ones(dst.shape, jnp.float32), dst, num_segments=3125), 1.0)
    deg_isqrt = deg ** (-0.5)
    xn = _layernorm(x, axis=-1)
    x = x + _L0_gnn_ref(xn, src, dst, edge_weight, deg_isqrt[:, None], L0_gnn_w1, L0_gnn_gamma1, L0_gnn_beta1, L0_gnn_w2, L0_gnn_eps_weight, L0_gnn_gamma_h, L0_gnn_beta_h) + _L0_mix_ref(xn[None], L0_mix_W_qkv, L0_mix_W_out, L0_mix_b_out)[0]
    x = x + _L0_ffn_ref(_layernorm(x, axis=-1)[None], L0_ffn_Wg, L0_ffn_bg, L0_ffn_bias, L0_ffn_W1, L0_ffn_b1, L0_ffn_W2, L0_ffn_b2)[0]
    xn = _layernorm(x, axis=-1)
    x = x + _L1_gnn_ref(xn, edge_attr_64, edge_weight, edge_index, L1_gnn_Wq, L1_gnn_bq, L1_gnn_Wk, L1_gnn_bk, L1_gnn_Wv, L1_gnn_bv, L1_gnn_We, L1_gnn_be, L1_gnn_Wo, L1_gnn_bo, L1_gnn_ln1_g, L1_gnn_ln1_b, L1_gnn_ln2_g, L1_gnn_ln2_b, L1_gnn_W1, L1_gnn_b1, L1_gnn_W2, L1_gnn_b2, L1_gnn_alpha, L1_gnn_beta) + _L1_mix_ref(xn[None], L1_mix_Wq, L1_mix_bq, L1_mix_Wk, L1_mix_bk, L1_mix_Wv, L1_mix_bv, L1_mix_Wo, L1_mix_bo, L1_mix_W1, L1_mix_b1, L1_mix_W2, L1_mix_b2, L1_mix_ln1_g, L1_mix_ln1_b, L1_mix_ln2_g, L1_mix_ln2_b)[0]
    x = x + _L1_ffn_ref(_layernorm(x, axis=-1)[None], L1_ffn_Wr, L1_ffn_br, L1_ffn_W1, L1_ffn_b1, L1_ffn_W2, L1_ffn_b2, L1_ffn_gamma, L1_ffn_beta)[0]
    return x

_drawn_inputs = setup_inputs


def setup_inputs(seed=0):
    import zlib

    import numpy as np

    out = dict(_drawn_inputs(seed))
    spreads = {'L0_gnn_gamma1': (1.0, 0.2),
     'L0_gnn_beta1': (0.0, 0.28),
     'L0_gnn_gamma_h': (1.0, 0.2),
     'L0_gnn_beta_h': (0.0, 0.1),
     'L0_mix_b_out': (0.0, 0.1),
     'L0_ffn_bias': (0.0, 0.354),
     'L1_gnn_bq': (0.0, 0.8),
     'L1_gnn_bk': (0.0, 2.0),
     'L1_gnn_bv': (0.0, 0.27),
     'L1_gnn_be': (0.0, 2.0),
     'L1_gnn_bo': (0.0, 0.294),
     'L1_gnn_ln1_g': (1.0, 0.561),
     'L1_gnn_ln1_b': (0.0, 0.1),
     'L1_gnn_ln2_g': (1.0, 0.2),
     'L1_gnn_ln2_b': (0.0, 0.479),
     'L1_gnn_b1': (0.0, 0.472),
     'L1_gnn_b2': (0.0, 0.301),
     'L1_mix_bq': (0.0, 2.0),
     'L1_mix_bk': (0.0, 2.0),
     'L1_mix_bv': (0.0, 0.3),
     'L1_mix_bo': (0.0, 0.331),
     'L1_mix_b1': (0.0, 0.566),
     'L1_mix_b2': (0.0, 0.398),
     'L1_mix_ln1_g': (1.0, 0.2),
     'L1_mix_ln1_b': (0.0, 0.302),
     'L1_mix_ln2_g': (1.0, 0.2),
     'L1_mix_ln2_b': (0.0, 0.341),
     'L1_ffn_br': (0.0, 0.8),
     'L1_ffn_b1': (0.0, 0.8),
     'L1_ffn_b2': (0.0, 0.661),
     'L1_ffn_gamma': (1.0, 0.2),
     'L1_ffn_beta': (0.0, 0.415)}
    factors = {'L0_ffn_bg': 22.886,
     'L0_ffn_b1': 26.226,
     'L0_ffn_b2': 8.0,
     'L1_mix_Wq': 38.224,
     'L1_mix_Wk': 28.705,
     'L1_mix_Wv': 3.428}
    for name, (base, spread) in spreads.items():
        noise = np.random.default_rng([zlib.crc32(name.encode()), seed]).standard_normal(out[name].shape)
        drawn = base * np.exp(spread * noise) if base else spread * noise
        out[name] = jnp.asarray(drawn.astype(out[name].dtype))
    for name, factor in factors.items():
        out[name] = (out[name] * factor).astype(out[name].dtype)
    return out
```

```python
from contextlib import ExitStack, contextmanager

import concourse.bass as bass
from concourse import mybir

F32 = mybir.dt.float32
I32 = mybir.dt.int32
U32 = mybir.dt.uint32
BF16 = mybir.dt.bfloat16
ACT = mybir.ActivationFunctionType
ALU = mybir.AluOpType
AX = mybir.AxisListType

N, D, E, ED = 3125, 256, 100000, 64
P = 128
NT = -(-N // P)
NP = NT * P
KB = D // P
SUBS = 4
EC = SUBS * P
NCH = -(-E // EC)
EP = NCH * EC
NI = NCH + NT - 1
HI = NI // 2
NS = NI * SUBS
PAD_DST = NP - 1
H, DH = 8, 32
EPS = 1e-5
TU = 5
TG = NT // TU
COLS = [(g * 512, min(512, N - g * 512)) for g in range(-(-N // 512))]
assert NI % 4 == 0 and TG * TU == NT and NCH * EC >= E and HI <= P


def hold(eng, sem, value, ticks):
    eng.wait_ge(sem, value)
    eng.sem_inc(ticks, 1)


class Shared:
    pass


@contextmanager
def semaphore(nc, sh, name):
    with nc.semaphore(name, num=sh.first_semaphore + sh.semaphores) as handle:
        sh.semaphores += 1
        yield handle


def clear_semaphores(nc, sh):
    with nc.Block() as block:
        @block.sync
        def _(sp):
            sp.sem_clear(range(sh.first_semaphore, sh.first_semaphore + sh.semaphores))
    sh.semaphores = 0


def stage_edge_tables(nc, sh, dst, src, ew, ef_t):
    with ExitStack() as ctx:
        def sb(name, shape, dt=F32):
            return ctx.enter_context(nc.sbuf_tensor(name, shape, dt))

        def sem(name):
            return ctx.enter_context(semaphore(nc, sh, name))

        pad_i = sb("pad_i", [1, 2, EP - E], I32)
        pad_f = sb("pad_f", [ED, EP - E])
        iota_i = sb("iota_i", [P, NCH], I32)
        iota_c = sb("iota_c", [P, NCH])
        inc_i = sb("inc_i", [P, 2], I32)
        inc_f = sb("inc_f", [P, 2])
        row_i = sb("row_i", [P, P], I32)
        ends = sb("ends", [1, 2, NCH], I32)
        ends_t = sb("ends_t", [1, 2, NCH], I32)
        ends_f = sb("ends_f", [1, 2, NCH])
        tiles = sb("tiles", [P, 2, NCH])
        count = sb("count", [P, NCH])
        through = sb("through", [P, NCH])
        before = sb("before", [P, NCH])
        base = sb("base", [P, NCH])
        hit = sb("hit", [P, 2, NCH])
        seen = sb("seen", [P, 2])
        chunk = sb("chunk", [P, 2])
        bsel = sb("bsel", [P, 2])
        tile = sb("tile", [P, 2])
        shift = sb("shift", [P, 2])
        tclip = sb("tclip", [P, 2])
        chunk_i = sb("chunk_i", [P, 2], I32)
        tclip_i = sb("tclip_i", [P, 2], I32)
        dst_r = sb("dst_r", [P, 2, EC], I32)
        src_r = sb("src_r", [P, 2, EC], I32)
        rows = sb("rows", [P, 3, 2, EC])
        dst_f = sb("dst_f", [P, 2, EC])
        valid = sb("valid", [P, 2, EC])
        inside = sb("inside", [P, 2, EC])
        key = sb("key", [P, 2, EC])
        goal = sb("goal", [P, 2, EC], BF16)
        wide = ctx.enter_context(nc.psum_tensor("wide", [P, 512], F32))
        turned = ctx.enter_context(nc.psum_tensor("turned", [P, 6, 512], F32))

        pads_set = sem("pads_set")
        arrays_in = sem("arrays_in")
        ef_padded = sem("ef_padded")
        ends_in = sem("ends_in")
        iotas = sem("iotas")
        consts = sem("consts")
        ends_ready = sem("ends_ready")
        ends_wide = sem("ends_wide")
        chunks_ready = sem("chunks_ready")
        rows_in = ctx.enter_context(nc.semaphore("rows_in"))
        rows_ready = sem("rows_ready")
        key_ready = sem("key_ready")
        goal_ready = sem("goal_ready")
        turned_ready = sem("turned_ready")
        ids_out = sem("ids_out")
        ids_in = sem("ids_in")

        with nc.Block() as block:
            @block.sync
            def _(sp):
                for to, of in ((sh.dst_p, dst), (sh.src_p, src), (sh.ew_p, ew)):
                    sp.dma_start(to[0:E].rearrange("(p e) -> p e", p=P * 5 // 4),
                                 of.rearrange("(p e) -> p e", p=P * 5 // 4)).then_inc(arrays_in, 16)
                sp.wait_ge(pads_set, 3)
                sp.dma_start(sh.dst_p[E:EP].rearrange("(a e) -> a e", a=1), pad_i[:, 0, :]).then_inc(arrays_in, 16)
                sp.dma_start(sh.src_p[E:EP].rearrange("(a e) -> a e", a=1), pad_i[:, 1, :]).then_inc(arrays_in, 16)
                sp.dma_start(sh.ew_p[E:EP].rearrange("(a e) -> a e", a=1), pad_f[0:1, :]).then_inc(arrays_in, 16)
                sp.wait_ge(arrays_in, 96)
                with nc.allow_non_contiguous_dma(reason="two words of each chunk"):
                    d = sh.dst_p.rearrange("(a c e) -> a c e", a=1, e=EC)
                    sp.dma_start(ends[:, 0, :], d[:, :, 0]).then_inc(ends_in, 16)
                    sp.dma_start(ends[:, 1, :], d[:, :, EC - 1]).then_inc(ends_in, 16)
                    sp.wait_ge(chunks_ready, 1)
                    sp.dma_start(sh.tile_d.rearrange("(b p) -> p b", b=2), tclip_i[0:HI, :]).then_inc(ids_out, 16)
                    sp.dma_start(sh.chunk_d.rearrange("(b p) -> p b", b=2), chunk_i[0:HI, :]).then_inc(ids_out, 16)
                sp.wait_ge(ids_out, 32)
                sp.dma_start(sh.tile_id[:, 0:NI], sh.tile_d.rearrange("(a i) -> a i", a=1)).then_inc(ids_in, 16)
                sp.dma_start(sh.chunk_id[:, 0:NI], sh.chunk_d.rearrange("(a i) -> a i", a=1)).then_inc(ids_in, 16)
                sp.wait_ge(goal_ready, 1)
                sp.dma_start(sh.goal_d.rearrange("(b p) e -> p b e", b=2), goal[0:HI, :, :]).then_inc(ids_in, 16)
                sp.wait_ge(key_ready, 1)
                sp.dma_start(sh.key_d.rearrange("(b p) e -> p b e", b=2), key[0:HI, :, :]).then_inc(ids_in, 16)
                sp.wait_ge(ids_in, 64)

            @block.gpsimd
            def _(pool):
                pool.memset(sh.ident[:, :], 0.0).then_inc(iotas, 1)
                pool.iota(iota_i[:, :], pattern=[[1, NCH]], base=0, channel_multiplier=0).then_inc(iotas, 1)
                pool.iota(inc_i[:, :], pattern=[[HI, 2]], base=0, channel_multiplier=1).then_inc(iotas, 1)
                pool.iota(row_i[:, :], pattern=[[1, P]], base=0, channel_multiplier=0).then_inc(iotas, 1)
                pool.wait_ge(iotas, 1)
                pool.affine_select(out=sh.ident[:, :], in_=sh.ident[:, :], compare_op=ALU.not_equal, fill=1.0,
                                   base=0, pattern=[[-1, P]], channel_multiplier=1).then_inc(consts, 1)
                pool.wait_ge(chunks_ready, 1)
                for b in range(2):
                    for to, of in ((dst_r[0:HI, b, :], sh.dst_p), (src_r[0:HI, b, :], sh.src_p),
                                   (rows[0:HI, 2, b, :], sh.ew_p)):
                        pool.indirect_dma_start(to, None, of.rearrange("(c e) -> c e", e=EC),
                                                bass.IndirectOffsetOnAxis(ap=chunk_i[0:HI, b:b + 1], axis=0)
                                                ).then_inc(rows_in, 16)

            @block.tensor
            def _(pe):
                pe.wait_ge(ends_ready, 1)
                pe.wait_ge(consts, 2)
                pe.matmul(wide[:, 0:2 * NCH], sh.ones[0:1, :], ends_f[:, :, :].rearrange("a b c -> a (b c)"),
                          start=True, stop=True).then_inc(ends_wide, 1)
                pe.wait_ge(rows_ready, 1)
                for a in range(3):
                    for b in range(2):
                        for k in range(SUBS):
                            last = pe.transpose(turned[:, 2 * a + b, k * HI:(k + 1) * HI],
                                                rows[0:HI, a, b, k * P:(k + 1) * P], sh.ident[0:HI, 0:HI])
                        last.then_inc(turned_ready, 1)

            @block.scalar
            def _(act):
                act.wait_ge(pads_set, 3)
                act.dma_start(sh.ef_p[:, E:EP], pad_f[:, :]).then_inc(ef_padded, 16)
                act.dma_start(sh.ef_p[:, 0:E], ef_t).then_inc(sh.ef_copied, 16)
                act.wait_ge(ef_padded, 16)

            @block.vector
            def _(dve):
                dve.memset(pad_i[:, 0, :], PAD_DST).then_inc(pads_set, 1)
                dve.memset(pad_i[:, 1, :], 0).then_inc(pads_set, 1)
                dve.memset(pad_f[:, :], 0.0).then_inc(pads_set, 1)
                dve.memset(sh.ones[:, :], 1.0).then_inc(consts, 1)
                dve.wait_ge(iotas, 4)
                dve.tensor_copy(iota_c[:, :], iota_i[:, :])
                dve.tensor_copy(inc_f[:, :], inc_i[:, :])
                dve.tensor_scalar(sh.minus_row[:, :], inc_i[:, 0:1], -1.0, None, ALU.mult)
                dve.memset(sh.ones_b[:, :], 1.0)
                dve.tensor_copy(sh.lane[:, :], row_i[:, :])
                dve.wait_ge(ends_in, 32)
                dve.tensor_scalar(ends_t[:, :, :], ends[:, :, :], 7, None, ALU.arith_shift_right)
                dve.drain()
                dve.tensor_copy(ends_f[:, :, :], ends_t[:, :, :]).then_inc(ends_ready, 1)
                dve.wait_ge(ends_wide, 1)
                dve.tensor_copy(tiles[:, :, :].rearrange("p b c -> p (b c)"), wide[:, 0:2 * NCH])
                dve.drain()
                dve.scalar_tensor_tensor(out=count[:, :], in0=tiles[:, 1, :], scalar=1.0, in1=tiles[:, 0, :],
                                         op0=ALU.add, op1=ALU.subtract)
                dve.memset(hit[:, :, :], 1.0)
                dve.drain()
                dve.tensor_tensor_scan(through[:, :], hit[:, 0, :], count[:, :], 0.0, ALU.mult, ALU.add)
                dve.drain()
                dve.tensor_tensor(before[:, :], through[:, :], count[:, :], ALU.subtract)
                dve.drain()
                dve.tensor_tensor(base[:, :], tiles[:, 0, :], before[:, :], ALU.subtract)
                for b in range(2):
                    dve.tensor_scalar(hit[:, b, :], before[:, :], inc_f[:, b:b + 1], None, ALU.is_le)
                dve.drain()
                dve.tensor_reduce(seen[:, :], hit[:, :, :], AX.X, ALU.add)
                dve.drain()
                dve.tensor_scalar(chunk[:, :], seen[:, :], -1.0, None, ALU.add)
                dve.drain()
                for b in range(2):
                    dve.tensor_scalar(hit[:, b, :], iota_c[:, :], chunk[:, b:b + 1], None, ALU.is_equal)
                dve.drain()
                for b in range(2):
                    dve.tensor_tensor(hit[:, b, :], hit[:, b, :], base[:, :], ALU.mult)
                dve.drain()
                dve.tensor_reduce(bsel[:, :], hit[:, :, :], AX.X, ALU.add)
                dve.drain()
                dve.tensor_tensor(tile[:, :], bsel[:, :], inc_f[:, :], ALU.add)
                dve.drain()
                dve.tensor_scalar(tclip[:, :], tile[:, :], float(NT - 1), None, ALU.min)
                dve.tensor_scalar(shift[:, :], tile[:, :], float(P), None, ALU.mult)
                dve.tensor_copy(chunk_i[:, :], chunk[:, :])
                dve.drain()
                dve.tensor_copy(tclip_i[:, :], tclip[:, :]).then_inc(chunks_ready, 1)
                dve.wait_ge(rows_in, 96)
                dve.tensor_copy(dst_f[0:HI], dst_r[0:HI])
                dve.tensor_copy(rows[0:HI, 1], src_r[0:HI])
                dve.drain()
                for b in range(2):
                    dve.tensor_scalar(rows[0:HI, 0, b, :], dst_f[0:HI, b, :], shift[0:HI, b:b + 1], None,
                                      ALU.subtract)
                dve.drain().then_inc(rows_ready, 1)
                dve.tensor_copy(goal[0:HI], rows[0:HI, 0]).then_inc(goal_ready, 1)
                dve.tensor_scalar(inside[0:HI], rows[0:HI, 0], 0.0, None, ALU.is_ge)
                dve.drain()
                dve.scalar_tensor_tensor(out=valid[0:HI], in0=rows[0:HI, 0], scalar=float(P), in1=inside[0:HI],
                                         op0=ALU.is_lt, op1=ALU.mult)
                dve.drain()
                dve.scalar_tensor_tensor(out=inside[0:HI], in0=dst_f[0:HI], scalar=1.0, in1=valid[0:HI],
                                         op0=ALU.add, op1=ALU.mult)
                dve.drain()
                dve.tensor_scalar(key[0:HI], inside[0:HI], -1.0, None, ALU.add).then_inc(key_ready, 1)
                for a, to in enumerate((sh.lane_of, sh.src_of, sh.weight_of)):
                    for b in range(2):
                        dve.wait_ge(turned_ready, 2 * a + b + 1)
                        dve.tensor_copy(to[:, b * HI * SUBS:(b + 1) * HI * SUBS].rearrange("p (i k) -> p k i", k=SUBS),
                                        turned[:, 2 * a + b, 0:HI * SUBS].rearrange("p (k i) -> p k i", k=SUBS))


def stage_norm(nc, sh, name, load=None, table=None, turn=True, source=None, to=None, gain=None, shift=None):
    with ExitStack() as ctx:
        def sb(n, shape, dt=F32):
            return ctx.enter_context(nc.sbuf_tensor(f"{name}_{n}", shape, dt))

        def sem(n):
            return ctx.enter_context(semaphore(nc, sh, f"{name}_{n}"))

        stats = sb("stats", [P, NT, 6])
        mean_var = sb("mean_var", [P, NT, 2])
        var = sb("var", [P, NT])
        std = sb("std", [P, NT])
        rstd = sb("rstd", [P, NT])
        turned = ctx.enter_context(nc.psum_tensor(f"{name}_turned", [P, TU, 512], F32))
        affine = sb("affine", [P, 2, KB])
        loaded = sem("loaded")
        affine_in = sem("affine_in")
        var_ready = sem("var_ready")
        std_ready = sem("std_ready")
        rows_ready = sem("rows_ready")
        turn_ready = sem("turn_ready")
        turn_used = sem("turn_used")
        stored = sem("stored")
        act_ticks = sem("act_ticks")

        with nc.Block() as block:
            @block.sync
            def _(sp):
                if gain is not None:
                    sp.dma_start(affine[:, 0, :], gain).then_inc(affine_in, 16)
                    sp.dma_start(affine[:, 1, :], shift).then_inc(affine_in, 16)
                if load is not None:
                    sp.dma_start(source[:, 0:NT - 1, :],
                                 load[0:(NT - 1) * P, :].rearrange("(t p) f -> p t f", p=P)).then_inc(loaded, 16)
                    sp.wait_ge(loaded, 17)
                    sp.dma_start(source[0:N - (NT - 1) * P, NT - 1, :], load[(NT - 1) * P:N, :]).then_inc(loaded, 16)
                if table is not None:
                    for g in range(TG):
                        sp.wait_ge(rows_ready, TU * (g + 1))
                        sp.dma_start(table[g * TU * P:(g + 1) * TU * P, :].rearrange("(t p) f -> p t f", p=P),
                                     to[:, g * TU:(g + 1) * TU, :]).then_inc(stored, 16)
                    sp.wait_ge(stored, 16 * TG)

            @block.vector
            def _(dve):
                if load is not None:
                    dve.memset(source[:, NT - 1, :], 0.0).then_inc(loaded, 1)
                    dve.wait_ge(loaded, 33)
                for t in range(NT):
                    dve.bn_stats(stats[:, t, :], source[:, t, :])
                dve.drain()
                for t in range(NT):
                    dve.bn_aggr(mean_var[:, t, :], stats[:, t, :])
                dve.drain()
                dve.tensor_scalar(var[:, :], mean_var[:, :, 1], EPS, None, ALU.add).then_inc(var_ready, 1)
                dve.wait_ge(std_ready, 1)
                dve.reciprocal(rstd[:, :], std[:, :])
                dve.drain()
                with dve.Fori(0, TG) as g:
                    for u in range(TU):
                        dve.tensor_scalar(to[:, bass.ds(TU * g + u, 1), :], source[:, bass.ds(TU * g + u, 1), :],
                                          mean_var[:, bass.ds(TU * g + u, 1), 0], rstd[:, bass.ds(TU * g + u, 1)],
                                          ALU.subtract, ALU.mult).then_inc(rows_ready, 1)

            @block.scalar
            def _(act):
                act.wait_ge(var_ready, 1)
                act.activation(std[:, :], var[:, :], ACT.Sqrt).then_inc(std_ready, 1)
                if turn:
                    if gain is not None:
                        act.wait_ge(affine_in, 32)
                    act.sem_inc(turn_used, TU)
                    with act.Fori(0, TG) as g:
                        for u in range(TU):
                            hold(act, turn_ready, TU * g + (u + 1), act_ticks)
                            if gain is None:
                                act.activation(sh.xt[:, :, bass.ds((TU * g + u) * P, P)],
                                               turned[:, u, 0:KB * P].rearrange("p (k n) -> p k n", k=KB),
                                               ACT.Copy).then_inc(turn_used, 1)
                                continue
                            for k in range(KB):
                                last = act.activation(sh.xt[:, k, bass.ds((TU * g + u) * P, P)],
                                                      turned[:, u, k * P:(k + 1) * P], ACT.Identity,
                                                      bias=affine[:, 1, k:k + 1], scale=affine[:, 0, k:k + 1])
                            last.then_inc(turn_used, 1)

            @block.tensor
            def _(pe):
                for t in range(NT if turn else 0):
                    pe.wait_ge(rows_ready, t + 1)
                    pe.wait_ge(turn_used, t + 1)
                    for k in range(KB):
                        last = pe.transpose(turned[:, t % TU, k * P:(k + 1) * P],
                                            to[:, t, k * P:(k + 1) * P], sh.ident[:, :])
                    last.then_inc(turn_ready, 1)


def stage_aggregate(nc, sh):
    UI = 4
    NB = UI * SUBS
    W = D + 1
    with ExitStack() as ctx:
        def sb(n, shape, dt=F32):
            return ctx.enter_context(nc.sbuf_tensor(f"agg_{n}", shape, dt))

        def sem(n):
            return ctx.enter_context(semaphore(nc, sh, f"agg_{n}"))

        index = sb("index", [P, NB], I32)
        rows = sb("rows", [P, NB, W])
        member = sb("member", [P, NB, P])
        sums = ctx.enter_context(nc.psum_tensor("agg_sums", [P, UI, 512], F32))
        ready = sem("ready")
        index_ready = sem("index_ready")
        gathered = [ctx.enter_context(nc.semaphore(f"agg_gathered{q}")) for q in range(NB)]
        weighted = sem("weighted")
        member_ready = sem("member_ready")
        summed = sem("summed")
        added = sem("added")
        pool_ticks = sem("pool_ticks")
        act_ticks = sem("act_ticks")

        with nc.Block() as block:
            @block.gpsimd
            def _(pool):
                with pool.Fori(0, NI // UI) as i:
                    for u in range(UI):
                        hold(pool, summed, UI * i + (u + 1), pool_ticks)
                        pool.tensor_copy(index[:, u * SUBS:(u + 1) * SUBS],
                                         sh.src_of[:, bass.ds((UI * i + u) * SUBS, SUBS)]).then_inc(index_ready, 1)
                        hold(pool, index_ready, UI * i + (u + 1), pool_ticks)
                        for k in range(SUBS):
                            q = u * SUBS + k
                            pool.indirect_dma_start(rows[:, q, 0:D], None, sh.xn_d,
                                                    bass.IndirectOffsetOnAxis(ap=index[:, q:q + 1], axis=0)
                                                    ).then_inc(gathered[q], 16)

            @block.scalar
            def _(act):
                with act.Fori(0, NI // UI) as i:
                    for u in range(UI):
                        for k in range(SUBS):
                            q = u * SUBS + k
                            hold(act, gathered[q], 16 * i + 16, act_ticks)
                            act.activation(rows[:, q, 0:D], rows[:, q, 0:D], ACT.Copy,
                                           scale=sh.weight_of[:, bass.ds((UI * i + u) * SUBS + k, 1)]
                                           ).then_inc(weighted, 1)

            @block.vector
            def _(dve):
                dve.memset(sh.acc[:, :, :], 0.0)
                dve.memset(rows[:, :, D:W], 1.0)
                dve.drain()
                dve.sem_inc(added, UI)
                with dve.Fori(0, NI // UI) as i:
                    for u in range(UI):
                        dve.wait_ge(summed, UI * i + (u + 1))
                        for k in range(SUBS):
                            dve.tensor_scalar(member[:, u * SUBS + k, :], sh.lane[:, :],
                                              sh.lane_of[:, bass.ds((UI * i + u) * SUBS + k, 1)], None,
                                              ALU.is_equal).then_inc(member_ready, 1)
                    for u in range(UI):
                        t = dve.value_load(sh.tile_id[0:1, bass.ds(UI * i + u, 1)], min_val=0, max_val=NT - 1)
                        dve.wait_ge(summed, UI * i + (u + 1 + UI))
                        dve.tensor_tensor(sh.acc[:, bass.ds(t, 1), 0:W].rearrange("p a w -> p (a w)"),
                                          sh.acc[:, bass.ds(t, 1), 0:W].rearrange("p a w -> p (a w)"),
                                          sums[:, u, 0:W], ALU.add).then_inc(added, 1)
                        dve.drain()

            @block.tensor
            def _(pe):
                pe.sem_inc(summed, UI)
                with pe.Fori(0, NI // UI) as i:
                    for u in range(UI):
                        pe.wait_ge(added, UI * i + (u + 1))
                        for k in range(SUBS):
                            q = u * SUBS + k
                            pe.wait_ge(weighted, NB * i + (q + 1))
                            pe.wait_ge(member_ready, NB * i + (q + 1))
                            last = pe.matmul(sums[:, u, 0:W], member[:, q, :], rows[:, q, :],
                                             start=(k == 0), stop=(k == SUBS - 1))
                        last.then_inc(summed, 1)


def stage_mix0(nc, sh, wk, wv, wq_t, w_out):
    HD = P
    with ExitStack() as ctx:
        def sb(n, shape, dt=F32):
            return ctx.enter_context(nc.sbuf_tensor(f"mix0_{n}", shape, dt))

        def ps(n, shape, dt=F32):
            return ctx.enter_context(nc.psum_tensor(f"mix0_{n}", shape, dt))

        def sem(n):
            return ctx.enter_context(semaphore(nc, sh, f"mix0_{n}"))

        wk_s = sb("wk", [P, KB, HD])
        wv_s = sb("wv", [P, KB, HD])
        wq_s = sb("wq", [HD, D])
        wo_s = sb("wo", [HD, D])
        kt = sb("kt", [HD, NP])
        top = sb("top", [HD, 1])
        low = sb("low", [HD, 1])
        total = sb("total", [HD, 1])
        scale = sb("scale", [HD, 1])
        ke = sb("ke", [P, 2, HD])
        z = sb("z", [HD, D])
        zt = sb("zt", [P, KB, HD])
        heads = sb("heads", [HD, HD])
        m = sb("m", [HD, D])
        keys = ps("keys", [P, 2, 512])
        turned = ps("turned", [P, 2, 512])
        zsum = ps("zsum", [P, 512])
        small = ps("small", [P, 2, 512])

        loaded = sem("loaded")
        keys_ready = sem("keys_ready")
        keys_kept = sem("keys_kept")
        top_ready = sem("top_ready")
        exp_ready = sem("exp_ready")
        turn_ready = sem("turn_ready")
        turn_kept = sem("turn_kept")
        pe_small = sem("pe_small")
        dve_small = sem("dve_small")

        with nc.Block() as block:
            @block.sync
            def _(sp):
                sp.dma_start(wk_s[:, :, :], wk).then_inc(loaded, 16)
                sp.dma_start(wv_s[:, :, :], wv).then_inc(loaded, 16)
                sp.dma_start(wq_s[:, :], wq_t).then_inc(loaded, 16)
                sp.dma_start(wo_s[:, :], w_out).then_inc(loaded, 16)

            @block.tensor
            def _(pe):
                pe.wait_ge(loaded, 64)
                for g, (c, w) in enumerate(COLS):
                    if g >= 2:
                        pe.wait_ge(keys_kept, g - 1)
                    for k in range(KB):
                        last = pe.matmul(keys[:, g % 2, 0:w], wk_s[:, k, :], sh.xt[:, k, c:c + w],
                                         start=(k == 0), stop=(k == KB - 1))
                    last.then_inc(keys_ready, 1)

                pe.wait_ge(exp_ready, 2)

                def turn(t):
                    if t >= 2:
                        pe.wait_ge(turn_kept, t - 1)
                    pe.transpose(turned[:, t % 2, 0:P], kt[:, t * P:(t + 1) * P], sh.ident[:, :]).then_inc(turn_ready, 1)

                turn(0)
                for t in range(NT):
                    if t + 1 < NT:
                        turn(t + 1)
                    pe.wait_ge(turn_kept, t + 1)
                    last = pe.matmul(zsum[:, 0:D], ke[:, t % 2, :], sh.xn[:, t, :], start=(t == 0), stop=(t == NT - 1))
                    last.then_inc(pe_small, 1)
                pe.wait_ge(dve_small, 1)
                for k in range(KB):
                    last = pe.transpose(small[:, 0, k * P:(k + 1) * P], z[:, k * P:(k + 1) * P], sh.ident[:, :])
                last.then_inc(pe_small, 1)
                pe.wait_ge(dve_small, 2)
                for k in range(KB):
                    last = pe.matmul(small[:, 1, 0:HD], wv_s[:, k, :], zt[:, k, :], start=(k == 0), stop=(k == KB - 1))
                last.then_inc(pe_small, 1)
                pe.wait_ge(dve_small, 3)
                pe.matmul(small[:, 0, 0:D], heads[:, :], wo_s[:, :], start=True, stop=True).then_inc(pe_small, 1)
                pe.wait_ge(dve_small, 4)
                for k in range(KB):
                    last = pe.matmul(small[:, 1, k * D:(k + 1) * D], wq_s[:, k * P:(k + 1) * P], m[:, :],
                                     start=True, stop=True)
                last.then_inc(pe_small, 1)

            @block.scalar
            def _(act):
                for g, (c, w) in enumerate(COLS):
                    act.wait_ge(keys_ready, g + 1)
                    act.activation(kt[:, c:c + w], keys[:, g % 2, 0:w], ACT.Copy).then_inc(keys_kept, 1)
                act.wait_ge(top_ready, 1)
                act.activation(kt[:, 0:N], kt[:, 0:N], ACT.Exp, bias=low[:, 0:1], accum_out=total[:, 0:1]
                               ).then_inc(exp_ready, 1)
                for t in range(NT):
                    act.wait_ge(turn_ready, t + 1)
                    if t >= 2:
                        act.wait_ge(pe_small, t - 1)
                    act.activation(ke[:, t % 2, :], turned[:, t % 2, 0:P], ACT.Copy).then_inc(turn_kept, 1)

            @block.vector
            def _(dve):
                dve.memset(kt[:, N:NP], 0.0).then_inc(exp_ready, 1)
                dve.memset(heads[:, :], 0.0)
                dve.wait_ge(keys_kept, len(COLS))
                dve.tensor_reduce(top[:, :], kt[:, 0:N], AX.X, ALU.max)
                dve.drain()
                dve.tensor_scalar(low[:, :], top[:, :], -1.0, None, ALU.mult).then_inc(top_ready, 1)
                dve.wait_ge(exp_ready, 2)
                dve.reciprocal(scale[:, :], total[:, :])
                dve.drain()
                dve.wait_ge(pe_small, NT)
                dve.tensor_scalar(z[:, :], zsum[:, 0:D], scale[:, 0:1], float(DH) ** -0.5, ALU.mult, ALU.mult
                                  ).then_inc(dve_small, 1)
                dve.wait_ge(pe_small, NT + 1)
                dve.tensor_copy(zt[:, :, :].rearrange("p k h -> p (k h)"), small[:, 0, 0:D]).then_inc(dve_small, 1)
                dve.wait_ge(pe_small, NT + 2)
                for h in range(HD // DH):
                    r = slice(h * DH, (h + 1) * DH)
                    last = dve.tensor_copy(heads[r, r], small[r, 1, r])
                last.then_inc(dve_small, 1)
                dve.wait_ge(pe_small, NT + 3)
                dve.tensor_copy(m[:, :], small[:, 0, 0:D]).then_inc(dve_small, 1)
                dve.wait_ge(pe_small, NT + 4)
                dve.tensor_copy(sh.c0[:, :, :].rearrange("p k f -> p (k f)"), small[:, 1, :])


def stage_gnn0(nc, sh, w1_t, w2_t, gamma1, beta1, gamma_h, beta_h, eps_w, b_out):
    NG = len(COLS)
    with ExitStack() as ctx:
        def sb(n, shape, dt=F32):
            return ctx.enter_context(nc.sbuf_tensor(f"gnn0_{n}", shape, dt))

        def ps(n, shape, dt=F32):
            return ctx.enter_context(nc.psum_tensor(f"gnn0_{n}", shape, dt))

        def sem(n):
            return ctx.enter_context(semaphore(nc, sh, f"gnn0_{n}"))

        w_s = sb("w", [P, 2, KB, D])
        gain = sb("gain", [P, 2, KB])
        shift = sb("shift", [P, 2, KB])
        bias = sb("bias", [P, KB])
        eps_s = sb("eps", [P, 1])
        yt = sb("yt", [P, KB, NP])
        ht = sb("ht", [P, KB, NP])
        norm_row = sb("norm_row", [P, NP])
        degree = sb("degree", [P, NT])
        root = sb("root", [P, NT])
        norm = sb("norm", [P, NT])
        stats = sb("stats", [P, 2, KB, NG, 6])
        mean_var = sb("mean_var", [P, 2, KB, 2])
        var = sb("var", [P, 2, KB])
        std = sb("std", [P, 2, KB])
        rstd = sb("rstd", [P, 2, KB])
        a = sb("a", [P, 2, KB])
        ma = sb("ma", [P, 2, KB])
        b = sb("b", [P, 2, KB])
        bank = ps("bank", [P, 4, 512])
        row = ps("row", [P, 2, 512])

        loaded = sem("loaded")
        y_ready = sem("y_ready")
        norm_ready = sem("norm_ready")
        roots = sem("roots")
        degree_ready = sem("degree_ready")
        row_ready = sem("row_ready")
        row_kept = sem("row_kept")
        turn_ready = sem("turn_ready")
        turn_kept = sem("turn_kept")
        prod = [sem("prod1"), sem("prod2")]
        kept = [sem("kept1"), sem("kept2")]
        var_ready = sem("var_ready")
        coef_ready = sem("coef_ready")
        relu = [sem("relu1"), sem("relu2")]
        mixed = sem("mixed")
        mix_added = sem("mix_added")
        back = sem("back")
        back_added = sem("back_added")
        x_ready = sem("x_ready")

        with nc.Block() as block:
            @block.sync
            def _(sp):
                sp.dma_start(w_s[:, 0], w1_t).then_inc(loaded, 16)
                sp.dma_start(w_s[:, 1], w2_t).then_inc(loaded, 16)
                for n, (g_, b_) in enumerate(((gamma1, beta1), (gamma_h, beta_h))):
                    sp.dma_start(gain[:, n, :], g_).then_inc(loaded, 16)
                    sp.dma_start(shift[:, n, :], b_).then_inc(loaded, 16)
                sp.dma_start(bias[:, :], b_out).then_inc(loaded, 16)
                sp.dma_start(eps_s[:, :], eps_w.partition_broadcast(P)).then_inc(loaded, 16)

            @block.gpsimd
            def _(pool):
                for g in range(TG):
                    t = slice(g * TU, (g + 1) * TU)
                    pool.tensor_tensor(sh.x[:, t, :], sh.x[:, t, :], sh.xn[:, t, :], ALU.add).then_inc(x_ready, 1)

            @block.tensor
            def _(pe):
                for t in range(NT):
                    pe.wait_ge(y_ready, t // TU + 1)
                    if t >= 4:
                        pe.wait_ge(turn_kept, t - 3)
                    for k in range(KB):
                        last = pe.transpose(bank[:, t % 4, k * P:(k + 1) * P], sh.acc[:, t, k * P:(k + 1) * P],
                                            sh.ident[:, :])
                    last.then_inc(turn_ready, 1)
                pe.wait_ge(norm_ready, 1)
                for g, (c, w) in enumerate(COLS):
                    if g >= 2:
                        pe.wait_ge(row_kept, g - 1)
                    for t in range(c // P, -(-(c + w) // P)):
                        last = pe.matmul(row[:, g % 2, t * P - c:t * P - c + P],
                                         norm[:, t:t + 1].to_broadcast([P, P]), sh.ident[:, :], start=True, stop=True)
                    last.then_inc(row_ready, 1)
                pe.wait_ge(loaded, 128)
                for n, (of, done) in enumerate(((yt, turn_kept), (ht, relu[0]))):
                    for g, (c, w) in enumerate(COLS):
                        if n == 0:
                            pe.wait_ge(turn_kept, min(NT, (c + w + P - 1) // P))
                        else:
                            pe.wait_ge(relu[0], KB * (g + 1))
                        for m in range(KB):
                            q = KB * g + m
                            if n == 0 and q < 4:
                                pe.wait_ge(turn_kept, NT)
                            elif q >= 4:
                                pe.wait_ge(kept[n], q - 3)
                            for k in range(KB):
                                last = pe.matmul(bank[:, q % 4, 0:w], w_s[:, n, k, m * P:(m + 1) * P],
                                                 of[:, k, c:c + w], start=(k == 0), stop=(k == KB - 1))
                            last.then_inc(prod[n], 1)
                for g, (c, w) in enumerate(COLS):
                    for m in range(KB):
                        q = KB * g + m
                        if q < 4:
                            pe.wait_ge(kept[1], KB * NG)
                        else:
                            pe.wait_ge(mix_added, q - 3)
                        for k in range(KB):
                            last = pe.matmul(bank[:, q % 4, 0:w], sh.c0[:, k, m * P:(m + 1) * P],
                                             sh.xt[:, k, c:c + w], start=(k == 0), stop=(k == KB - 1))
                        last.then_inc(mixed, 1)
                for t in range(NT):
                    w = min(P, N - t * P)
                    pe.wait_ge(mix_added, KB * (t // 4 + 1))
                    if t >= 2:
                        pe.wait_ge(back_added, t - 1)
                    for k in range(KB):
                        last = pe.transpose(row[0:w, t % 2, k * P:(k + 1) * P], yt[:, k, t * P:t * P + w],
                                            sh.ident[:, :])
                    last.then_inc(back, 1)

            @block.scalar
            def _(act):
                act.wait_ge(degree_ready, 1)
                act.activation(root[:, :], degree[:, :], ACT.Sqrt).then_inc(roots, 1)
                for t in range(NT):
                    act.wait_ge(turn_ready, t + 1)
                    act.activation(yt[:, :, t * P:(t + 1) * P],
                                   bank[:, t % 4, 0:D].rearrange("p (k n) -> p k n", k=KB), ACT.Copy
                                   ).then_inc(turn_kept, 1)
                for g, (c, w) in enumerate(COLS):
                    w = min(512, NP - c)
                    act.wait_ge(row_ready, g + 1)
                    act.activation(norm_row[:, c:c + w], row[:, g % 2, 0:w], ACT.Copy).then_inc(row_kept, 1)
                for g, (c, w) in enumerate(COLS):
                    for m in range(KB):
                        act.wait_ge(prod[0], KB * g + m + 1)
                        act.activation(ht[:, m, c:c + w], bank[:, (KB * g + m) % 4, 0:w], ACT.Copy
                                       ).then_inc(kept[0], 1)
                for n, of in enumerate((ht, yt)):
                    act.wait_ge(var_ready, n + 1)
                    act.activation(std[:, n, :], var[:, n, :], ACT.Sqrt).then_inc(roots, 1)
                    act.wait_ge(coef_ready, n + 1)
                    act.wait_ge(kept[n], KB * NG)
                    for g, (c, w) in enumerate(COLS):
                        for m in range(KB):
                            act.activation(of[:, m, c:c + w], of[:, m, c:c + w], ACT.Relu, bias=b[:, n, m:m + 1],
                                           scale=a[:, n, m:m + 1]).then_inc(relu[n], 1)

            @block.vector
            def _(dve):
                dve.wait_ge(loaded, 128)
                dve.tensor_scalar(degree[:, :], sh.acc[:, :, D], 1.0, None, ALU.max).then_inc(degree_ready, 1)
                for g in range(TG):
                    t = slice(g * TU, (g + 1) * TU)
                    dve.scalar_tensor_tensor(out=sh.acc[:, t, 0:D], in0=sh.xn[:, t, :], scalar=eps_s[:, 0:1],
                                             in1=sh.acc[:, t, 0:D], op0=ALU.mult, op1=ALU.add).then_inc(y_ready, 1)
                dve.wait_ge(roots, 1)
                dve.reciprocal(norm[:, :], root[:, :]).then_inc(norm_ready, 1)

                def coefs(n):
                    dve.drain()
                    for m in range(KB):
                        dve.bn_aggr(mean_var[:, n, m, :], stats[:, n, m, :, :].rearrange("p g s -> p (g s)"))
                    dve.drain()
                    dve.tensor_scalar(var[:, n, :], mean_var[:, n, :, 1], EPS, None, ALU.add).then_inc(var_ready, 1)
                    dve.wait_ge(roots, n + 2)
                    dve.reciprocal(rstd[:, n, :], std[:, n, :])
                    dve.drain()
                    dve.tensor_tensor(a[:, n, :], gain[:, n, :], rstd[:, n, :], ALU.mult)
                    dve.drain()
                    dve.tensor_tensor(ma[:, n, :], mean_var[:, n, :, 0], a[:, n, :], ALU.mult)
                    dve.drain()
                    dve.tensor_tensor(b[:, n, :], shift[:, n, :], ma[:, n, :], ALU.subtract).then_inc(coef_ready, 1)

                for g, (c, w) in enumerate(COLS):
                    for m in range(KB):
                        dve.wait_ge(kept[0], KB * g + m + 1)
                        dve.bn_stats(stats[:, 0, m, g, :], ht[:, m, c:c + w])
                coefs(0)
                dve.wait_ge(row_kept, NG)
                for g, (c, w) in enumerate(COLS):
                    for m in range(KB):
                        q = KB * g + m
                        dve.wait_ge(prod[1], q + 1)
                        dve.tensor_tensor(yt[:, m, c:c + w], bank[:, q % 4, 0:w], norm_row[:, c:c + w], ALU.mult
                                          ).then_inc(kept[1], 1)
                        dve.wait_ge(kept[1], q + 1)
                        dve.bn_stats(stats[:, 1, m, g, :], yt[:, m, c:c + w])
                coefs(1)
                for g, (c, w) in enumerate(COLS):
                    for m in range(KB):
                        q = KB * g + m
                        dve.wait_ge(mixed, q + 1)
                        dve.wait_ge(relu[1], q + 1)
                        dve.scalar_tensor_tensor(out=yt[:, m, c:c + w], in0=bank[:, q % 4, 0:w],
                                                 scalar=bias[:, m:m + 1], in1=yt[:, m, c:c + w],
                                                 op0=ALU.add, op1=ALU.add).then_inc(mix_added, 1)
                for t in range(NT):
                    w = min(P, N - t * P)
                    dve.wait_ge(back, t + 1)
                    dve.wait_ge(x_ready, t // TU + 1)
                    dve.tensor_tensor(sh.x[0:w, t, :], sh.x[0:w, t, :], row[0:w, t % 2, 0:D], ALU.add
                                      ).then_inc(back_added, 1)


F1 = 512
FB = F1 // P
GT = 4
NGR = -(-NT // GT)


def stage_gate(nc, sh, wg, bg, bias, b2):
    X8 = 8
    with ExitStack() as ctx:
        def sb(n, shape, dt=F32):
            return ctx.enter_context(nc.sbuf_tensor(f"gate_{n}", shape, dt))

        def sem(n):
            return ctx.enter_context(semaphore(nc, sh, f"gate_{n}"))

        wg_s = sb("wg", [P, KB, X8])
        b_s = sb("b", [P, 2, X8])
        b2_s = sb("b2", [X8, D])
        logits = sb("logits", [P, NT, X8])
        best = sb("best", [P, NT, X8])
        place = sb("place", [P, NT, X8], U32)
        place_f = sb("place_f", [P, NT, 2])
        gap = sb("gap", [P, NT])
        second = sb("second", [P, NT])
        total = sb("total", [P, NT])
        share = sb("share", [P, NT, 2])
        lane8 = sb("lane8", [P, NT, X8])
        part = sb("part", [P, 2, NT, X8])
        gate_t = sb("gate_t", [X8, 2, P])
        raw = ctx.enter_context(nc.psum_tensor("gate_raw", [P, 512], F32))
        turned = ctx.enter_context(nc.psum_tensor("gate_turned", [P, 2, 512], F32))
        added = ctx.enter_context(nc.psum_tensor("gate_added", [P, 2, 512], F32))
        loaded = sem("loaded")
        raw_ready = sem("raw_ready")
        gap_ready = sem("gap_ready")
        second_ready = sem("second_ready")
        gate_ready = sem("gate_ready")
        turn_ready = sem("turn_ready")
        turn_kept = sem("turn_kept")
        bias_ready = sem("bias_ready")
        bias_added = sem("bias_added")

        with nc.Block() as block:
            @block.sync
            def _(sp):
                sp.dma_start(wg_s[:, :, :], wg).then_inc(loaded, 16)
                sp.dma_start(b_s[:, 0, :], bg.partition_broadcast(P)).then_inc(loaded, 16)
                sp.dma_start(b_s[:, 1, :], bias.partition_broadcast(P)).then_inc(loaded, 16)
                sp.dma_start(b2_s[:, :], b2).then_inc(loaded, 16)

            @block.tensor
            def _(pe):
                pe.wait_ge(loaded, 64)
                for t in range(NT):
                    for k in range(KB):
                        last = pe.matmul(raw[:, t * X8:(t + 1) * X8], sh.xt[:, k, t * P:(t + 1) * P], wg_s[:, k, :],
                                         start=(k == 0), stop=(k == KB - 1))
                last.then_inc(raw_ready, 1)
                pe.wait_ge(gate_ready, 1)

                def turn(t):
                    if t >= 2:
                        pe.wait_ge(turn_kept, t - 1)
                    pe.transpose(turned[0:X8, t % 2, 0:P], sh.gate[:, t, :], sh.ident[:, :]).then_inc(turn_ready, 1)

                turn(0)
                for t in range(NT):
                    if t + 1 < NT:
                        turn(t + 1)
                    pe.wait_ge(turn_kept, t + 1)
                    if t >= 2:
                        pe.wait_ge(bias_added, t - 1)
                    pe.matmul(added[:, t % 2, 0:D], gate_t[:, t % 2, :], b2_s[:, :], start=True, stop=True
                              ).then_inc(bias_ready, 1)

            @block.scalar
            def _(act):
                act.wait_ge(gap_ready, 1)
                act.activation(second[:, :], gap[:, :], ACT.Exp).then_inc(second_ready, 1)
                for t in range(NT):
                    act.wait_ge(turn_ready, t + 1)
                    if t >= 2:
                        act.wait_ge(bias_ready, t - 1)
                    act.activation(gate_t[:, t % 2, :], turned[0:X8, t % 2, 0:P], ACT.Copy).then_inc(turn_kept, 1)

            @block.vector
            def _(dve):
                dve.tensor_copy(lane8[:, :, :], sh.lane[:, 0:X8].unsqueeze(1).to_broadcast([P, NT, X8]))
                dve.wait_ge(loaded, 64)
                dve.wait_ge(raw_ready, 1)
                dve.tensor_tensor(best[:, :, :], raw[:, 0:NT * X8].rearrange("p (t e) -> p t e", e=X8),
                                  b_s[:, 0, :].unsqueeze(1).to_broadcast([P, NT, X8]), ALU.add)
                dve.drain()
                dve.tensor_tensor(logits[:, :, :], best[:, :, :],
                                  b_s[:, 1, :].unsqueeze(1).to_broadcast([P, NT, X8]), ALU.add)
                dve.drain()
                for t in range(NT):
                    dve.max(best[:, t, :], logits[:, t, :])
                dve.drain()
                for t in range(NT):
                    dve.max_index(place[:, t, :], best[:, t, :], logits[:, t, :])
                dve.tensor_tensor(gap[:, :], best[:, :, 1], best[:, :, 0], ALU.subtract).then_inc(gap_ready, 1)
                dve.drain()
                dve.tensor_copy(place_f[:, :, :], place[:, :, 0:2])
                dve.wait_ge(second_ready, 1)
                dve.tensor_scalar(total[:, :], second[:, :], 1.0, None, ALU.add)
                dve.drain()
                dve.reciprocal(share[:, :, 0], total[:, :])
                for j in range(2):
                    dve.tensor_tensor(part[:, j], lane8[:, :, :],
                                      place_f[:, :, j:j + 1].to_broadcast([P, NT, X8]), ALU.is_equal)
                dve.drain()
                dve.tensor_tensor(share[:, :, 1], second[:, :], share[:, :, 0], ALU.mult)
                dve.drain()
                for j in range(2):
                    dve.tensor_tensor(part[:, j], part[:, j],
                                      share[:, :, j:j + 1].to_broadcast([P, NT, X8]), ALU.mult)
                dve.drain()
                dve.tensor_tensor(sh.gate[:, :, :], part[:, 0], part[:, 1], ALU.add).then_inc(gate_ready, 1)
                for t in range(NT):
                    dve.wait_ge(bias_ready, t + 1)
                    dve.tensor_tensor(sh.x[:, t, :], sh.x[:, t, :], added[:, t % 2, 0:D], ALU.add
                                      ).then_inc(bias_added, 1)


def stage_ffn(nc, sh, name, parts, w1_of, w2_of, b1_of, function, weight_of, into):
    with ExitStack() as ctx:
        def sb(n, shape, dt=F32):
            return ctx.enter_context(nc.sbuf_tensor(f"{name}_{n}", shape, dt))

        def sem(n):
            return ctx.enter_context(semaphore(nc, sh, f"{name}_{n}"))

        w1 = sb("w1", [P, 2, KB, F1])
        w2 = sb("w2", [P, 2, FB, D])
        b1 = sb("b1", [P, 2, FB])
        hidden = sb("hidden", [P, FB, GT * P])
        up = ctx.enter_context(nc.psum_tensor(f"{name}_up", [P, FB, 512], F32))
        down = ctx.enter_context(nc.psum_tensor(f"{name}_down", [P, GT, 512], F32))
        weights_in = [sem(f"weights_in{q}") for q in range(2)]
        pe_ticks = sem("pe_ticks")
        up_ready = sem("up_ready")
        hidden_ready = sem("hidden_ready")
        down_ready = sem("down_ready")
        summed = sem("summed")

        with nc.Block() as block:
            @block.sync
            def _(sp):
                with sp.Fori(0, parts // 2) as pair:
                    for q in range(2):
                        sp.wait_ge(down_ready, 2 * NGR * pair + NGR * (q + 1))
                        sp.dma_start(w1[:, q], w1_of(pair, q)).then_inc(weights_in[q], 16)
                        sp.dma_start(w2[:, q], w2_of(pair, q)).then_inc(weights_in[q], 16)
                        sp.dma_start(b1[:, q], b1_of(pair, q)).then_inc(weights_in[q], 16)

            def groups(eng, pair, q, body):
                before = 2 * NGR * pair + NGR * q
                with eng.Fori(0, NGR - 1) as g:
                    body(before + g, g, GT)
                body(before + (NGR - 1), NGR - 1, NT - GT * (NGR - 1))

            @block.tensor
            def _(pe):
                pe.sem_inc(down_ready, 2 * NGR)
                with pe.Fori(0, parts // 2) as pair:
                    for q in range(2):
                        hold(pe, weights_in[q], 48 * pair + 48, pe_ticks)

                        def body(n, g, tiles, q=q):
                            for m in range(FB):
                                for k in range(KB):
                                    last = pe.matmul(up[:, m, 0:tiles * P], w1[:, q, k, m * P:(m + 1) * P],
                                                     sh.xt[:, k, bass.ds(g * (GT * P), tiles * P)],
                                                     start=(k == 0), stop=(k == KB - 1))
                                last.then_inc(up_ready, 1)
                            pe.wait_ge(summed, n + 1)
                            for m in range(FB):
                                pe.wait_ge(hidden_ready, FB * n + (m + 1))
                                for j in range(tiles):
                                    last = pe.matmul(down[:, j, 0:D], hidden[:, m, j * P:(j + 1) * P], w2[:, q, m, :],
                                                     start=(m == 0), stop=(m == FB - 1))
                            last.then_inc(down_ready, 1)

                        groups(pe, pair, q, body)

            @block.scalar
            def _(act):
                with act.Fori(0, parts // 2) as pair:
                    for q in range(2):
                        def body(n, g, tiles, q=q):
                            for m in range(FB):
                                act.wait_ge(up_ready, FB * n + (m + 1))
                                act.activation(hidden[:, m, 0:tiles * P], up[:, m, 0:tiles * P], function,
                                               bias=b1[:, q, m:m + 1]).then_inc(hidden_ready, 1)

                        groups(act, pair, q, body)

            @block.vector
            def _(dve):
                dve.sem_inc(summed, 1)
                with dve.Fori(0, parts // 2) as pair:
                    for q in range(2):
                        def body(n, g, tiles, q=q):
                            dve.wait_ge(down_ready, n + (1 + 2 * NGR))
                            for j in range(tiles):
                                t = g * GT + j
                                last = dve.scalar_tensor_tensor(out=into[:, bass.ds(t, 1), :].rearrange("p a f -> p (a f)"),
                                                                in0=down[:, j, 0:D], scalar=weight_of(t, pair, q),
                                                                in1=into[:, bass.ds(t, 1), :].rearrange("p a f -> p (a f)"),
                                                                op0=ALU.mult, op1=ALU.add)
                            last.then_inc(summed, 1)

                        groups(dve, pair, q, body)


def stage_rows(nc, sh, name, gain, shift, more=(), into=None, out=None):
    with ExitStack() as ctx:
        def sem(n):
            return ctx.enter_context(semaphore(nc, sh, f"{name}_{n}"))

        vectors = [gain, shift, *more]
        rows = ctx.enter_context(nc.sbuf_tensor(f"{name}_rows", [P, 2 + len(more), D], F32))
        loaded = sem("loaded")
        scaled = sem("scaled")
        shift_ready = sem("shift_ready")
        shifted = sem("shifted")
        added = sem("added")
        stored = sem("stored")

        with nc.Block() as block:
            @block.sync
            def _(sp):
                for n, v in enumerate(vectors):
                    sp.dma_start(rows[:, n, :], v.partition_broadcast(P)).then_inc(loaded, 16)
                if out is not None:
                    for g in range(TG):
                        sp.wait_ge(added, g + 1)
                        a, z = g * TU * P, min(N, (g + 1) * TU * P)
                        full = (z - a) // P
                        sp.dma_start(out[a:a + full * P, :].rearrange("(t p) f -> p t f", p=P),
                                     into[:, g * TU:g * TU + full, :]).then_inc(stored, 16)
                        if z - a > full * P:
                            sp.dma_start(out[a + full * P:z, :], into[0:z - a - full * P, g * TU + full, :]
                                         ).then_inc(stored, 16)
                    sp.wait_ge(stored, 16 * (TG + 1))

            @block.vector
            def _(dve):
                dve.wait_ge(loaded, 16 * len(vectors))
                for n in range(len(more)):
                    dve.tensor_tensor(rows[:, 1, :], rows[:, 1, :], rows[:, 2 + n, :], ALU.add)
                    dve.drain()
                dve.sem_inc(shift_ready, 1)
                for g in range(TG):
                    t = slice(g * TU, (g + 1) * TU)
                    dve.tensor_tensor(sh.work[:, t, :], sh.work[:, t, :],
                                      rows[:, 0, :].unsqueeze(1).to_broadcast([P, TU, D]), ALU.mult).then_inc(scaled, 1)
                if into is not None:
                    for g in range(TG):
                        t = slice(g * TU, (g + 1) * TU)
                        dve.wait_ge(shifted, g + 1)
                        dve.tensor_tensor(into[:, t, :], into[:, t, :], sh.work[:, t, :], ALU.add).then_inc(added, 1)

            @block.gpsimd
            def _(pool):
                pool.wait_ge(shift_ready, 1)
                for g in range(TG):
                    t = slice(g * TU, (g + 1) * TU)
                    pool.wait_ge(scaled, g + 1)
                    pool.tensor_tensor(sh.work[:, t, :], sh.work[:, t, :],
                                       rows[:, 1, :].unsqueeze(1).to_broadcast([P, TU, D]), ALU.add).then_inc(shifted, 1)


def stage_mix1(nc, sh, wq, wk, wv, wo, bq, bk, bv, bo):
    NG = len(COLS)
    with ExitStack() as ctx:
        def sb(n, shape, dt=F32):
            return ctx.enter_context(nc.sbuf_tensor(f"mix1_{n}", shape, dt))

        def ps(n, shape, dt=F32):
            return ctx.enter_context(nc.psum_tensor(f"mix1_{n}", shape, dt))

        def sem(n):
            return ctx.enter_context(semaphore(nc, sh, f"mix1_{n}"))

        w_s = sb("w", [P, 4, KB, D])
        b_s = sb("b", [P, 3, KB])
        bo_s = sb("bo", [P, D])
        phi = sb("phi", [P, 2, KB, NP])
        pos = sb("pos", [P, 2, 512])
        neg = sb("neg", [P, 2, 512])
        ksum = sb("ksum", [P, KB])
        kt = sb("kt", [P, 2, D])
        z = sb("z", [P, KB, D])
        zt = sb("zt", [P, KB, KB, P])
        own = sb("own", [P, P])
        kv = sb("kv", [P, KB, P])
        heads = sb("heads", [P, KB, P])
        den = sb("den", [P, KB, P])
        m = sb("m", [P, KB, D])
        rden = sb("rden", [P, 2, 512])
        bank = ps("bank", [P, 4, 512])
        zsum = ps("zsum", [P, KB, 512])
        small = ps("small", [P, 2, 512])

        loaded = sem("loaded")
        prod = sem("prod")
        pos_ready = sem("pos_ready")
        neg_ready = sem("neg_ready")
        exp_ready = sem("exp_ready")
        phi_ready = sem("phi_ready")
        turn_ready = sem("turn_ready")
        turn_kept = sem("turn_kept")
        zsummed = sem("zsummed")
        pe_small = sem("pe_small")
        dve_small = sem("dve_small")
        den_ready = sem("den_ready")
        divided = sem("divided")
        out_ready = sem("out_ready")
        out_added = sem("out_added")
        biased = sem("biased")

        with nc.Block() as block:
            @block.sync
            def _(sp):
                for n, w in enumerate((wk, wq, wv, wo)):
                    sp.dma_start(w_s[:, n], w).then_inc(loaded, 16)
                for n, b in enumerate((bk, bq, bv)):
                    sp.dma_start(b_s[:, n, :], b).then_inc(loaded, 16)
                sp.dma_start(bo_s[:, :], bo.partition_broadcast(P)).then_inc(loaded, 16)

            @block.gpsimd
            def _(pool):
                pool.wait_ge(loaded, 128)
                for g in range(TG):
                    t = slice(g * TU, (g + 1) * TU)
                    pool.tensor_tensor(sh.work[:, t, :], sh.xn[:, t, :],
                                       bo_s[:, :].unsqueeze(1).to_broadcast([P, TU, D]), ALU.add).then_inc(biased, 1)

            @block.tensor
            def _(pe):
                pe.wait_ge(loaded, 128)
                for n in range(2):
                    for g, (c, w) in enumerate(COLS):
                        for m_ in range(KB):
                            q = KB * (NG * n + g) + m_
                            if q >= 4:
                                pe.wait_ge(neg_ready, q - 3)
                            for k in range(KB):
                                last = pe.matmul(bank[:, q % 4, 0:w], w_s[:, n, k, m_ * P:(m_ + 1) * P],
                                                 sh.xt[:, k, c:c + w], start=(k == 0), stop=(k == KB - 1))
                            last.then_inc(prod, 1)

                def turn(t):
                    pe.wait_ge(phi_ready, min(KB * NG, KB * (t // 4 + 1)))
                    if t == NT - 1:
                        pe.wait_ge(dve_small, 1)
                    if t >= 2:
                        pe.wait_ge(turn_kept, t - 1)
                    for k in range(KB):
                        last = pe.transpose(small[:, t % 2, k * P:(k + 1) * P], phi[:, 0, k, t * P:(t + 1) * P],
                                            sh.ident[:, :])
                    last.then_inc(turn_ready, 1)

                turn(0)
                for t in range(NT):
                    if t + 1 < NT:
                        turn(t + 1)
                    pe.wait_ge(turn_kept, t + 1)
                    for m_ in range(KB):
                        last = pe.matmul(zsum[:, m_, 0:D], kt[:, t % 2, m_ * P:(m_ + 1) * P], sh.xn[:, t, :],
                                         start=(t == 0), stop=(t == NT - 1))
                    last.then_inc(zsummed, 1)
                pe.wait_ge(dve_small, 2)
                for m_ in range(KB):
                    for k in range(KB):
                        last = pe.transpose(small[:, 0, (2 * m_ + k) * P:(2 * m_ + k + 1) * P],
                                            z[:, m_, k * P:(k + 1) * P], sh.ident[:, :])
                last.then_inc(pe_small, 1)
                for m_ in range(KB):
                    last = pe.matmul(small[:, 1, (2 + m_) * P:(3 + m_) * P], ksum[:, m_:m_ + 1].to_broadcast([P, P]),
                                     sh.ident[:, :], start=True, stop=True)
                pe.wait_ge(dve_small, 3)
                for m_ in range(KB):
                    for k in range(KB):
                        last = pe.matmul(small[:, 1, m_ * P:(m_ + 1) * P], w_s[:, 2, k, m_ * P:(m_ + 1) * P],
                                         zt[:, m_, k, :], start=(k == 0), stop=(k == KB - 1))
                last.then_inc(pe_small, 1)
                pe.wait_ge(dve_small, 4)
                for m_ in range(KB):
                    last = pe.matmul(small[:, 0, m_ * D:(m_ + 1) * D], heads[:, m_, :], w_s[:, 3, m_, :],
                                     start=True, stop=True)
                last.then_inc(pe_small, 1)
                for g, (c, w) in enumerate(COLS):
                    for m_ in range(KB):
                        q = KB * g + m_
                        pe.wait_ge(phi_ready, KB * NG + q + 1)
                        if q >= 4:
                            pe.wait_ge(den_ready, q - 3)
                        pe.matmul(bank[:, q % 4, 0:w], den[:, m_, :], phi[:, 1, m_, c:c + w],
                                  start=True, stop=True).then_inc(pe_small, 1)
                pe.wait_ge(dve_small, 5)
                for t in range(NT):
                    w = min(P, N - t * P)
                    pe.wait_ge(divided, KB * (t // 4 + 1))
                    if t >= 2:
                        pe.wait_ge(out_added, t - 1)
                    for m_ in range(KB):
                        last = pe.matmul(zsum[0:w, t % 2, 0:D], phi[:, 1, m_, t * P:t * P + w], m[:, m_, :],
                                         start=(m_ == 0), stop=(m_ == KB - 1))
                    last.then_inc(out_ready, 1)

            @block.scalar
            def _(act):
                act.wait_ge(loaded, 128)
                for q in range(2 * NG * KB):
                    n, g, m_ = q // (NG * KB), q // KB % NG, q % KB
                    w = COLS[g][1]
                    act.wait_ge(prod, q + 1)
                    if q >= 2:
                        act.wait_ge(phi_ready, q - 1)
                    act.activation(pos[:, q % 2, 0:w], bank[:, q % 4, 0:w], ACT.Relu, bias=b_s[:, n, m_:m_ + 1]
                                   ).then_inc(pos_ready, 1)
                    if q >= 1:
                        w = COLS[(q - 1) // KB % NG][1]
                        act.wait_ge(neg_ready, q)
                        act.activation(neg[:, (q - 1) % 2, 0:w], neg[:, (q - 1) % 2, 0:w], ACT.Exp).then_inc(exp_ready, 1)
                act.wait_ge(neg_ready, 2 * NG * KB)
                w = COLS[-1][1]
                act.activation(neg[:, 1, 0:w], neg[:, 1, 0:w], ACT.Exp).then_inc(exp_ready, 1)
                for t in range(NT):
                    act.wait_ge(turn_ready, t + 1)
                    if t >= 2:
                        act.wait_ge(zsummed, t - 1)
                    act.activation(kt[:, t % 2, :], small[:, t % 2, 0:D], ACT.Copy).then_inc(turn_kept, 1)

            @block.vector
            def _(dve):
                dve.memset(phi[:, 0, :, N:NP], 0.0).then_inc(dve_small, 1)
                dve.memset(own[:, :], 0.0)
                dve.drain()
                for h in range(P // DH):
                    r = slice(h * DH, (h + 1) * DH)
                    dve.memset(own[r, r], 1.0)
                dve.wait_ge(loaded, 128)

                def finish(q):
                    n, g, m_ = q // (NG * KB), q // KB % NG, q % KB
                    c, w = COLS[g]
                    dve.wait_ge(exp_ready, q + 1)
                    dve.tensor_tensor(phi[:, n, m_, c:c + w], pos[:, q % 2, 0:w], neg[:, q % 2, 0:w], ALU.add
                                      ).then_inc(phi_ready, 1)

                for q in range(2 * NG * KB):
                    n, g, m_ = q // (NG * KB), q // KB % NG, q % KB
                    w = COLS[g][1]
                    dve.wait_ge(pos_ready, q + 1)
                    if q >= 2:
                        dve.wait_ge(phi_ready, q - 1)
                    dve.tensor_scalar(neg[:, q % 2, 0:w], bank[:, q % 4, 0:w], b_s[:, n, m_:m_ + 1], 0.0,
                                      ALU.add, ALU.min).then_inc(neg_ready, 1)
                    if q >= 1:
                        finish(q - 1)
                finish(2 * NG * KB - 1)
                dve.wait_ge(phi_ready, KB * NG)
                dve.tensor_reduce(ksum[:, :], phi[:, 0, :, 0:N], AX.X, ALU.add)
                dve.wait_ge(zsummed, NT)
                for m_ in range(KB):
                    last = dve.tensor_copy(z[:, m_, :], zsum[:, m_, 0:D])
                dve.drain().then_inc(dve_small, 1)
                for m_ in range(KB):
                    dve.tensor_scalar(den[:, m_, :], own[:, :], ksum[:, m_:m_ + 1], None, ALU.mult)
                dve.wait_ge(pe_small, 1)
                dve.tensor_copy(zt[:, :, :, :].rearrange("p m k n -> p (m k n)"), small[:, 0, :])
                dve.drain().then_inc(dve_small, 1)
                dve.wait_ge(pe_small, 2)
                for m_ in range(KB):
                    dve.tensor_scalar(kv[:, m_, :], small[:, 1, (2 + m_) * P:(3 + m_) * P], b_s[:, 2, m_:m_ + 1],
                                      None, ALU.mult)
                dve.drain()
                for m_ in range(KB):
                    dve.tensor_tensor(kv[:, m_, :], kv[:, m_, :], small[:, 1, m_ * P:(m_ + 1) * P], ALU.add)
                dve.drain()
                for m_ in range(KB):
                    last = dve.tensor_tensor(heads[:, m_, :], kv[:, m_, :], own[:, :], ALU.mult)
                last.then_inc(dve_small, 1)
                dve.wait_ge(pe_small, 3)
                dve.tensor_copy(m[:, :, :].rearrange("p m f -> p (m f)"), small[:, 0, :]).then_inc(dve_small, 1)
                for g, (c, w) in enumerate(COLS):
                    for m_ in range(KB):
                        q = KB * g + m_
                        dve.wait_ge(pe_small, 4 + q)
                        dve.tensor_scalar(rden[:, q % 2, 0:w], bank[:, q % 4, 0:w], 1e-6, None, ALU.add
                                          ).then_inc(den_ready, 1)
                        dve.drain()
                        dve.reciprocal(rden[:, q % 2, 0:w], rden[:, q % 2, 0:w])
                        dve.drain()
                        dve.tensor_tensor(phi[:, 1, m_, c:c + w], phi[:, 1, m_, c:c + w], rden[:, q % 2, 0:w],
                                          ALU.mult).then_inc(divided, 1)
                for t in range(NT):
                    w = min(P, N - t * P)
                    dve.wait_ge(out_ready, t + 1)
                    dve.wait_ge(biased, t // TU + 1)
                    dve.tensor_tensor(sh.work[0:w, t, :], sh.work[0:w, t, :], zsum[0:w, t % 2, 0:D], ALU.add
                                      ).then_inc(out_added, 1)


def stage_project(nc, sh, w, bq, bk, bv):
    with ExitStack() as ctx:
        def sem(n):
            return ctx.enter_context(semaphore(nc, sh, f"proj_{n}"))

        w_s = ctx.enter_context(nc.sbuf_tensor("proj_w", [P, KB, 3 * D], F32))
        b_s = ctx.enter_context(nc.sbuf_tensor("proj_b", [P, 3 * D], F32))
        kv = ctx.enter_context(nc.sbuf_tensor("proj_kv", [P, 4, 2 * D], F32))
        out = ctx.enter_context(nc.psum_tensor("proj_out", [P, 2, 2, 512], F32))
        loaded = sem("loaded")
        prod = sem("prod")
        kept = sem("kept")
        stored = [sem(f"stored{q}") for q in range(4)]

        with nc.Block() as block:
            @block.sync
            def _(sp):
                sp.dma_start(w_s[:, :, :], w).then_inc(loaded, 16)
                for n, v in enumerate((bq, bk, bv)):
                    sp.dma_start(b_s[:, n * D:(n + 1) * D], v.partition_broadcast(P)).then_inc(loaded, 16)
                for t in range(NT):
                    sp.wait_ge(kept, t + 1)
                    for n, table in enumerate((sh.k_d, sh.v_d)):
                        sp.dma_start(table[t * P:(t + 1) * P, :], kv[:, t % 4, n * D:(n + 1) * D]
                                     ).then_inc(stored[t % 4], 16)
                for q in range(4):
                    sp.wait_ge(stored[q], 32 * len(range(q, NT, 4)))

            @block.tensor
            def _(pe):
                pe.wait_ge(loaded, 64)
                for t in range(NT):
                    if t >= 2:
                        pe.wait_ge(kept, t - 1)
                    for a, z in ((0, 2 * D), (2 * D, 3 * D)):
                        for k in range(KB):
                            last = pe.matmul(out[:, t % 2, a // (2 * D), 0:z - a], sh.xt[:, k, t * P:(t + 1) * P],
                                             w_s[:, k, a:z], start=(k == 0), stop=(k == KB - 1))
                    last.then_inc(prod, 1)

            @block.vector
            def _(dve):
                dve.wait_ge(loaded, 64)
                for t in range(NT):
                    dve.wait_ge(prod, t + 1)
                    if t >= 4:
                        dve.wait_ge(stored[t % 4], 32 * (t // 4))
                    dve.tensor_tensor(sh.q[:, t, :], out[:, t % 2, 0, 0:D], b_s[:, 0:D], ALU.add)
                    dve.tensor_tensor(kv[:, t % 4, 0:D], out[:, t % 2, 0, D:2 * D], b_s[:, D:2 * D], ALU.add)
                    dve.tensor_tensor(kv[:, t % 4, D:2 * D], out[:, t % 2, 1, 0:D], b_s[:, 2 * D:3 * D], ALU.add
                                      ).then_inc(kept, 1)


def stage_scores(nc, sh, we, be):
    UI = 4
    NB = UI * SUBS
    with ExitStack() as ctx:
        def sb(n, shape, dt=F32):
            return ctx.enter_context(nc.sbuf_tensor(f"score_{n}", shape, dt))

        def ps(n, shape, dt=F32):
            return ctx.enter_context(nc.psum_tensor(f"score_{n}", shape, dt))

        def sem(n):
            return ctx.enter_context(semaphore(nc, sh, f"score_{n}"))

        index = sb("index", [P, NB], I32)
        rows = sb("rows", [P, NB, D])
        goal = sb("goal", [1, UI, EC], BF16)
        off = sb("off", [P, 2, EC])
        member = sb("member", [P, 2, EC])
        feats = sb("feats", [ED + 1, UI, EC])
        we_s = sb("we", [ED + 1, DH])
        summed = sb("summed", [P, 2, SUBS * D])
        dots = sb("dots", [P, 2, SUBS * H])
        wide = ps("wide", [P, 2, 512])
        edge = ps("edge", [P, 2, 512])
        query = ps("query", [P, 2, SUBS * D])

        loaded = sem("loaded")
        index_ready = sem("index_ready")
        gathered = [ctx.enter_context(nc.semaphore(f"score_gathered{q}")) for q in range(NB)]
        goal_in = [sem(f"goal_in{u}") for u in range(UI)]
        feats_in = [sem(f"feats_in{u}") for u in range(UI)]
        wide_ready = sem("wide_ready")
        off_ready = sem("off_ready")
        member_ready = sem("member_ready")
        edge_ready = sem("edge_ready")
        query_ready = sem("query_ready")
        rows_used = sem("rows_used")
        query_used = sem("query_used")
        pool_ticks = sem("pool_ticks")

        with nc.Block() as block:
            @block.gpsimd
            def _(pool):
                with pool.Fori(0, NI // UI) as i:
                    for u in range(UI):
                        hold(pool, rows_used, UI * i + (u + 1), pool_ticks)
                        pool.tensor_copy(index[:, u * SUBS:(u + 1) * SUBS],
                                         sh.src_of[:, bass.ds((UI * i + u) * SUBS, SUBS)]).then_inc(index_ready, 1)
                        hold(pool, index_ready, UI * i + (u + 1), pool_ticks)
                        for k in range(SUBS):
                            q = u * SUBS + k
                            pool.indirect_dma_start(rows[:, q, :], None, sh.k_d,
                                                    bass.IndirectOffsetOnAxis(ap=index[:, q:q + 1], axis=0)
                                                    ).then_inc(gathered[q], 16)

            @block.sync
            def _(sp):
                sp.dma_start(we_s[0:ED, :], we).then_inc(loaded, 16)
                sp.dma_start(we_s[ED:ED + 1, :], be).then_inc(loaded, 16)
                sp.wait_ge(sh.ef_copied, 16)
                with sp.Fori(0, NI // UI) as i:
                    for u in range(UI):
                        c = sp.value_load(sh.chunk_id[0:1, bass.ds(UI * i + u, 1)], min_val=0, max_val=NCH - 1)
                        sp.wait_ge(edge_ready, UI * i + (u + 1))
                        sp.dma_start(goal[:, u, :], sh.goal_d[bass.ds(UI * i + u, 1), :]).then_inc(goal_in[u], 16)
                        sp.dma_start(feats[0:ED, u, :], sh.ef_p[:, bass.ds(c * EC, EC)]).then_inc(feats_in[u], 16)

            @block.tensor
            def _(pe):
                pe.wait_ge(loaded, 33)
                pe.sem_inc(edge_ready, UI)
                pe.sem_inc(query_ready, 2)
                with pe.Fori(0, NI // UI) as i:
                    for pair in range(0, UI, 2):
                        for u in (pair, pair + 1):
                            pe.wait_ge(goal_in[u], 16 * i + 16)
                            pe.wait_ge(off_ready, UI * i + (u + 1))
                            pe.matmul(wide[:, u % 2, :], sh.ones_b[0:1, :], goal[:, u, :], start=True, stop=True
                                      ).then_inc(wide_ready, 1)
                        for u in (pair, pair + 1):
                            pe.wait_ge(feats_in[u], 16 * i + 16)
                            pe.wait_ge(rows_used, UI * i + (u + 1 + UI - 2))
                            for k in range(SUBS):
                                last = pe.matmul(edge[:, u % 2, k * DH:(k + 1) * DH], feats[:, u, k * P:(k + 1) * P],
                                                 we_s[:, :], start=True, stop=True)
                            last.then_inc(edge_ready, 1)
                        for u in (pair, pair + 1):
                            t = pe.value_load(sh.tile_id[0:1, bass.ds(UI * i + u, 1)], min_val=0, max_val=NT - 1)
                            pe.wait_ge(member_ready, UI * i + (u + 1))
                            pe.wait_ge(query_used, UI * i + (u + 1))
                            for k in range(SUBS):
                                last = pe.matmul(query[:, u % 2, k * D:(k + 1) * D], member[:, u % 2, k * P:(k + 1) * P],
                                                 sh.q[:, bass.ds(t, 1), :], start=True, stop=True)
                            last.then_inc(query_ready, 1)

            @block.scalar
            def _(act):
                act.sem_inc(off_ready, 2)
                with act.Fori(0, NI // UI) as i:
                    for pair in range(0, UI, 2):
                        for u in (pair, pair + 1):
                            act.wait_ge(wide_ready, UI * i + (u + 1))
                            act.activation(off[:, u % 2, :], wide[:, u % 2, :], ACT.Abs, bias=sh.minus_row[:, 0:1]
                                           ).then_inc(off_ready, 1)
                        for u in (pair, pair + 1):
                            act.wait_ge(off_ready, UI * i + (u + 3))
                            act.wait_ge(query_ready, UI * i + (u + 1))
                            act.activation(member[:, u % 2, :], off[:, u % 2, :], ACT.Relu, bias=sh.ones[:, 0:1],
                                           scale=-1.0).then_inc(member_ready, 1)

            @block.vector
            def _(dve):
                dve.memset(feats[ED:ED + 1, :, :], 1.0).then_inc(loaded, 1)
                dve.sem_inc(rows_used, UI)
                dve.sem_inc(query_used, 2)
                with dve.Fori(0, NI // UI) as i:
                    for pair in range(0, UI, 2):
                        for u in (pair, pair + 1):
                            for k in range(SUBS):
                                dve.wait_ge(gathered[u * SUBS + k], 16 * i + 16)
                            dve.wait_ge(edge_ready, UI * i + (u + 1 + UI))
                            dve.tensor_tensor(
                                summed[:, u % 2, :].rearrange("p (k h d) -> p k h d", k=SUBS, h=H),
                                rows[:, u * SUBS:(u + 1) * SUBS, :].rearrange("p k (h d) -> p k h d", h=H),
                                edge[:, u % 2, 0:SUBS * DH].rearrange("p (k d) -> p k d", k=SUBS).unsqueeze(2)
                                .to_broadcast([P, SUBS, H, DH]), ALU.add).then_inc(rows_used, 1)
                        dve.drain()
                        for u in (pair, pair + 1):
                            dve.wait_ge(query_ready, UI * i + (u + 3))
                            dve.tensor_tensor(summed[:, u % 2, :], summed[:, u % 2, :], query[:, u % 2, :], ALU.mult
                                              ).then_inc(query_used, 1)
                        dve.drain()
                        for u in (pair, pair + 1):
                            dve.tensor_reduce(dots[:, u % 2, :], summed[:, u % 2, :].rearrange("p (g d) -> p g d", d=DH),
                                              AX.X, ALU.add)
                        dve.drain()
                        u = pair
                        dve.scalar_tensor_tensor(
                            out=sh.scores[:, bass.ds((UI * i + u) * SUBS * H, 2 * SUBS * H)]
                            .rearrange("p (k h) -> p k h", h=H),
                            in0=dots[:, :, :].rearrange("p n (k h) -> p (n k) h", h=H), scalar=float(DH) ** -0.5,
                            in1=sh.weight_of[:, bass.ds((UI * i + u) * SUBS, 2 * SUBS)].unsqueeze(2)
                            .to_broadcast([P, 2 * SUBS, H]), op0=ALU.mult, op1=ALU.mult)
                    dve.drain()


def stage_softmax(nc, sh):
    SP_ = 8
    PP = NS // SP_
    SL = SP_ * P
    NBL = NS // 16
    BIG = 1.0e30
    assert NS % 16 == 0 and PP <= P
    with ExitStack() as ctx:
        def sb(n, shape, dt=F32):
            return ctx.enter_context(nc.sbuf_tensor(f"max_{n}", shape, dt))

        def ps(n, shape, dt=F32):
            return ctx.enter_context(nc.psum_tensor(f"max_{n}", shape, dt))

        def sem(n):
            return ctx.enter_context(semaphore(nc, sh, f"max_{n}"))

        st = sb("st", [P, NBL, P])
        line = sb("line", [P, H, SL])
        free = sh.acc[:, :, :].rearrange("p t w -> p (t w)")
        key = free[:, 0:SL]
        new = free[:, SL:2 * SL]
        last_ = free[:, 2 * SL:3 * SL]
        edge_key = free[:, 3 * SL:4 * SL]
        side = sb("side", [P, H + 2])
        side_t = sb("side_t", [H + 2, P])
        keys = sb("keys", [1, 2, P])
        same = sb("same", [1, 3, P])
        wide = sb("wide", [H, 3, P])
        carry = sb("carry", [H, 2, P])
        carried = sb("carried", [P, H])
        turned = ps("turned", [P, 4, 512])
        small = ps("small", [P, 2, 512])

        turn_ready = sem("turn_ready")
        turn_kept = sem("turn_kept")
        lines_out = sem("lines_out")
        lines_in = sem("lines_in")
        key_in = sem("key_in")
        pe_small = sem("pe_small")
        dve_small = sem("dve_small")
        keys_moved = sem("keys_moved")
        maxima = sem("maxima")
        maxima_out = sem("maxima_out")
        maxima_in = sem("maxima_in")
        back_ready = sem("back_ready")
        back_used = sem("back_used")
        keys_kept = sem("keys_kept")

        score_lines = sh.scores_d.rearrange("h (b s) e -> s h b e", s=16)

        def blocks(q):
            return range(4 * q, min(4 * q + 4, NBL))

        NQ = -(-NBL // 4)

        with nc.Block() as block:
            @block.tensor
            def _(pe):
                for q in range(NQ):
                    if q >= 4:
                        pe.wait_ge(turn_kept, q - 3)
                    for b in blocks(q):
                        last = pe.transpose(turned[:, q % 4, (b % 4) * P:(b % 4 + 1) * P],
                                            sh.scores[:, b * P:(b + 1) * P], sh.ident[:, :])
                    last.then_inc(turn_ready, 1)
                for r in range(2):
                    pe.wait_ge(dve_small, 3 * r + 1)
                    pe.transpose(small[0:H + 2, 0, 0:PP], side[0:PP, :], sh.ident[0:PP, 0:PP]).then_inc(pe_small, 1)
                    pe.wait_ge(dve_small, 3 * r + 2)
                    pe.matmul(small[0:H, 1, 0:3 * P], sh.ones[0:1, 0:H], same[:, :, :].rearrange("a n p -> a (n p)"),
                              start=True, stop=True).then_inc(pe_small, 1)
                    pe.wait_ge(dve_small, 3 * r + 3)
                    pe.transpose(small[0:P, 0, 0:H], carry[:, 1, :], sh.ident[0:H, 0:H]).then_inc(pe_small, 1)
                pe.wait_ge(maxima_in, 256)
                for q in range(NQ):
                    if q >= 4:
                        pe.wait_ge(back_used, q - 3)
                    for b in blocks(q):
                        last = pe.transpose(turned[:, q % 4, (b % 4) * P:(b % 4 + 1) * P], st[:, b, :], sh.ident[:, :])
                    last.then_inc(back_ready, 1)

            @block.sync
            def _(sp):
                sp.dma_start(key[0:PP, :], sh.key_d.rearrange("i e -> (i e)").rearrange("(p s) -> p s", s=SL)
                             ).then_inc(key_in, 16)
                sp.wait_ge(turn_kept, NQ)
                for s in range(16):
                    sp.dma_start(score_lines[s], st[s * H:(s + 1) * H, :, :]).then_inc(lines_out, 16)
                sp.wait_ge(lines_out, 256)
                sp.dma_start(line[0:PP, :, :], sh.scores_d.rearrange("h j e -> h (j e)")
                             .rearrange("h (p s) -> p h s", s=SL)).then_inc(lines_in, 16)
                for r in range(2):
                    sp.wait_ge(dve_small, 3 * r + 1)
                    sp.wait_ge(keys_kept, r + 1)
                    for n in range(2):
                        sp.dma_start(keys[:, n, 0:PP], side_t[H + n:H + n + 1, 0:PP]).then_inc(keys_moved, 16)
                sp.wait_ge(maxima, 1)
                sp.dma_start(sh.scores_d.rearrange("h j e -> h (j e)").rearrange("h (p s) -> p h s", s=SL),
                             line[0:PP, :, :]).then_inc(maxima_out, 16)
                sp.wait_ge(maxima_out, 16)
                for s in range(16):
                    sp.dma_start(st[s * H:(s + 1) * H, :, :], score_lines[s]).then_inc(maxima_in, 16)

            @block.scalar
            def _(act):
                for q in range(NQ):
                    n = len(blocks(q))
                    act.wait_ge(turn_ready, q + 1)
                    act.activation(st[:, 4 * q:4 * q + n, :].rearrange("p b e -> p (b e)"), turned[:, q % 4, 0:n * P],
                                   ACT.Copy).then_inc(turn_kept, 1)
                for q in range(NQ):
                    a, z = 4 * q * P, 4 * q * P + len(blocks(q)) * P
                    act.wait_ge(back_used, q + 1)
                    act.activation(sh.scores[:, a:z], sh.scores[:, a:z], ACT.Exp)

            @block.vector
            def _(dve):
                dve.memset(keys[:, :, :], -2.0)
                dve.memset(side_t[:, :], 0.0)
                dve.memset(same[:, :, :], 0.0)
                dve.memset(carry[:, :, :], 0.0)
                dve.wait_ge(key_in, 16)
                dve.memset(new[:, 0:1], 0.0)
                dve.memset(last_[:, SL - 1:SL], 0.0)
                dve.tensor_tensor(new[0:PP, 1:SL], key[0:PP, 1:SL], key[0:PP, 0:SL - 1], ALU.not_equal)
                dve.drain()
                dve.tensor_scalar(new[0:PP, 1:SL], new[0:PP, 1:SL], -BIG, None, ALU.mult)
                dve.drain()
                dve.tensor_copy(last_[0:PP, 0:SL - 1], new[0:PP, 1:SL])
                dve.wait_ge(lines_in, 16)
                for r in range(2):
                    near, far = (0, SL - 1) if r == 0 else (SL - 1, 0)
                    step = new if r == 0 else last_
                    for h in range(H):
                        if r == 0:
                            dve.tensor_tensor_scan(line[0:PP, h, :], step[0:PP, :], line[0:PP, h, :], -BIG,
                                                   ALU.add, ALU.max)
                        else:
                            dve.tensor_tensor_scan(line[0:PP, h, ::-1], step[0:PP, ::-1], line[0:PP, h, ::-1], -BIG,
                                                   ALU.add, ALU.max)
                    dve.tensor_scalar(edge_key[0:PP, :], key[0:PP, :], key[0:PP, near:near + 1], -BIG,
                                      ALU.not_equal, ALU.mult)
                    dve.drain()
                    dve.tensor_copy(side[0:PP, 0:H], line[0:PP, :, far])
                    dve.tensor_copy(side[0:PP, H:H + 1], key[0:PP, near:near + 1])
                    dve.tensor_copy(side[0:PP, H + 1:H + 2], key[0:PP, far:far + 1])
                    dve.drain().then_inc(dve_small, 1)
                    dve.wait_ge(pe_small, 3 * r + 1)
                    dve.tensor_copy(side_t[:, 0:PP], small[0:H + 2, 0, 0:PP]).then_inc(keys_kept, 1)
                    dve.wait_ge(keys_moved, 32 * (r + 1))
                    if r == 0:
                        dve.tensor_tensor(same[:, 0, 1:PP], keys[:, 0, 1:PP], keys[:, 1, 0:PP - 1], ALU.not_equal)
                    else:
                        dve.memset(same[:, 0, PP - 1:PP], 0.0)
                        dve.tensor_tensor(same[:, 0, 0:PP - 1], keys[:, 0, 0:PP - 1], keys[:, 1, 1:PP], ALU.not_equal)
                    end = 0 if r == 0 else PP - 1
                    dve.drain()
                    dve.memset(same[:, 0, end:end + 1], 1.0)
                    dve.tensor_tensor(same[:, 1, 0:PP], keys[:, 0, 0:PP], keys[:, 1, 0:PP], ALU.not_equal)
                    dve.drain()
                    dve.tensor_tensor(same[:, 1, 0:PP], same[:, 1, 0:PP], same[:, 0, 0:PP], ALU.max)
                    dve.drain()
                    dve.tensor_scalar(same[:, 0:2, 0:PP], same[:, 0:2, 0:PP], -BIG, None, ALU.mult)
                    dve.drain().then_inc(dve_small, 1)
                    dve.wait_ge(pe_small, 3 * r + 2)
                    dve.tensor_copy(wide[:, :, :].rearrange("h n p -> h (n p)"), small[0:H, 1, 0:3 * P])
                    dve.drain()
                    if r == 0:
                        dve.tensor_tensor_scan(carry[:, 0, 0:PP], wide[:, 1, 0:PP], side_t[0:H, 0:PP], -BIG,
                                               ALU.add, ALU.max)
                        dve.drain()
                        dve.tensor_tensor(carry[:, 1, 1:PP], carry[:, 0, 0:PP - 1], wide[:, 0, 1:PP], ALU.add)
                    else:
                        dve.tensor_tensor_scan(carry[:, 0, PP - 1::-1], wide[:, 1, PP - 1::-1], side_t[0:H, PP - 1::-1],
                                               -BIG, ALU.add, ALU.max)
                        dve.drain()
                        dve.tensor_tensor(carry[:, 1, 0:PP - 1], carry[:, 0, 1:PP], wide[:, 0, 0:PP - 1], ALU.add)
                    dve.memset(carry[:, 1, end:end + 1], -BIG)
                    dve.drain().then_inc(dve_small, 1)
                    dve.wait_ge(pe_small, 3 * r + 3)
                    dve.tensor_copy(carried[:, :], small[:, 0, 0:H])
                    dve.drain()
                    dve.tensor_scalar(carried[:, :], carried[:, :], -BIG, None, ALU.max)
                    dve.drain()
                    for h in range(H):
                        dve.scalar_tensor_tensor(out=line[0:PP, h, :], in0=edge_key[0:PP, :],
                                                 scalar=carried[0:PP, h:h + 1], in1=line[0:PP, h, :],
                                                 op0=ALU.add, op1=ALU.max)
                    dve.drain()
                dve.sem_inc(maxima, 1)
                for q in range(NQ):
                    a, z = 4 * q * P, 4 * q * P + len(blocks(q)) * P
                    dve.wait_ge(back_ready, q + 1)
                    dve.tensor_tensor(sh.scores[:, a:z], sh.scores[:, a:z], turned[:, q % 4, 0:z - a], ALU.subtract
                                      ).then_inc(back_used, 1)


def stage_attend(nc, sh):
    UI = 4
    NB = UI * SUBS
    W = D + H
    with ExitStack() as ctx:
        def sb(n, shape, dt=F32):
            return ctx.enter_context(nc.sbuf_tensor(f"att_{n}", shape, dt))

        def sem(n):
            return ctx.enter_context(semaphore(nc, sh, f"att_{n}"))

        index = sb("index", [P, NB], I32)
        rows = sb("rows", [P, NB, D])
        member = sb("member", [P, NB, P])
        sums = ctx.enter_context(nc.psum_tensor("att_sums", [P, UI, 512], F32))
        totals = ctx.enter_context(nc.psum_tensor("att_totals", [P, UI, 512], F32))
        index_ready = sem("index_ready")
        gathered = [ctx.enter_context(nc.semaphore(f"att_gathered{q}")) for q in range(NB)]
        ready = sem("ready")
        summed = sem("summed")
        added = sem("added")
        pool_ticks = sem("pool_ticks")

        with nc.Block() as block:
            @block.gpsimd
            def _(pool):
                with pool.Fori(0, NI // UI) as i:
                    for u in range(UI):
                        hold(pool, summed, UI * i + (u + 1), pool_ticks)
                        pool.tensor_copy(index[:, u * SUBS:(u + 1) * SUBS],
                                         sh.src_of[:, bass.ds((UI * i + u) * SUBS, SUBS)]).then_inc(index_ready, 1)
                        hold(pool, index_ready, UI * i + (u + 1), pool_ticks)
                        for k in range(SUBS):
                            q = u * SUBS + k
                            pool.indirect_dma_start(rows[:, q, :], None, sh.v_d,
                                                    bass.IndirectOffsetOnAxis(ap=index[:, q:q + 1], axis=0)
                                                    ).then_inc(gathered[q], 16)

            @block.vector
            def _(dve):
                dve.memset(sh.acc[:, :, :], 0.0)
                dve.drain()
                dve.sem_inc(added, UI)
                with dve.Fori(0, NI // UI) as i:
                    for u in range(UI):
                        dve.wait_ge(summed, UI * i + (u + 1))
                        for k in range(SUBS):
                            dve.tensor_scalar(member[:, u * SUBS + k, :], sh.lane[:, :],
                                              sh.lane_of[:, bass.ds((UI * i + u) * SUBS + k, 1)], None,
                                              ALU.is_equal)
                        for k in range(SUBS):
                            dve.wait_ge(gathered[u * SUBS + k], 16 * i + 16)
                        r = rows[:, u * SUBS:(u + 1) * SUBS, :].rearrange("p k (h d) -> p (k h) d", h=H)
                        dve.tensor_tensor(r, r, sh.scores[:, bass.ds((UI * i + u) * SUBS * H, SUBS * H)].unsqueeze(2)
                                          .to_broadcast([P, SUBS * H, DH]), ALU.mult)
                        dve.drain().then_inc(ready, 1)
                    for u in range(UI):
                        t = dve.value_load(sh.tile_id[0:1, bass.ds(UI * i + u, 1)], min_val=0, max_val=NT - 1)
                        dve.wait_ge(summed, UI * i + (u + 1 + UI))
                        a = sh.acc[:, bass.ds(t, 1), 0:D].rearrange("p a w -> p (a w)")
                        dve.tensor_tensor(a, a, sums[:, u, 0:D], ALU.add)
                        a = sh.acc[:, bass.ds(t, 1), D:W].rearrange("p a w -> p (a w)")
                        dve.tensor_tensor(a, a, totals[:, u, 0:H], ALU.add).then_inc(added, 1)
                        dve.drain()

            @block.tensor
            def _(pe):
                pe.sem_inc(summed, UI)
                with pe.Fori(0, NI // UI) as i:
                    for u in range(UI):
                        pe.wait_ge(added, UI * i + (u + 1))
                        pe.wait_ge(ready, UI * i + (u + 1))
                        for k in range(SUBS):
                            q = u * SUBS + k
                            pe.matmul(sums[:, u, 0:D], member[:, q, :], rows[:, q, :],
                                      start=(k == 0), stop=(k == SUBS - 1))
                            last = pe.matmul(totals[:, u, 0:H], member[:, q, :],
                                             sh.scores[:, bass.ds(((UI * i + u) * SUBS + k) * H, H)],
                                             start=(k == 0), stop=(k == SUBS - 1))
                        last.then_inc(summed, 1)


def stage_attention_out(nc, sh, wo, bo, alpha, beta, b2):
    with ExitStack() as ctx:
        def sb(n, shape, dt=F32):
            return ctx.enter_context(nc.sbuf_tensor(f"ao_{n}", shape, dt))

        def sem(n):
            return ctx.enter_context(semaphore(nc, sh, f"ao_{n}"))

        wo_s = sb("wo", [P, KB, D])
        bo_s = sb("bo", [P, D])
        b2_s = sb("b2", [P, D])
        ab = sb("ab", [P, 1])
        total = sb("total", [P, NT, H])
        at = sb("at", [P, 2, KB, P])
        out = sb("out", [P, 2, D])
        turned = ctx.enter_context(nc.psum_tensor("ao_turned", [P, 2, 512], F32))
        prod = ctx.enter_context(nc.psum_tensor("ao_prod", [P, 2, 512], F32))
        loaded = sem("loaded")
        divided = sem("divided")
        turn_ready = sem("turn_ready")
        turn_kept = sem("turn_kept")
        prod_ready = sem("prod_ready")
        prod_used = sem("prod_used")
        xn_ready = sem("xn_ready")
        b2_ready = sem("b2_ready")
        pooled = sem("pooled")

        with nc.Block() as block:
            @block.sync
            def _(sp):
                sp.dma_start(wo_s[:, :, :], wo).then_inc(loaded, 16)
                sp.dma_start(bo_s[:, :], bo.partition_broadcast(P)).then_inc(loaded, 16)
                sp.dma_start(b2_s[:, :], b2.partition_broadcast(P)).then_inc(loaded, 16)
                sp.dma_start(ab[:, :], alpha.partition_broadcast(P)).then_inc(loaded, 16)
                sp.dma_start(sh.beta[:, :], beta.partition_broadcast(P)).then_inc(loaded, 16)

            @block.tensor
            def _(pe):
                pe.wait_ge(loaded, 80)

                def turn(t):
                    pe.wait_ge(divided, t // TU + 1)
                    if t >= 2:
                        pe.wait_ge(turn_kept, t - 1)
                    for k in range(KB):
                        last = pe.transpose(turned[:, t % 2, k * P:(k + 1) * P], sh.acc[:, t, k * P:(k + 1) * P],
                                            sh.ident[:, :])
                    last.then_inc(turn_ready, 1)

                turn(0)
                for t in range(NT):
                    if t + 1 < NT:
                        turn(t + 1)
                    pe.wait_ge(turn_kept, t + 1)
                    if t >= 2:
                        pe.wait_ge(prod_used, t - 1)
                    for k in range(KB):
                        last = pe.matmul(prod[:, t % 2, 0:D], at[:, t % 2, k, :], wo_s[:, k, :],
                                         start=(k == 0), stop=(k == KB - 1))
                    last.then_inc(prod_ready, 1)

            @block.scalar
            def _(act):
                for t in range(NT):
                    act.wait_ge(turn_ready, t + 1)
                    if t >= 2:
                        act.wait_ge(prod_ready, t - 1)
                    act.activation(at[:, t % 2, :, :].rearrange("p k n -> p (k n)"), turned[:, t % 2, 0:D], ACT.Copy
                                   ).then_inc(turn_kept, 1)

            @block.gpsimd
            def _(pool):
                pool.wait_ge(b2_ready, 1)
                for g in range(TG):
                    t = slice(g * TU, (g + 1) * TU)
                    pool.wait_ge(xn_ready, TU * (g + 1))
                    pool.tensor_tensor(sh.x[:, t, :], sh.x[:, t, :], sh.xn[:, t, :], ALU.add).then_inc(pooled, 1)
                    pool.wait_ge(pooled, 2 * g + 1)
                    pool.tensor_tensor(sh.x[:, t, :], sh.x[:, t, :],
                                       b2_s[:, :].unsqueeze(1).to_broadcast([P, TU, D]), ALU.add).then_inc(pooled, 1)

            @block.vector
            def _(dve):
                dve.wait_ge(loaded, 80)
                dve.tensor_scalar(b2_s[:, :], b2_s[:, :], sh.beta[:, 0:1], None, ALU.mult).then_inc(b2_ready, 1)
                dve.tensor_scalar(total[:, :, :], sh.acc[:, :, D:D + H], 0.5, None, ALU.max)
                dve.drain()
                dve.reciprocal(total[:, :, :], total[:, :, :])
                dve.drain()
                for g in range(TG):
                    for t in range(g * TU, (g + 1) * TU):
                        a = sh.acc[:, t, 0:D].rearrange("p (h d) -> p h d", h=H)
                        last = dve.tensor_tensor(a, a, total[:, t, :].unsqueeze(2).to_broadcast([P, H, DH]), ALU.mult)
                    last.then_inc(divided, 1)
                for t in range(NT):
                    dve.wait_ge(prod_ready, t + 1)
                    dve.tensor_tensor(out[:, t % 2, :], prod[:, t % 2, 0:D], bo_s[:, :], ALU.add).then_inc(prod_used, 1)
                    dve.drain()
                    dve.scalar_tensor_tensor(out=sh.xn[:, t, :], in0=out[:, t % 2, :], scalar=ab[:, 0:1],
                                             in1=sh.xn[:, t, :], op0=ALU.mult, op1=ALU.add).then_inc(xn_ready, 1)


def stage_route(nc, sh, wr, br, b2):
    X8 = 8
    CAPACITY = float(-(-N * 5 // (4 * X8)))
    with ExitStack() as ctx:
        def sb(n, shape, dt=F32):
            return ctx.enter_context(nc.sbuf_tensor(f"route_{n}", shape, dt))

        def sem(n):
            return ctx.enter_context(semaphore(nc, sh, f"route_{n}"))

        wr_s = sb("wr", [P, KB, X8])
        br_s = sb("br", [P, X8])
        b2_s = sb("b2", [X8, D])
        mean = sb("mean", [P, KB])
        v = sb("v", [P, 8, X8])
        top = sb("top", [P, 2, X8])
        place = sb("place", [P, X8], U32)
        place_f = sb("place_f", [P, 2])
        one = sb("one", [P, 6])
        dense = sb("dense", [P, X8])
        column = sb("column", [X8, 1])
        row = sb("row", [P, D])
        bank = ctx.enter_context(nc.psum_tensor("route_bank", [P, 2, 512], F32))
        loaded = sem("loaded")
        mean_ready = sem("mean_ready")
        prod = sem("prod")
        act_in = sem("act_in")
        act_out = sem("act_out")
        column_ready = sem("column_ready")
        row_ready = sem("row_ready")
        done = sem("done")

        with nc.Block() as block:
            @block.sync
            def _(sp):
                sp.dma_start(wr_s[:, :, :], wr).then_inc(loaded, 16)
                sp.dma_start(br_s[:, :], br.partition_broadcast(P)).then_inc(loaded, 16)
                sp.dma_start(b2_s[:, :], b2).then_inc(loaded, 16)

            @block.tensor
            def _(pe):
                pe.wait_ge(loaded, 48)
                pe.wait_ge(mean_ready, 1)
                for k in range(KB):
                    last = pe.matmul(bank[:, 0, 0:X8], mean[:, k:k + 1].to_broadcast([P, P]), wr_s[:, k, :],
                                     start=(k == 0), stop=(k == KB - 1))
                last.then_inc(prod, 1)
                pe.wait_ge(column_ready, 1)
                pe.matmul(bank[:, 1, 0:D], column[:, 0:1].to_broadcast([X8, P]), b2_s[:, :], start=True, stop=True
                          ).then_inc(prod, 1)

            @block.scalar
            def _(act):
                for n, (a, b) in enumerate(((1, 1), (3, 4))):
                    act.wait_ge(act_in, n + 1)
                    act.activation(v[:, b, :], v[:, a, :], ACT.Exp).then_inc(act_out, 1)
                act.wait_ge(act_in, 3)
                act.activation(one[:, 4:5], one[:, 4:5], ACT.Exp).then_inc(act_out, 1)

            @block.gpsimd
            def _(pool):
                pool.wait_ge(row_ready, 1)
                for g in range(3):
                    t = slice(g * TU, (g + 1) * TU)
                    pool.tensor_tensor(sh.xn[:, t, :], sh.xn[:, t, :], row[:, :].unsqueeze(1).to_broadcast([P, TU, D]),
                                       ALU.add).then_inc(done, 1)

            @block.vector
            def _(dve):
                dve.tensor_reduce(mean[:, :], sh.xt[:, :, 0:N], AX.X, ALU.add)
                dve.drain()
                dve.tensor_scalar(mean[:, :], mean[:, :], 1.0 / N, None, ALU.mult).then_inc(mean_ready, 1)
                dve.wait_ge(prod, 1)
                dve.tensor_tensor(v[:, 0, :], bank[:, 0, 0:X8], br_s[:, :], ALU.add)
                dve.drain()

                def softmax(a, n, out):
                    dve.tensor_reduce(one[:, 0:1], v[:, a, :], AX.X, ALU.max)
                    dve.drain()
                    dve.tensor_scalar(v[:, a + 1, :], v[:, a, :], one[:, 0:1], None, ALU.subtract).then_inc(act_in, 1)
                    dve.wait_ge(act_out, n + 1)
                    dve.tensor_reduce(one[:, 1:2], v[:, out, :], AX.X, ALU.add)
                    dve.drain()
                    dve.reciprocal(one[:, 2:3], one[:, 1:2])
                    dve.drain()
                    dve.tensor_scalar(v[:, out, :], v[:, out, :], one[:, 2:3], None, ALU.mult)
                    dve.drain()

                softmax(0, 0, 1)
                dve.tensor_scalar(v[:, 5, :], v[:, 1, :], float(N), 1e-30, ALU.mult, ALU.max)
                dve.drain()
                dve.reciprocal(v[:, 6, :], v[:, 5, :])
                dve.drain()
                dve.tensor_scalar(v[:, 7, :], v[:, 6, :], CAPACITY, 1.0, ALU.mult, ALU.min)
                dve.drain()
                dve.tensor_tensor(v[:, 2, :], v[:, 1, :], v[:, 7, :], ALU.mult)
                dve.drain()
                softmax(2, 1, 4)
                dve.max(top[:, 0, :], v[:, 4, :])
                dve.drain()
                dve.max_index(place[:, :], top[:, 0, :], v[:, 4, :])
                dve.tensor_tensor(one[:, 4:5], top[:, 0, 1:2], top[:, 0, 0:1], ALU.subtract).then_inc(act_in, 1)
                dve.drain()
                dve.tensor_copy(sh.expert[:, :], place[:, 0:2])
                dve.tensor_copy(place_f[:, :], place[:, 0:2])
                dve.wait_ge(act_out, 3)
                dve.tensor_scalar(one[:, 5:6], one[:, 4:5], 1.0, None, ALU.add)
                dve.drain()
                dve.reciprocal(sh.share[:, 0:1], one[:, 5:6])
                dve.drain()
                dve.tensor_tensor(sh.share[:, 1:2], sh.share[:, 0:1], one[:, 4:5], ALU.mult)
                dve.drain()
                for j in range(2):
                    dve.tensor_scalar(v[:, 5 + j, :], sh.lane[:, 0:X8], place_f[:, j:j + 1], sh.share[:, j:j + 1],
                                      ALU.is_equal, ALU.mult)
                dve.drain()
                dve.tensor_tensor(dense[:, :], v[:, 5, :], v[:, 6, :], ALU.add)
                dve.drain()
                dve.tensor_tensor(v[0:X8, 7, :], dense[0:X8, :], sh.ident[0:X8, 0:X8], ALU.mult)
                dve.drain()
                dve.tensor_reduce(column[:, :], v[0:X8, 7, :], AX.X, ALU.add).then_inc(column_ready, 1)
                dve.wait_ge(prod, 2)
                dve.tensor_copy(row[:, :], bank[:, 1, 0:D]).then_inc(row_ready, 1)
                dve.drain()
                for g in range(3, TG):
                    t = slice(g * TU, (g + 1) * TU)
                    dve.tensor_tensor(sh.xn[:, t, :], sh.xn[:, t, :], row[:, :].unsqueeze(1).to_broadcast([P, TU, D]),
                                      ALU.add)


def build(nc, a, out):
    with ExitStack() as ctx:
        def sb(name, shape, dt=F32):
            return ctx.enter_context(nc.sbuf_tensor(name, shape, dt))

        def dram(name, shape, dt=F32):
            return nc.dram_tensor(name, shape, dt, kind="Internal").ap()

        def blocks(w):
            return w.rearrange("(k p) f -> p k f", p=P)

        sh = Shared()
        sh.first_semaphore, sh.semaphores = 130, 0
        sh.dst_p = dram("dst_p", (EP,), I32)
        sh.src_p = dram("src_p", (EP,), I32)
        sh.ew_p = dram("ew_p", (EP,))
        sh.ef_p = dram("ef_p", (ED, EP))
        sh.tile_d = dram("tile_d", (NI,), I32)
        sh.chunk_d = dram("chunk_d", (NI,), I32)
        sh.key_d = dram("key_d", (NI, EC))
        sh.goal_d = dram("goal_d", (NI, EC), BF16)
        sh.xn_d = dram("xn_d", (NP, D))
        sh.k_d = dram("k_d", (NP, D))
        sh.v_d = dram("v_d", (NP, D))
        sh.scores_d = dram("scores_d", (H, NS, P))

        sh.ident = sb("ident", [P, P])
        sh.lane = sb("lane", [P, P])
        sh.ones = sb("ones", [P, P])
        sh.ones_b = sb("ones_b", [1, P], BF16)
        sh.minus_row = sb("minus_row", [P, 1])
        sh.tile_id = sb("tile_id", [1, NI], I32)
        sh.chunk_id = sb("chunk_id", [1, NI], I32)
        sh.src_of = sb("src_of", [P, NS], I32)
        sh.lane_of = sb("lane_of", [P, NS])
        sh.weight_of = sb("weight_of", [P, NS])
        sh.x = sb("x", [P, NT, D])
        sh.xn = sb("xn", [P, NT, D])
        sh.xt = sb("xt", [P, KB, NP])
        sh.acc = sb("acc", [P, NT, D + H])
        sh.work = sh.acc[:, :, 0:D]
        sh.beta = sb("beta", [P, 1])
        sh.expert = sb("expert", [P, 2], I32)
        sh.share = sb("share", [P, 2])
        sh.ef_copied = ctx.enter_context(nc.semaphore("ef_copied"))

        stage_edge_tables(nc, sh, a["dst"], a["src"], a["edge_weight"], a["ef_t"])

        stage_norm(nc, sh, "n0", load=a["x"], table=sh.xn_d, source=sh.x, to=sh.xn)
        stage_aggregate(nc, sh)
        with nc.sbuf_tensor("c0", [P, KB, D], F32) as sh.c0:
            stage_mix0(nc, sh, blocks(a["L0_mix_Wk"]), blocks(a["L0_mix_Wv"]), a["L0_mix_Wq_t"], a["L0_mix_W_out"])
            stage_gnn0(nc, sh, blocks(a["L0_gnn_w1_t"]), blocks(a["L0_gnn_w2_t"]), a["L0_gnn_gamma1_f"],
                       a["L0_gnn_beta1_f"], a["L0_gnn_gamma_h_f"], a["L0_gnn_beta_h_f"], a["L0_gnn_eps_weight"],
                       a["L0_mix_b_out_f"])
        clear_semaphores(nc, sh)
        stage_norm(nc, sh, "n1", source=sh.x, to=sh.xn)
        with nc.sbuf_tensor("gate", [P, NT, 8], F32) as sh.gate:
            stage_gate(nc, sh, blocks(a["L0_ffn_Wg"]), a["L0_ffn_bg"], a["L0_ffn_bias"], a["L0_ffn_b2"])
            gate = sh.gate[:, :, :].rearrange("p t e -> p (t e)")

            def expert0(array, pattern):
                return lambda pair, q: a[array][bass.ds(2 * pair + q, 1)].rearrange(pattern, p=P)

            stage_ffn(nc, sh, "moe", 8, expert0("L0_ffn_W1", "e (k p) f -> p (e k) f"),
                      expert0("L0_ffn_W2", "e (k p) f -> p (e k) f"), expert0("L0_ffn_b1_f", "e p k -> p (e k)"),
                      ACT.Relu, lambda t, pair, q: gate[:, bass.ds(t * 8 + (2 * pair + q), 1)], sh.x)

        def halves(pre):
            w1 = blocks(a[pre + "W1"])
            w2 = a[pre + "W2"].rearrange("(e k p) f -> p e k f", p=P, e=2)
            return (lambda pair, q: w1[:, :, q * F1:(q + 1) * F1], lambda pair, q: w2[:, q],
                    lambda pair, q: a[pre + "b1_f"][q])

        stage_norm(nc, sh, "n2", source=sh.x, to=sh.xn)
        stage_mix1(nc, sh, *[blocks(a["L1_mix_" + w]) for w in ("Wq", "Wk", "Wv", "Wo")],
                   *[a["L1_mix_" + b] for b in ("bq_f", "bk_f", "bv_f", "bo")])
        stage_norm(nc, sh, "n3", source=sh.work, to=sh.work, gain=a["L1_mix_ln1_g_f"], shift=a["L1_mix_ln1_b_f"])
        stage_rows(nc, sh, "r3", a["L1_mix_ln1_g"], a["L1_mix_ln1_b"], [a["L1_mix_b2"]])
        stage_ffn(nc, sh, "ffm", 2, *halves("L1_mix_"), ACT.Relu, lambda t, pair, q: sh.ones[:, 0:1], sh.work)
        stage_norm(nc, sh, "n4", source=sh.work, to=sh.work, turn=False)
        stage_rows(nc, sh, "r4", a["L1_mix_ln2_g"], a["L1_mix_ln2_b"], into=sh.x)
        clear_semaphores(nc, sh)

        stage_norm(nc, sh, "n5", source=sh.xn, to=sh.work, gain=a["L1_gnn_ln1_g_f"], shift=a["L1_gnn_ln1_b_f"])
        with nc.sbuf_tensor("scores", [P, NS * H], F32) as sh.scores:
            sh.q = sh.work
            stage_project(nc, sh, blocks(a["L1_gnn_Wqkv"]), a["L1_gnn_bq"], a["L1_gnn_bk"], a["L1_gnn_bv"])
            stage_scores(nc, sh, a["L1_gnn_We"], a["L1_gnn_be"])
            stage_softmax(nc, sh)
            stage_attend(nc, sh)
        clear_semaphores(nc, sh)
        stage_attention_out(nc, sh, blocks(a["L1_gnn_Wo"]), a["L1_gnn_bo"], a["L1_gnn_alpha"], a["L1_gnn_beta"],
                            a["L1_gnn_b2"])
        stage_norm(nc, sh, "n6", source=sh.xn, to=sh.work, gain=a["L1_gnn_ln2_g_f"], shift=a["L1_gnn_ln2_b_f"])
        stage_ffn(nc, sh, "ffg", 2, *halves("L1_gnn_"), ACT.Gelu, lambda t, pair, q: sh.beta[:, 0:1], sh.x)

        stage_norm(nc, sh, "n7", source=sh.x, to=sh.xn)
        stage_route(nc, sh, blocks(a["L1_ffn_Wr"]), a["L1_ffn_br"], a["L1_ffn_b2"])

        def expert1(array, pattern):
            def part(pair, q):
                e = nc.sync.value_load(sh.expert[0:1, q:q + 1], min_val=0, max_val=7)
                return a[array][bass.ds(e, 1)].rearrange(pattern, p=P)
            return part

        stage_ffn(nc, sh, "ffx", 2, expert1("L1_ffn_W1", "e (k p) f -> p (e k) f"),
                  expert1("L1_ffn_W2", "e (k p) f -> p (e k) f"), expert1("L1_ffn_b1_f", "e p k -> p (e k)"),
                  ACT.Gelu, lambda t, pair, q: sh.share[:, q:q + 1], sh.xn)
        stage_norm(nc, sh, "n8", source=sh.xn, to=sh.work, turn=False)
        stage_rows(nc, sh, "r8", a["L1_ffn_gamma"], a["L1_ffn_beta"], into=sh.x, out=out)


def kernel(**inputs):
    import numpy as np
    import concourse.bacc as bacc
    from concourse.bass_utils import run_bass_kernel_spmd

    given = {name: np.asarray(array) for name, array in inputs.items()}

    def by_feature(v, parts=()):
        v = v.reshape(*parts, -1, P)
        return np.swapaxes(v, -1, -2)

    laid = {name: given[name] for name in (
        "x", "src", "dst", "edge_weight", "L0_gnn_eps_weight", "L0_mix_W_out", "L0_ffn_Wg", "L0_ffn_bg",
        "L0_ffn_bias", "L0_ffn_W1", "L0_ffn_W2", "L0_ffn_b2", "L1_gnn_bq", "L1_gnn_bk", "L1_gnn_bv",
        "L1_gnn_We", "L1_gnn_Wo", "L1_gnn_bo", "L1_gnn_W1", "L1_gnn_W2", "L1_gnn_b2", "L1_gnn_alpha",
        "L1_gnn_beta", "L1_mix_Wq", "L1_mix_Wk", "L1_mix_Wv", "L1_mix_Wo", "L1_mix_bo", "L1_mix_W1", "L1_mix_W2",
        "L1_mix_b2", "L1_mix_ln1_g", "L1_mix_ln1_b", "L1_mix_ln2_g", "L1_mix_ln2_b", "L1_ffn_Wr", "L1_ffn_br",
        "L1_ffn_W1", "L1_ffn_W2", "L1_ffn_b2", "L1_ffn_gamma", "L1_ffn_beta")}
    for name in ("L0_gnn_gamma1", "L0_gnn_beta1", "L0_gnn_gamma_h", "L0_gnn_beta_h", "L0_mix_b_out",
                 "L1_mix_bq", "L1_mix_bk", "L1_mix_bv", "L1_mix_ln1_g", "L1_mix_ln1_b", "L1_gnn_ln1_g",
                 "L1_gnn_ln1_b", "L1_gnn_ln2_g", "L1_gnn_ln2_b"):
        laid[name + "_f"] = by_feature(given[name])
    laid["L0_ffn_b1_f"] = by_feature(given["L0_ffn_b1"], (8,))
    laid["L1_ffn_b1_f"] = by_feature(given["L1_ffn_b1"], (8,))
    laid["L1_mix_b1_f"] = by_feature(given["L1_mix_b1"], (2,))
    laid["L1_gnn_b1_f"] = by_feature(given["L1_gnn_b1"], (2,))
    laid["ef_t"] = given["edge_attr_64"].T
    laid["L1_gnn_be"] = given["L1_gnn_be"].reshape(1, DH)
    laid["L1_gnn_Wqkv"] = np.concatenate([given["L1_gnn_" + w] for w in ("Wq", "Wk", "Wv")], axis=1)
    laid["L0_gnn_w1_t"], laid["L0_gnn_w2_t"] = given["L0_gnn_w1"].T, given["L0_gnn_w2"].T
    qkv = given["L0_mix_W_qkv"]
    laid["L0_mix_Wq_t"], laid["L0_mix_Wk"], laid["L0_mix_Wv"] = qkv[:, 0:P].T, qkv[:, P:2 * P], qkv[:, 2 * P:3 * P]

    nc = bacc.Bacc("TRN2", target_bir_lowering=False, num_devices=1)
    arrays, args = {}, {}
    for name, array in laid.items():
        array = np.ascontiguousarray(array)
        arrays[f"in_{name}_dram"] = array
        args[name] = nc.dram_tensor(f"in_{name}_dram", array.shape, mybir.dt.from_np(array.dtype),
                                    kind="ExternalInput").ap()
    out = nc.dram_tensor("out_0_dram", (N, D), F32, kind="ExternalOutput").ap()
    build(nc, args, out)
    result = run_bass_kernel_spmd(nc, [arrays], core_ids=[0])
    return np.asarray(result.results[0]["out_0_dram"])
```

```python
from contextlib import ExitStack, contextmanager

import concourse.bass as bass
from concourse import mybir

F32 = mybir.dt.float32
I32 = mybir.dt.int32
U32 = mybir.dt.uint32
BF16 = mybir.dt.bfloat16
ACT = mybir.ActivationFunctionType
ALU = mybir.AluOpType
AX = mybir.AxisListType

N, D, E, ED = 3125, 256, 100000, 64
P = 128
NT = -(-N // P)
NP = NT * P
KB = D // P
SUBS = 4
EC = SUBS * P
NCH = -(-E // EC)
EP = NCH * EC
NI = NCH + NT - 1
HI = NI // 2
NS = NI * SUBS
PAD_DST = NP - 1
H, DH = 8, 32
EPS = 1e-5
TU = 5
TG = NT // TU
COLS = [(g * 512, min(512, N - g * 512)) for g in range(-(-N // 512))]
assert NI % 4 == 0 and TG * TU == NT and NCH * EC >= E and HI <= P


def hold(eng, sem, value, ticks):
    eng.wait_ge(sem, value)
    eng.sem_inc(ticks, 1)


class Shared:
    pass


@contextmanager
def semaphore(nc, sh, name):
    with nc.semaphore(name, num=sh.first_semaphore + sh.semaphores) as handle:
        sh.semaphores += 1
        yield handle


def clear_semaphores(nc, sh):
    with nc.Block() as block:
        @block.sync
        def _(sp):
            sp.sem_clear(range(sh.first_semaphore, sh.first_semaphore + sh.semaphores))
    sh.semaphores = 0


def stage_copy_edges(nc, sh, dst, src, ew):
    R, W = 125, E // 125
    with ExitStack() as ctx:
        def sb(name, shape, dt=F32):
            return ctx.enter_context(nc.sbuf_tensor(name, shape, dt))

        def sem(name):
            return ctx.enter_context(semaphore(nc, sh, name))

        pad_i = sb("pad_i", [1, 2, EP - E], I32)
        pad_f = sb("pad_f", [1, EP - E])
        here = sb("here", [R, W], I32)
        after = sb("after", [R, W], I32)
        falls = sb("falls", [R, W])
        any_fall = sb("any_fall", [R, 1])
        count = ctx.enter_context(nc.psum_tensor("fall_count", [P, 512], F32))
        pads_set = sem("pads_set")
        arrays_in = sem("arrays_in")
        pairs_in = sem("pairs_in")
        falls_ready = sem("falls_ready")
        counted = sem("counted")

        with nc.Block() as block:
            @block.sync
            def _(sp):
                for to, of in ((sh.dst_p, dst), (sh.src_p, src), (sh.ew_p, ew)):
                    sp.dma_start(to[0:E].rearrange("(p e) -> p e", p=R), of.rearrange("(p e) -> p e", p=R)
                                 ).then_inc(arrays_in, 16)
                sp.wait_ge(pads_set, 5)
                sp.dma_start(sh.dst_p[E:EP].rearrange("(a e) -> a e", a=1), pad_i[:, 0, :]).then_inc(arrays_in, 16)
                sp.dma_start(sh.src_p[E:EP].rearrange("(a e) -> a e", a=1), pad_i[:, 1, :]).then_inc(arrays_in, 16)
                sp.dma_start(sh.ew_p[E:EP].rearrange("(a e) -> a e", a=1), pad_f[:, :]).then_inc(arrays_in, 16)
                sp.wait_ge(arrays_in, 96)

            @block.scalar
            def _(act):
                act.dma_start(here[:, :], dst.rearrange("(p e) -> p e", p=R)).then_inc(pairs_in, 16)
                act.dma_start(after[0:R - 1, :], dst[1:1 + (R - 1) * W].rearrange("(p e) -> p e", p=R - 1)
                              ).then_inc(pairs_in, 16)
                act.dma_start(after[R - 1:R, 0:W - 1], dst[1 + (R - 1) * W:E].rearrange("(a e) -> a e", a=1)
                              ).then_inc(pairs_in, 16)

            @block.gpsimd
            def _(pool):
                pool.wait_ge(pads_set, 5)
                pool.affine_select(out=sh.ident[:, :], in_=sh.ones[:, :], compare_op=ALU.is_equal, fill=0.0,
                                   base=0, pattern=[[-1, P]], channel_multiplier=1)

            @block.vector
            def _(dve):
                dve.memset(pad_i[:, 0, :], PAD_DST).then_inc(pads_set, 1)
                dve.memset(pad_i[:, 1, :], 0).then_inc(pads_set, 1)
                dve.memset(pad_f[:, :], 0.0).then_inc(pads_set, 1)
                dve.memset(sh.ones[:, :], 1.0).then_inc(pads_set, 1)
                dve.memset(sh.zeros[:, :], 0.0).then_inc(pads_set, 1)
                dve.memset(falls[:, :], 0.0)
                dve.wait_ge(pairs_in, 48)
                dve.drain()
                dve.tensor_tensor(falls[:, 0:W - 1], here[:, 0:W - 1], after[:, 0:W - 1], ALU.is_gt)
                dve.tensor_tensor(falls[0:R - 1, W - 1:W], here[0:R - 1, W - 1:W], after[0:R - 1, W - 1:W], ALU.is_gt)
                dve.drain()
                dve.tensor_reduce(any_fall[:, :], falls[:, :], AX.X, ALU.max).then_inc(falls_ready, 1)
                dve.wait_ge(counted, 1)
                dve.tensor_copy(sh.unsorted[:, :], count[0:1, 0:1])

            @block.tensor
            def _(pe):
                pe.wait_ge(falls_ready, 1)
                pe.wait_ge(pads_set, 5)
                pe.matmul(count[0:1, 0:1], any_fall[:, :], sh.ones[0:R, 0:1], start=True, stop=True).then_inc(counted, 1)


def stage_sort(nc, sh, ef):
    J = EP // P
    BANKS = [(c, min(512, NP - c)) for c in range(0, NP, 512)]
    with ExitStack() as ctx:
        def sb(n, shape, dt=F32):
            return ctx.enter_context(nc.sbuf_tensor(f"sort_{n}", shape, dt))

        def sem(n):
            return ctx.enter_context(semaphore(nc, sh, f"sort_{n}"))

        arrays = [sb("dst", [P, J], I32), sb("src", [P, J], I32), sb("ew", [P, J]), sb("id", [P, J], I32)]
        sorted_d = [sh.dst_p, sh.src_p, sh.ew_p, sh.order_d]
        dst_f = sb("dst_f", [P, J])
        node_i = sb("node_i", [P, NP], I32)
        node = sb("node", [P, NP])
        earlier = sb("earlier", [P, P])
        start = sb("start", [P, NP])
        here = sb("here", [P, NP])
        place = sb("place", [P, NP])
        rank = sb("rank", [P, J])
        to = sb("to", [P, 1], I32)
        sent = [sb(f"sent{n}", [P, 1], a.dtype) for n, a in enumerate(arrays)]
        of = sb("of", [P, 1], I32)
        row = sb("row", [P, ED])
        column = sb("column", [ED, P])
        bank = ctx.enter_context(nc.psum_tensor("sort_bank", [P, 7, 512], F32))
        turned = ctx.enter_context(nc.psum_tensor("sort_turned", [P, 512], F32))
        loaded = sem("loaded")
        made = sem("made")
        here_ready = sem("here_ready")
        counted = sem("counted")
        pool_ticks = sem("pool_ticks")
        pe_ticks = sem("pe_ticks")
        send_ready = sem("send_ready")
        scattered = [ctx.enter_context(nc.semaphore(f"sort_scattered{n}")) for n in range(4)]
        sent_out = sem("sent_out")
        order_in = sem("order_in")
        order_ready = sem("order_ready")
        row_in = ctx.enter_context(nc.semaphore("sort_row_in"))
        turn_ready = sem("turn_ready")
        column_ready = sem("column_ready")
        column_out = sem("column_out")
        flat = bank[:, :, :].rearrange("p b c -> p (b c)")

        with nc.Block() as block:
            @block.sync
            def _(sp):
                with sp.If(sp.value_load(sh.unsorted[0:1, 0:1], min_val=0, max_val=P) != 0):
                    for n, d in enumerate((sh.dst_p, sh.src_p, sh.ew_p)):
                        sp.dma_start(arrays[n][:, :], d.rearrange("(p j) -> p j", p=P)).then_inc(loaded, 16)
                    sp.wait_ge(sent_out, 4 * J + 4)
                    sp.sem_inc(column_out, 16)
                    with sp.Fori(0, J) as j:
                        sp.wait_ge(column_out, 16 * j + 16)
                        sp.dma_start(of[:, :], sh.order_d[bass.ds(j * P, P)].rearrange("(p a) -> p a", a=1)
                                     ).then_inc(order_in, 16)
                        sp.wait_ge(column_ready, j + 1)
                        sp.dma_start(sh.ef_p[:, bass.ds(j * P, P)], column[:, :]).then_inc(column_out, 16)
                    sp.wait_ge(column_out, 16 * J + 16)

            @block.gpsimd
            def _(pool):
                with pool.If(pool.value_load(sh.unsorted[0:1, 0:1], min_val=0, max_val=P) != 0):
                    pool.iota(arrays[3][:, :], pattern=[[1, J]], base=0, channel_multiplier=J).then_inc(made, 1)
                    pool.iota(node_i[:, :], pattern=[[1, NP]], base=0, channel_multiplier=0).then_inc(made, 1)
                    pool.affine_select(out=earlier[:, :], in_=sh.ones[:, :], compare_op=ALU.is_gt, fill=0.0,
                                       base=0, pattern=[[1, P]], channel_multiplier=-1).then_inc(made, 1)
                    with pool.Fori(0, J) as j:
                        hold(pool, send_ready, j + 1, pool_ticks)
                        for n in range(4):
                            pool.indirect_dma_start(sorted_d[n].rearrange("(e a) -> e a", a=1),
                                                    bass.IndirectOffsetOnAxis(ap=to[:, 0:1], axis=0),
                                                    sent[n][:, :], None).then_inc(scattered[n], 16)
                        for n in range(4):
                            hold(pool, scattered[n], 16 * j + 16, sent_out)
                    with pool.Fori(0, J) as j:
                        hold(pool, order_ready, j + 1, pool_ticks)
                        pool.indirect_dma_start(row[:, :], None, ef, bass.IndirectOffsetOnAxis(ap=of[:, 0:1], axis=0)
                                                ).then_inc(row_in, 16)

            @block.tensor
            def _(pe):
                with pe.If(pe.value_load(sh.unsorted[0:1, 0:1], min_val=0, max_val=P) != 0):
                    pe.wait_ge(here_ready, 1)
                    for b, (c, w) in enumerate(BANKS):
                        last = pe.matmul(bank[:, b, 0:w], sh.ones[:, :], start[:, c:c + w], start=True, stop=True)
                    last.then_inc(counted, 1)
                    pe.wait_ge(made, 3)
                    with pe.Fori(0, J) as j:
                        for n, lhs in enumerate((earlier, sh.ones)):
                            pe.wait_ge(here_ready, 2 * j + (n + 2))
                            for b, (c, w) in enumerate(BANKS):
                                last = pe.matmul(bank[:, b, 0:w], lhs[:, :], here[:, c:c + w], start=True, stop=True)
                            last.then_inc(counted, 1)
                    with pe.Fori(0, J) as j:
                        hold(pe, row_in, 16 * j + 16, pe_ticks)
                        pe.transpose(turned[0:ED, 0:P], row[:, :], sh.ident[:, :]).then_inc(turn_ready, 1)

            @block.vector
            def _(dve):
                with dve.If(dve.value_load(sh.unsorted[0:1, 0:1], min_val=0, max_val=P) != 0):
                    dve.memset(start[:, :], 0.0)
                    dve.wait_ge(loaded, 48)
                    dve.wait_ge(made, 3)
                    dve.tensor_copy(dst_f[:, :], arrays[0][:, :])
                    dve.tensor_copy(node[:, :], node_i[:, :])
                    dve.drain()
                    with dve.Fori(0, J) as j:
                        dve.scalar_tensor_tensor(out=start[:, :], in0=node[:, :], scalar=dst_f[:, bass.ds(j, 1)],
                                                 in1=start[:, :], op0=ALU.is_equal, op1=ALU.add)
                        dve.drain()
                    dve.sem_inc(here_ready, 1)
                    dve.wait_ge(counted, 1)
                    dve.tensor_copy(here[:, :], flat[:, 0:NP])
                    dve.memset(place[:, :], 1.0)
                    dve.drain()
                    dve.tensor_tensor_scan(start[:, :], place[:, :], here[:, :], 0.0, ALU.mult, ALU.add)
                    dve.drain()
                    dve.tensor_tensor(start[:, :], start[:, :], here[:, :], ALU.subtract)
                    dve.drain()
                    with dve.Fori(0, J) as j:
                        dve.tensor_scalar(here[:, :], node[:, :], dst_f[:, bass.ds(j, 1)], None, ALU.is_equal)
                        dve.drain()
                        dve.sem_inc(here_ready, 1)
                        dve.wait_ge(counted, 2 * j + 2)
                        dve.tensor_tensor(place[:, :], start[:, :], flat[:, 0:NP], ALU.add)
                        dve.drain()
                        dve.sem_inc(here_ready, 1)
                        dve.tensor_tensor(place[:, :], place[:, :], here[:, :], ALU.mult)
                        dve.drain()
                        dve.tensor_reduce(rank[:, bass.ds(j, 1)], place[:, :], AX.X, ALU.add)
                        dve.wait_ge(counted, 2 * j + 3)
                        dve.tensor_tensor(start[:, :], start[:, :], flat[:, 0:NP], ALU.add)
                        dve.drain()
                    dve.sem_inc(sent_out, 4)
                    with dve.Fori(0, J) as j:
                        dve.wait_ge(sent_out, 4 * j + 4)
                        dve.tensor_copy(to[:, :], rank[:, bass.ds(j, 1)])
                        for n in range(4):
                            dve.tensor_copy(sent[n][:, :], arrays[n][:, bass.ds(j, 1)])
                        dve.drain()
                        dve.sem_inc(send_ready, 1)
                    with dve.Fori(0, J) as j:
                        dve.wait_ge(order_in, 16 * j + 16)
                        dve.tensor_scalar(of[:, :], of[:, :], E - 1, None, ALU.min)
                        dve.drain()
                        dve.sem_inc(order_ready, 1)
                        dve.wait_ge(turn_ready, j + 1)
                        dve.tensor_copy(column[:, :], turned[0:ED, 0:P])
                        dve.drain()
                        dve.sem_inc(column_ready, 1)


def stage_edge_tables(nc, sh):
    with ExitStack() as ctx:
        def sb(name, shape, dt=F32):
            return ctx.enter_context(nc.sbuf_tensor(name, shape, dt))

        def sem(name):
            return ctx.enter_context(semaphore(nc, sh, name))

        iota_i = sb("iota_i", [P, NCH], I32)
        iota_c = sb("iota_c", [P, NCH])
        inc_i = sb("inc_i", [P, 2], I32)
        inc_f = sb("inc_f", [P, 2])
        row_i = sb("row_i", [P, P], I32)
        ends = sb("ends", [1, 2, NCH], I32)
        ends_t = sb("ends_t", [1, 2, NCH], I32)
        ends_f = sb("ends_f", [1, 2, NCH])
        tiles = sb("tiles", [P, 2, NCH])
        count = sb("count", [P, NCH])
        through = sb("through", [P, NCH])
        before = sb("before", [P, NCH])
        base = sb("base", [P, NCH])
        hit = sb("hit", [P, 2, NCH])
        seen = sb("seen", [P, 2])
        chunk = sb("chunk", [P, 2])
        bsel = sb("bsel", [P, 2])
        tile = sb("tile", [P, 2])
        shift = sb("shift", [P, 2])
        tclip = sb("tclip", [P, 2])
        chunk_i = sb("chunk_i", [P, 2], I32)
        tclip_i = sb("tclip_i", [P, 2], I32)
        dst_r = sb("dst_r", [P, 2, EC], I32)
        src_r = sb("src_r", [P, 2, EC], I32)
        rows = sb("rows", [P, 3, 2, EC])
        dst_f = sb("dst_f", [P, 2, EC])
        valid = sb("valid", [P, 2, EC])
        inside = sb("inside", [P, 2, EC])
        key = sb("key", [P, 2, EC])
        goal = sb("goal", [P, 2, EC], BF16)
        wide = ctx.enter_context(nc.psum_tensor("wide", [P, 512], F32))
        turned = ctx.enter_context(nc.psum_tensor("turned", [P, 6, 512], F32))

        ends_in = sem("ends_in")
        iotas = sem("iotas")
        ends_ready = sem("ends_ready")
        ends_wide = sem("ends_wide")
        chunks_ready = sem("chunks_ready")
        rows_in = ctx.enter_context(nc.semaphore("rows_in"))
        rows_ready = sem("rows_ready")
        key_ready = sem("key_ready")
        goal_ready = sem("goal_ready")
        turned_ready = sem("turned_ready")
        ids_out = sem("ids_out")
        ids_in = sem("ids_in")

        with nc.Block() as block:
            @block.sync
            def _(sp):
                with nc.allow_non_contiguous_dma(reason="two words of each chunk"):
                    d = sh.dst_p.rearrange("(a c e) -> a c e", a=1, e=EC)
                    sp.dma_start(ends[:, 0, :], d[:, :, 0]).then_inc(ends_in, 16)
                    sp.dma_start(ends[:, 1, :], d[:, :, EC - 1]).then_inc(ends_in, 16)
                    sp.wait_ge(chunks_ready, 1)
                    sp.dma_start(sh.tile_d.rearrange("(b p) -> p b", b=2), tclip_i[0:HI, :]).then_inc(ids_out, 16)
                    sp.dma_start(sh.chunk_d.rearrange("(b p) -> p b", b=2), chunk_i[0:HI, :]).then_inc(ids_out, 16)
                sp.wait_ge(ids_out, 32)
                sp.dma_start(sh.tile_id[:, 0:NI], sh.tile_d.rearrange("(a i) -> a i", a=1)).then_inc(ids_in, 16)
                sp.dma_start(sh.chunk_id[:, 0:NI], sh.chunk_d.rearrange("(a i) -> a i", a=1)).then_inc(ids_in, 16)
                sp.wait_ge(goal_ready, 1)
                sp.dma_start(sh.goal_d.rearrange("(b p) e -> p b e", b=2), goal[0:HI, :, :]).then_inc(ids_in, 16)
                sp.wait_ge(key_ready, 1)
                sp.dma_start(sh.key_d.rearrange("(b p) e -> p b e", b=2), key[0:HI, :, :]).then_inc(ids_in, 16)
                sp.wait_ge(ids_in, 64)

            @block.gpsimd
            def _(pool):
                pool.iota(iota_i[:, :], pattern=[[1, NCH]], base=0, channel_multiplier=0).then_inc(iotas, 1)
                pool.iota(inc_i[:, :], pattern=[[HI, 2]], base=0, channel_multiplier=1).then_inc(iotas, 1)
                pool.iota(row_i[:, :], pattern=[[1, P]], base=0, channel_multiplier=0).then_inc(iotas, 1)
                pool.wait_ge(chunks_ready, 1)
                for b in range(2):
                    for to, of in ((dst_r[0:HI, b, :], sh.dst_p), (src_r[0:HI, b, :], sh.src_p),
                                   (rows[0:HI, 2, b, :], sh.ew_p)):
                        pool.indirect_dma_start(to, None, of.rearrange("(c e) -> c e", e=EC),
                                                bass.IndirectOffsetOnAxis(ap=chunk_i[0:HI, b:b + 1], axis=0)
                                                ).then_inc(rows_in, 16)

            @block.tensor
            def _(pe):
                pe.wait_ge(ends_ready, 1)
                pe.matmul(wide[:, 0:2 * NCH], sh.ones[0:1, :], ends_f[:, :, :].rearrange("a b c -> a (b c)"),
                          start=True, stop=True).then_inc(ends_wide, 1)
                pe.wait_ge(rows_ready, 1)
                for a in range(3):
                    for b in range(2):
                        for k in range(SUBS):
                            last = pe.transpose(turned[:, 2 * a + b, k * HI:(k + 1) * HI],
                                                rows[0:HI, a, b, k * P:(k + 1) * P], sh.ident[0:HI, 0:HI])
                        last.then_inc(turned_ready, 1)

            @block.vector
            def _(dve):
                dve.wait_ge(iotas, 3)
                dve.tensor_copy(iota_c[:, :], iota_i[:, :])
                dve.tensor_copy(inc_f[:, :], inc_i[:, :])
                dve.tensor_scalar(sh.minus_row[:, :], inc_i[:, 0:1], -1.0, None, ALU.mult)
                dve.memset(sh.ones_b[:, :], 1.0)
                dve.memset(sh.src_of[:, NS:], 0)
                dve.tensor_copy(sh.lane[:, :], row_i[:, :])
                dve.wait_ge(ends_in, 32)
                dve.tensor_scalar(ends_t[:, :, :], ends[:, :, :], 7, None, ALU.arith_shift_right)
                dve.drain()
                dve.tensor_copy(ends_f[:, :, :], ends_t[:, :, :]).then_inc(ends_ready, 1)
                dve.wait_ge(ends_wide, 1)
                dve.tensor_copy(tiles[:, :, :].rearrange("p b c -> p (b c)"), wide[:, 0:2 * NCH])
                dve.drain()
                dve.scalar_tensor_tensor(out=count[:, :], in0=tiles[:, 1, :], scalar=1.0, in1=tiles[:, 0, :],
                                         op0=ALU.add, op1=ALU.subtract)
                dve.memset(hit[:, :, :], 1.0)
                dve.drain()
                dve.tensor_tensor_scan(through[:, :], hit[:, 0, :], count[:, :], 0.0, ALU.mult, ALU.add)
                dve.drain()
                dve.tensor_tensor(before[:, :], through[:, :], count[:, :], ALU.subtract)
                dve.drain()
                dve.tensor_tensor(base[:, :], tiles[:, 0, :], before[:, :], ALU.subtract)
                for b in range(2):
                    dve.tensor_scalar(hit[:, b, :], before[:, :], inc_f[:, b:b + 1], None, ALU.is_le)
                dve.drain()
                dve.tensor_reduce(seen[:, :], hit[:, :, :], AX.X, ALU.add)
                dve.drain()
                dve.tensor_scalar(chunk[:, :], seen[:, :], -1.0, None, ALU.add)
                dve.drain()
                for b in range(2):
                    dve.tensor_scalar(hit[:, b, :], iota_c[:, :], chunk[:, b:b + 1], None, ALU.is_equal)
                dve.drain()
                for b in range(2):
                    dve.tensor_tensor(hit[:, b, :], hit[:, b, :], base[:, :], ALU.mult)
                dve.drain()
                dve.tensor_reduce(bsel[:, :], hit[:, :, :], AX.X, ALU.add)
                dve.drain()
                dve.tensor_tensor(tile[:, :], bsel[:, :], inc_f[:, :], ALU.add)
                dve.drain()
                dve.tensor_scalar(tclip[:, :], tile[:, :], float(NT - 1), None, ALU.min)
                dve.tensor_scalar(shift[:, :], tile[:, :], float(P), None, ALU.mult)
                dve.tensor_copy(chunk_i[:, :], chunk[:, :])
                dve.drain()
                dve.tensor_copy(tclip_i[:, :], tclip[:, :]).then_inc(chunks_ready, 1)
                dve.wait_ge(rows_in, 96)
                dve.tensor_copy(dst_f[0:HI], dst_r[0:HI])
                dve.tensor_copy(rows[0:HI, 1], src_r[0:HI])
                dve.drain()
                for b in range(2):
                    dve.tensor_scalar(rows[0:HI, 0, b, :], dst_f[0:HI, b, :], shift[0:HI, b:b + 1], None,
                                      ALU.subtract)
                dve.drain().then_inc(rows_ready, 1)
                dve.tensor_copy(goal[0:HI], rows[0:HI, 0]).then_inc(goal_ready, 1)
                dve.tensor_scalar(inside[0:HI], rows[0:HI, 0], 0.0, None, ALU.is_ge)
                dve.drain()
                dve.scalar_tensor_tensor(out=valid[0:HI], in0=rows[0:HI, 0], scalar=float(P), in1=inside[0:HI],
                                         op0=ALU.is_lt, op1=ALU.mult)
                dve.drain()
                dve.scalar_tensor_tensor(out=inside[0:HI], in0=dst_f[0:HI], scalar=1.0, in1=valid[0:HI],
                                         op0=ALU.add, op1=ALU.mult)
                dve.drain()
                dve.tensor_scalar(key[0:HI], inside[0:HI], -1.0, None, ALU.add).then_inc(key_ready, 1)
                for a, to in enumerate((sh.lane_of, sh.src_of, sh.weight_of)):
                    for b in range(2):
                        dve.wait_ge(turned_ready, 2 * a + b + 1)
                        dve.tensor_copy(to[:, b * HI * SUBS:(b + 1) * HI * SUBS].rearrange("p (i k) -> p k i", k=SUBS),
                                        turned[:, 2 * a + b, 0:HI * SUBS].rearrange("p (k i) -> p k i", k=SUBS))


def stage_norm(nc, sh, name, load=None, table=None, turn=True, source=None, to=None, gain=None, shift=None):
    with ExitStack() as ctx:
        def sb(n, shape, dt=F32):
            return ctx.enter_context(nc.sbuf_tensor(f"{name}_{n}", shape, dt))

        def sem(n):
            return ctx.enter_context(semaphore(nc, sh, f"{name}_{n}"))

        stats = sb("stats", [P, NT, 6])
        mean_var = sb("mean_var", [P, NT, 2])
        var = sb("var", [P, NT])
        std = sb("std", [P, NT])
        rstd = sb("rstd", [P, NT])
        turned = ctx.enter_context(nc.psum_tensor(f"{name}_turned", [P, TU, 512], F32))
        affine = sb("affine", [P, 2, KB])
        loaded = sem("loaded")
        affine_in = sem("affine_in")
        var_ready = sem("var_ready")
        std_ready = sem("std_ready")
        rows_ready = sem("rows_ready")
        turn_ready = sem("turn_ready")
        turn_used = sem("turn_used")
        stored = sem("stored")
        act_ticks = sem("act_ticks")

        with nc.Block() as block:
            @block.sync
            def _(sp):
                if gain is not None:
                    sp.dma_start(affine[:, 0, :], gain).then_inc(affine_in, 16)
                    sp.dma_start(affine[:, 1, :], shift).then_inc(affine_in, 16)
                if load is not None:
                    sp.dma_start(source[:, 0:NT - 1, :],
                                 load[0:(NT - 1) * P, :].rearrange("(t p) f -> p t f", p=P)).then_inc(loaded, 16)
                    sp.wait_ge(loaded, 17)
                    sp.dma_start(source[0:N - (NT - 1) * P, NT - 1, :], load[(NT - 1) * P:N, :]).then_inc(loaded, 16)
                if table is not None:
                    for g in range(TG):
                        sp.wait_ge(rows_ready, TU * (g + 1))
                        sp.dma_start(table[g * TU * P:(g + 1) * TU * P, :].rearrange("(t p) f -> p t f", p=P),
                                     to[:, g * TU:(g + 1) * TU, :]).then_inc(stored, 16)
                    sp.wait_ge(stored, 16 * TG)

            @block.vector
            def _(dve):
                if load is not None:
                    dve.memset(source[:, NT - 1, :], 0.0).then_inc(loaded, 1)
                    dve.wait_ge(loaded, 33)
                if source is None:
                    dve.sem_inc(rows_ready, NT)
                    return
                for t in range(NT):
                    dve.bn_stats(stats[:, t, :], source[:, t, :])
                dve.drain()
                for t in range(NT):
                    dve.bn_aggr(mean_var[:, t, :], stats[:, t, :])
                dve.drain()
                dve.tensor_scalar(var[:, :], mean_var[:, :, 1], EPS, None, ALU.add).then_inc(var_ready, 1)
                dve.wait_ge(std_ready, 1)
                dve.reciprocal(rstd[:, :], std[:, :])
                dve.drain()
                with dve.Fori(0, TG) as g:
                    for u in range(TU):
                        dve.tensor_scalar(to[:, bass.ds(TU * g + u, 1), :], source[:, bass.ds(TU * g + u, 1), :],
                                          mean_var[:, bass.ds(TU * g + u, 1), 0], rstd[:, bass.ds(TU * g + u, 1)],
                                          ALU.subtract, ALU.mult).then_inc(rows_ready, 1)

            @block.scalar
            def _(act):
                if source is not None:
                    act.wait_ge(var_ready, 1)
                    act.activation(std[:, :], var[:, :], ACT.Sqrt).then_inc(std_ready, 1)
                if turn:
                    if gain is not None:
                        act.wait_ge(affine_in, 32)
                    act.sem_inc(turn_used, TU)
                    with act.Fori(0, TG) as g:
                        for u in range(TU):
                            hold(act, turn_ready, TU * g + (u + 1), act_ticks)
                            if gain is None:
                                act.activation(sh.xt[:, :, bass.ds((TU * g + u) * P, P)],
                                               turned[:, u, 0:KB * P].rearrange("p (k n) -> p k n", k=KB),
                                               ACT.Copy).then_inc(turn_used, 1)
                                continue
                            for k in range(KB):
                                last = act.activation(sh.xt[:, k, bass.ds((TU * g + u) * P, P)],
                                                      turned[:, u, k * P:(k + 1) * P], ACT.Identity,
                                                      bias=affine[:, 1, k:k + 1], scale=affine[:, 0, k:k + 1])
                            last.then_inc(turn_used, 1)

            @block.tensor
            def _(pe):
                for t in range(NT if turn else 0):
                    pe.wait_ge(rows_ready, t + 1)
                    pe.wait_ge(turn_used, t + 1)
                    for k in range(KB):
                        last = pe.transpose(turned[:, t % TU, k * P:(k + 1) * P],
                                            to[:, t, k * P:(k + 1) * P], sh.ident[:, :])
                    last.then_inc(turn_ready, 1)


def stage_aggregate(nc, sh):
    UI = 4
    NB = UI * SUBS
    W = D + 1
    with ExitStack() as ctx:
        def sb(n, shape, dt=F32):
            return ctx.enter_context(nc.sbuf_tensor(f"agg_{n}", shape, dt))

        def sem(n):
            return ctx.enter_context(semaphore(nc, sh, f"agg_{n}"))

        index = sb("index", [P, NB], I32)
        rows = sb("rows", [P, NB, W])
        member = sb("member", [P, NB, P])
        sums = ctx.enter_context(nc.psum_tensor("agg_sums", [P, UI, 512], F32))
        ready = sem("ready")
        index_ready = sem("index_ready")
        gathered, past = sh.gathered, list(sh.past)
        weighted = sem("weighted")
        member_ready = sem("member_ready")
        summed = sem("summed")
        added = sem("added")
        pool_ticks = sem("pool_ticks")
        act_ticks = sem("act_ticks")

        with nc.Block() as block:
            @block.sync
            def _(sp):
                sp.dma_start(sh.xs_d.rearrange("(p r) f -> p r f", p=P),
                             sh.zeros[:, :].unsqueeze(1).to_broadcast([P, (NGS + 1) * GS // P, D])
                             ).then_inc(sh.xs_zeroed, 16)

            @block.gpsimd
            def _(pool):
                with pool.Fori(0, NI // UI) as i:
                    for u in range(UI):
                        hold(pool, index_ready, UI * i + (u + 1), pool_ticks)
                        for k in range(SUBS):
                            q = u * SUBS + k
                            pool.indirect_dma_start(rows[:, q, 0:D], None, sh.xn_d,
                                                    bass.IndirectOffsetOnAxis(ap=index[:, q:q + 1], axis=0)
                                                    ).then_inc(gathered[q], 16)

            @block.scalar
            def _(act):
                with act.Fori(0, NI // UI) as i:
                    for u in range(UI):
                        for k in range(SUBS):
                            q = u * SUBS + k
                            hold(act, gathered[q], 16 * i + (past[q] + 16), act_ticks)
                            act.activation(rows[:, q, 0:D], rows[:, q, 0:D], ACT.Copy,
                                           scale=sh.weight_of[:, bass.ds((UI * i + u) * SUBS + k, 1)]
                                           ).then_inc(weighted, 1)

            @block.vector
            def _(dve):
                dve.memset(sh.acc[:, :, :], 0.0)
                dve.memset(rows[:, :, D:W], 1.0)
                dve.tensor_copy(index[:, :], sh.src_of[:, 0:NB])
                dve.drain()
                dve.sem_inc(index_ready, UI)
                dve.sem_inc(added, UI)
                with dve.Fori(0, NI // UI) as i:
                    for u in range(UI):
                        dve.wait_ge(summed, UI * i + (u + 1))
                        for k in range(SUBS):
                            dve.tensor_scalar(member[:, u * SUBS + k, :], sh.lane[:, :],
                                              sh.lane_of[:, bass.ds((UI * i + u) * SUBS + k, 1)], None,
                                              ALU.is_equal).then_inc(member_ready, 1)
                    for u in range(UI):
                        t = dve.value_load(sh.tile_id[0:1, bass.ds(UI * i + u, 1)], min_val=0, max_val=NT - 1)
                        dve.wait_ge(summed, UI * i + (u + 1 + UI))
                        dve.tensor_tensor(sh.acc[:, bass.ds(t, 1), 0:W].rearrange("p a w -> p (a w)"),
                                          sh.acc[:, bass.ds(t, 1), 0:W].rearrange("p a w -> p (a w)"),
                                          sums[:, u, 0:W], ALU.add).then_inc(added, 1)
                        dve.tensor_copy(index[:, u * SUBS:(u + 1) * SUBS],
                                        sh.src_of[:, bass.ds((UI * i + (u + UI)) * SUBS, SUBS)]).then_inc(index_ready, 1)
                        dve.drain()

            @block.tensor
            def _(pe):
                pe.sem_inc(summed, UI)
                with pe.Fori(0, NI // UI) as i:
                    for u in range(UI):
                        pe.wait_ge(added, UI * i + (u + 1))
                        for k in range(SUBS):
                            q = u * SUBS + k
                            pe.wait_ge(weighted, NB * i + (q + 1))
                            pe.wait_ge(member_ready, NB * i + (q + 1))
                            last = pe.matmul(sums[:, u, 0:W], member[:, q, :], rows[:, q, :],
                                             start=(k == 0), stop=(k == SUBS - 1))
                        last.then_inc(summed, 1)
        for q in range(NB):
            sh.past[q] += 16 * (NI // UI)



def stage_mix0(nc, sh, wk, wv, wq_t, w_out):
    HD = P
    with ExitStack() as ctx:
        def sb(n, shape, dt=F32):
            return ctx.enter_context(nc.sbuf_tensor(f"mix0_{n}", shape, dt))

        def ps(n, shape, dt=F32):
            return ctx.enter_context(nc.psum_tensor(f"mix0_{n}", shape, dt))

        def sem(n):
            return ctx.enter_context(semaphore(nc, sh, f"mix0_{n}"))

        wk_s = sb("wk", [P, KB, HD])
        wv_s = sb("wv", [P, KB, HD])
        wq_s = sb("wq", [HD, D])
        wo_s = sb("wo", [HD, D])
        kt = sb("kt", [HD, NP])
        top = sb("top", [HD, 1])
        low = sb("low", [HD, 1])
        total = sb("total", [HD, 1])
        scale = sb("scale", [HD, 1])
        ke = sb("ke", [P, 2, HD])
        z = sb("z", [HD, D])
        zt = sb("zt", [P, KB, HD])
        heads = sb("heads", [HD, HD])
        m = sb("m", [HD, D])
        keys = ps("keys", [P, 2, 512])
        turned = ps("turned", [P, 2, 512])
        zsum = ps("zsum", [P, 512])
        small = ps("small", [P, 2, 512])

        loaded = sem("loaded")
        keys_ready = sem("keys_ready")
        keys_kept = sem("keys_kept")
        top_ready = sem("top_ready")
        exp_ready = sem("exp_ready")
        turn_ready = sem("turn_ready")
        turn_kept = sem("turn_kept")
        pe_small = sem("pe_small")
        dve_small = sem("dve_small")

        with nc.Block() as block:
            @block.sync
            def _(sp):
                sp.dma_start(wk_s[:, :, :], wk).then_inc(loaded, 16)
                sp.dma_start(wv_s[:, :, :], wv).then_inc(loaded, 16)
                sp.dma_start(wq_s[:, :], wq_t).then_inc(loaded, 16)
                sp.dma_start(wo_s[:, :], w_out).then_inc(loaded, 16)

            @block.tensor
            def _(pe):
                pe.wait_ge(loaded, 64)
                for g, (c, w) in enumerate(COLS):
                    if g >= 2:
                        pe.wait_ge(keys_kept, g - 1)
                    for k in range(KB):
                        last = pe.matmul(keys[:, g % 2, 0:w], wk_s[:, k, :], sh.xt[:, k, c:c + w],
                                         start=(k == 0), stop=(k == KB - 1))
                    last.then_inc(keys_ready, 1)

                pe.wait_ge(exp_ready, 2)

                def turn(t):
                    if t >= 2:
                        pe.wait_ge(turn_kept, t - 1)
                    pe.transpose(turned[:, t % 2, 0:P], kt[:, t * P:(t + 1) * P], sh.ident[:, :]).then_inc(turn_ready, 1)

                turn(0)
                for t in range(NT):
                    if t + 1 < NT:
                        turn(t + 1)
                    pe.wait_ge(turn_kept, t + 1)
                    last = pe.matmul(zsum[:, 0:D], ke[:, t % 2, :], sh.xn[:, t, :], start=(t == 0), stop=(t == NT - 1))
                    last.then_inc(pe_small, 1)
                pe.wait_ge(dve_small, 1)
                for k in range(KB):
                    last = pe.transpose(small[:, 0, k * P:(k + 1) * P], z[:, k * P:(k + 1) * P], sh.ident[:, :])
                last.then_inc(pe_small, 1)
                pe.wait_ge(dve_small, 2)
                for k in range(KB):
                    last = pe.matmul(small[:, 1, 0:HD], wv_s[:, k, :], zt[:, k, :], start=(k == 0), stop=(k == KB - 1))
                last.then_inc(pe_small, 1)
                pe.wait_ge(dve_small, 3)
                pe.matmul(small[:, 0, 0:D], heads[:, :], wo_s[:, :], start=True, stop=True).then_inc(pe_small, 1)
                pe.wait_ge(dve_small, 4)
                for k in range(KB):
                    last = pe.matmul(small[:, 1, k * D:(k + 1) * D], wq_s[:, k * P:(k + 1) * P], m[:, :],
                                     start=True, stop=True)
                last.then_inc(pe_small, 1)

            @block.scalar
            def _(act):
                for g, (c, w) in enumerate(COLS):
                    act.wait_ge(keys_ready, g + 1)
                    act.activation(kt[:, c:c + w], keys[:, g % 2, 0:w], ACT.Copy).then_inc(keys_kept, 1)
                act.wait_ge(top_ready, 1)
                act.activation(kt[:, 0:N], kt[:, 0:N], ACT.Exp, bias=low[:, 0:1], accum_out=total[:, 0:1]
                               ).then_inc(exp_ready, 1)
                for t in range(NT):
                    act.wait_ge(turn_ready, t + 1)
                    if t >= 2:
                        act.wait_ge(pe_small, t - 1)
                    act.activation(ke[:, t % 2, :], turned[:, t % 2, 0:P], ACT.Copy).then_inc(turn_kept, 1)

            @block.vector
            def _(dve):
                dve.memset(kt[:, N:NP], 0.0).then_inc(exp_ready, 1)
                dve.memset(heads[:, :], 0.0)
                dve.wait_ge(keys_kept, len(COLS))
                dve.tensor_reduce(top[:, :], kt[:, 0:N], AX.X, ALU.max)
                dve.drain()
                dve.tensor_scalar(low[:, :], top[:, :], -1.0, None, ALU.mult).then_inc(top_ready, 1)
                dve.wait_ge(exp_ready, 2)
                dve.reciprocal(scale[:, :], total[:, :])
                dve.drain()
                dve.wait_ge(pe_small, NT)
                dve.tensor_scalar(z[:, :], zsum[:, 0:D], scale[:, 0:1], float(DH) ** -0.5, ALU.mult, ALU.mult
                                  ).then_inc(dve_small, 1)
                dve.wait_ge(pe_small, NT + 1)
                dve.tensor_copy(zt[:, :, :].rearrange("p k h -> p (k h)"), small[:, 0, 0:D]).then_inc(dve_small, 1)
                dve.wait_ge(pe_small, NT + 2)
                for h in range(HD // DH):
                    r = slice(h * DH, (h + 1) * DH)
                    last = dve.tensor_copy(heads[r, r], small[r, 1, r])
                last.then_inc(dve_small, 1)
                dve.wait_ge(pe_small, NT + 3)
                dve.tensor_copy(m[:, :], small[:, 0, 0:D]).then_inc(dve_small, 1)
                dve.wait_ge(pe_small, NT + 4)
                dve.tensor_copy(sh.c0[:, :, :].rearrange("p k f -> p (k f)"), small[:, 1, :])


def stage_gnn0(nc, sh, w1_t, w2_t, gamma1, beta1, gamma_h, beta_h, eps_w, b_out):
    NG = len(COLS)
    with ExitStack() as ctx:
        def sb(n, shape, dt=F32):
            return ctx.enter_context(nc.sbuf_tensor(f"gnn0_{n}", shape, dt))

        def ps(n, shape, dt=F32):
            return ctx.enter_context(nc.psum_tensor(f"gnn0_{n}", shape, dt))

        def sem(n):
            return ctx.enter_context(semaphore(nc, sh, f"gnn0_{n}"))

        w_s = sb("w", [P, 2, KB, D])
        gain = sb("gain", [P, 2, KB])
        shift = sb("shift", [P, 2, KB])
        bias = sb("bias", [P, KB])
        eps_s = sb("eps", [P, 1])
        yt = sb("yt", [P, KB, NP])
        ht = sb("ht", [P, KB, NP])
        norm_row = sb("norm_row", [P, NP])
        degree = sb("degree", [P, NT])
        root = sb("root", [P, NT])
        norm = sb("norm", [P, NT])
        stats = sb("stats", [P, 2, KB, NG, 6])
        mean_var = sb("mean_var", [P, 2, KB, 2])
        var = sb("var", [P, 2, KB])
        std = sb("std", [P, 2, KB])
        rstd = sb("rstd", [P, 2, KB])
        a = sb("a", [P, 2, KB])
        ma = sb("ma", [P, 2, KB])
        b = sb("b", [P, 2, KB])
        bank = ps("bank", [P, 4, 512])
        row = ps("row", [P, 2, 512])

        loaded = sem("loaded")
        y_ready = sem("y_ready")
        norm_ready = sem("norm_ready")
        roots = sem("roots")
        degree_ready = sem("degree_ready")
        row_ready = sem("row_ready")
        row_kept = sem("row_kept")
        turn_ready = sem("turn_ready")
        turn_kept = sem("turn_kept")
        prod = [sem("prod1"), sem("prod2")]
        kept = [sem("kept1"), sem("kept2")]
        var_ready = sem("var_ready")
        coef_ready = sem("coef_ready")
        relu = [sem("relu1"), sem("relu2")]
        mixed = sem("mixed")
        mix_added = sem("mix_added")
        back = sem("back")
        back_added = sem("back_added")
        x_ready = sem("x_ready")

        with nc.Block() as block:
            @block.sync
            def _(sp):
                sp.dma_start(w_s[:, 0], w1_t).then_inc(loaded, 16)
                sp.dma_start(w_s[:, 1], w2_t).then_inc(loaded, 16)
                for n, (g_, b_) in enumerate(((gamma1, beta1), (gamma_h, beta_h))):
                    sp.dma_start(gain[:, n, :], g_).then_inc(loaded, 16)
                    sp.dma_start(shift[:, n, :], b_).then_inc(loaded, 16)
                sp.dma_start(bias[:, :], b_out).then_inc(loaded, 16)
                sp.dma_start(eps_s[:, :], eps_w.partition_broadcast(P)).then_inc(loaded, 16)

            @block.gpsimd
            def _(pool):
                for g in range(TG):
                    t = slice(g * TU, (g + 1) * TU)
                    pool.tensor_tensor(sh.x[:, t, :], sh.x[:, t, :], sh.xn[:, t, :], ALU.add).then_inc(x_ready, 1)

            @block.tensor
            def _(pe):
                for t in range(NT):
                    pe.wait_ge(y_ready, t // TU + 1)
                    if t >= 4:
                        pe.wait_ge(turn_kept, t - 3)
                    for k in range(KB):
                        last = pe.transpose(bank[:, t % 4, k * P:(k + 1) * P], sh.acc[:, t, k * P:(k + 1) * P],
                                            sh.ident[:, :])
                    last.then_inc(turn_ready, 1)
                pe.wait_ge(norm_ready, 1)
                for g, (c, w) in enumerate(COLS):
                    if g >= 2:
                        pe.wait_ge(row_kept, g - 1)
                    for t in range(c // P, -(-(c + w) // P)):
                        last = pe.matmul(row[:, g % 2, t * P - c:t * P - c + P],
                                         norm[:, t:t + 1].to_broadcast([P, P]), sh.ident[:, :], start=True, stop=True)
                    last.then_inc(row_ready, 1)
                pe.wait_ge(loaded, 128)
                for n, (of, done) in enumerate(((yt, turn_kept), (ht, relu[0]))):
                    for g, (c, w) in enumerate(COLS):
                        if n == 0:
                            pe.wait_ge(turn_kept, min(NT, (c + w + P - 1) // P))
                        else:
                            pe.wait_ge(relu[0], KB * (g + 1))
                        for m in range(KB):
                            q = KB * g + m
                            if n == 0 and q < 4:
                                pe.wait_ge(turn_kept, NT)
                            elif q >= 4:
                                pe.wait_ge(kept[n], q - 3)
                            for k in range(KB):
                                last = pe.matmul(bank[:, q % 4, 0:w], w_s[:, n, k, m * P:(m + 1) * P],
                                                 of[:, k, c:c + w], start=(k == 0), stop=(k == KB - 1))
                            last.then_inc(prod[n], 1)
                for g, (c, w) in enumerate(COLS):
                    for m in range(KB):
                        q = KB * g + m
                        if q < 4:
                            pe.wait_ge(kept[1], KB * NG)
                        else:
                            pe.wait_ge(mix_added, q - 3)
                        for k in range(KB):
                            last = pe.matmul(bank[:, q % 4, 0:w], sh.c0[:, k, m * P:(m + 1) * P],
                                             sh.xt[:, k, c:c + w], start=(k == 0), stop=(k == KB - 1))
                        last.then_inc(mixed, 1)
                for t in range(NT):
                    w = min(P, N - t * P)
                    pe.wait_ge(mix_added, KB * (t // 4 + 1))
                    if t >= 2:
                        pe.wait_ge(back_added, t - 1)
                    for k in range(KB):
                        last = pe.transpose(row[0:w, t % 2, k * P:(k + 1) * P], yt[:, k, t * P:t * P + w],
                                            sh.ident[:, :])
                    last.then_inc(back, 1)

            @block.scalar
            def _(act):
                act.wait_ge(degree_ready, 1)
                act.activation(root[:, :], degree[:, :], ACT.Sqrt).then_inc(roots, 1)
                for t in range(NT):
                    act.wait_ge(turn_ready, t + 1)
                    act.activation(yt[:, :, t * P:(t + 1) * P],
                                   bank[:, t % 4, 0:D].rearrange("p (k n) -> p k n", k=KB), ACT.Copy
                                   ).then_inc(turn_kept, 1)
                for g, (c, w) in enumerate(COLS):
                    w = min(512, NP - c)
                    act.wait_ge(row_ready, g + 1)
                    act.activation(norm_row[:, c:c + w], row[:, g % 2, 0:w], ACT.Copy).then_inc(row_kept, 1)
                for g, (c, w) in enumerate(COLS):
                    for m in range(KB):
                        act.wait_ge(prod[0], KB * g + m + 1)
                        act.activation(ht[:, m, c:c + w], bank[:, (KB * g + m) % 4, 0:w], ACT.Copy
                                       ).then_inc(kept[0], 1)
                for n, of in enumerate((ht, yt)):
                    act.wait_ge(var_ready, n + 1)
                    act.activation(std[:, n, :], var[:, n, :], ACT.Sqrt).then_inc(roots, 1)
                    act.wait_ge(coef_ready, n + 1)
                    act.wait_ge(kept[n], KB * NG)
                    for g, (c, w) in enumerate(COLS):
                        for m in range(KB):
                            act.activation(of[:, m, c:c + w], of[:, m, c:c + w], ACT.Relu, bias=b[:, n, m:m + 1],
                                           scale=a[:, n, m:m + 1]).then_inc(relu[n], 1)

            @block.vector
            def _(dve):
                dve.wait_ge(loaded, 128)
                dve.tensor_scalar(degree[:, :], sh.acc[:, :, D], 1.0, None, ALU.max).then_inc(degree_ready, 1)
                for g in range(TG):
                    t = slice(g * TU, (g + 1) * TU)
                    dve.scalar_tensor_tensor(out=sh.acc[:, t, 0:D], in0=sh.xn[:, t, :], scalar=eps_s[:, 0:1],
                                             in1=sh.acc[:, t, 0:D], op0=ALU.mult, op1=ALU.add).then_inc(y_ready, 1)
                dve.wait_ge(roots, 1)
                dve.reciprocal(norm[:, :], root[:, :]).then_inc(norm_ready, 1)

                def coefs(n):
                    dve.drain()
                    for m in range(KB):
                        dve.bn_aggr(mean_var[:, n, m, :], stats[:, n, m, :, :].rearrange("p g s -> p (g s)"))
                    dve.drain()
                    dve.tensor_scalar(var[:, n, :], mean_var[:, n, :, 1], EPS, None, ALU.add).then_inc(var_ready, 1)
                    dve.wait_ge(roots, n + 2)
                    dve.reciprocal(rstd[:, n, :], std[:, n, :])
                    dve.drain()
                    dve.tensor_tensor(a[:, n, :], gain[:, n, :], rstd[:, n, :], ALU.mult)
                    dve.drain()
                    dve.tensor_tensor(ma[:, n, :], mean_var[:, n, :, 0], a[:, n, :], ALU.mult)
                    dve.drain()
                    dve.tensor_tensor(b[:, n, :], shift[:, n, :], ma[:, n, :], ALU.subtract).then_inc(coef_ready, 1)

                for g, (c, w) in enumerate(COLS):
                    for m in range(KB):
                        dve.wait_ge(kept[0], KB * g + m + 1)
                        dve.bn_stats(stats[:, 0, m, g, :], ht[:, m, c:c + w])
                coefs(0)
                dve.wait_ge(row_kept, NG)
                for g, (c, w) in enumerate(COLS):
                    for m in range(KB):
                        q = KB * g + m
                        dve.wait_ge(prod[1], q + 1)
                        dve.tensor_tensor(yt[:, m, c:c + w], bank[:, q % 4, 0:w], norm_row[:, c:c + w], ALU.mult
                                          ).then_inc(kept[1], 1)
                        dve.wait_ge(kept[1], q + 1)
                        dve.bn_stats(stats[:, 1, m, g, :], yt[:, m, c:c + w])
                coefs(1)
                for g, (c, w) in enumerate(COLS):
                    for m in range(KB):
                        q = KB * g + m
                        dve.wait_ge(mixed, q + 1)
                        dve.wait_ge(relu[1], q + 1)
                        dve.scalar_tensor_tensor(out=yt[:, m, c:c + w], in0=bank[:, q % 4, 0:w],
                                                 scalar=bias[:, m:m + 1], in1=yt[:, m, c:c + w],
                                                 op0=ALU.add, op1=ALU.add).then_inc(mix_added, 1)
                for t in range(NT):
                    w = min(P, N - t * P)
                    dve.wait_ge(back, t + 1)
                    dve.wait_ge(x_ready, t // TU + 1)
                    dve.tensor_tensor(sh.x[0:w, t, :], sh.x[0:w, t, :], row[0:w, t % 2, 0:D], ALU.add
                                      ).then_inc(back_added, 1)


F1 = 512
FB = F1 // P
GT = 4
NGR = -(-NT // GT)


def stage_gate(nc, sh, wg, bg, bias, b2):
    X8 = 8
    with ExitStack() as ctx:
        def sb(n, shape, dt=F32):
            return ctx.enter_context(nc.sbuf_tensor(f"gate_{n}", shape, dt))

        def sem(n):
            return ctx.enter_context(semaphore(nc, sh, f"gate_{n}"))

        wg_s = sb("wg", [P, KB, X8])
        b_s = sb("b", [P, 2, X8])
        b2_s = sb("b2", [X8, D])
        logits = sb("logits", [P, NT, X8])
        best = sb("best", [P, NT, X8])
        place = sb("place", [P, NT, X8], U32)
        place_f = sb("place_f", [P, NT, 2])
        gap = sb("gap", [P, NT])
        second = sb("second", [P, NT])
        total = sb("total", [P, NT])
        lane8 = sb("lane8", [P, NT, X8])
        part = sb("part", [P, 2, NT, X8])
        gate_t = sb("gate_t", [X8, 2, P])
        raw = ctx.enter_context(nc.psum_tensor("gate_raw", [P, 512], F32))
        turned = ctx.enter_context(nc.psum_tensor("gate_turned", [P, 2, 512], F32))
        added = ctx.enter_context(nc.psum_tensor("gate_added", [P, 2, 512], F32))
        loaded = sem("loaded")
        raw_ready = sem("raw_ready")
        gap_ready = sem("gap_ready")
        second_ready = sem("second_ready")
        gate_ready = sem("gate_ready")
        turn_ready = sem("turn_ready")
        turn_kept = sem("turn_kept")
        bias_ready = sem("bias_ready")
        bias_added = sem("bias_added")

        with nc.Block() as block:
            @block.sync
            def _(sp):
                sp.dma_start(wg_s[:, :, :], wg).then_inc(loaded, 16)
                sp.dma_start(b_s[:, 0, :], bg.partition_broadcast(P)).then_inc(loaded, 16)
                sp.dma_start(b_s[:, 1, :], bias.partition_broadcast(P)).then_inc(loaded, 16)
                sp.dma_start(b2_s[:, :], b2).then_inc(loaded, 16)

            @block.tensor
            def _(pe):
                pe.wait_ge(loaded, 64)
                for t in range(NT):
                    for k in range(KB):
                        last = pe.matmul(raw[:, t * X8:(t + 1) * X8], sh.xt[:, k, t * P:(t + 1) * P], wg_s[:, k, :],
                                         start=(k == 0), stop=(k == KB - 1))
                last.then_inc(raw_ready, 1)
                pe.wait_ge(gate_ready, 1)

                def turn(t):
                    if t >= 2:
                        pe.wait_ge(turn_kept, t - 1)
                    pe.transpose(turned[0:X8, t % 2, 0:P], sh.gate[:, t, :], sh.ident[:, :]).then_inc(turn_ready, 1)

                turn(0)
                for t in range(NT):
                    if t + 1 < NT:
                        turn(t + 1)
                    pe.wait_ge(turn_kept, t + 1)
                    if t >= 2:
                        pe.wait_ge(bias_added, t - 1)
                    pe.matmul(added[:, t % 2, 0:D], gate_t[:, t % 2, :], b2_s[:, :], start=True, stop=True
                              ).then_inc(bias_ready, 1)

            @block.scalar
            def _(act):
                act.wait_ge(gap_ready, 1)
                act.activation(second[:, :], gap[:, :], ACT.Exp).then_inc(second_ready, 1)
                for t in range(NT):
                    act.wait_ge(turn_ready, t + 1)
                    if t >= 2:
                        act.wait_ge(bias_ready, t - 1)
                    act.activation(gate_t[:, t % 2, :], turned[0:X8, t % 2, 0:P], ACT.Copy).then_inc(turn_kept, 1)

            @block.vector
            def _(dve):
                dve.tensor_copy(lane8[:, :, :], sh.lane[:, 0:X8].unsqueeze(1).to_broadcast([P, NT, X8]))
                dve.wait_ge(loaded, 64)
                dve.wait_ge(raw_ready, 1)
                dve.tensor_tensor(best[:, :, :], raw[:, 0:NT * X8].rearrange("p (t e) -> p t e", e=X8),
                                  b_s[:, 0, :].unsqueeze(1).to_broadcast([P, NT, X8]), ALU.add)
                dve.drain()
                dve.tensor_tensor(logits[:, :, :], best[:, :, :],
                                  b_s[:, 1, :].unsqueeze(1).to_broadcast([P, NT, X8]), ALU.add)
                dve.drain()
                for t in range(NT):
                    dve.max(best[:, t, :], logits[:, t, :])
                dve.drain()
                for t in range(NT):
                    dve.max_index(place[:, t, :], best[:, t, :], logits[:, t, :])
                dve.tensor_tensor(gap[:, :], best[:, :, 1], best[:, :, 0], ALU.subtract).then_inc(gap_ready, 1)
                dve.drain()
                dve.tensor_copy(place_f[:, :, :], place[:, :, 0:2])
                dve.wait_ge(second_ready, 1)
                dve.tensor_scalar(total[:, :], second[:, :], 1.0, None, ALU.add)
                dve.drain()
                dve.reciprocal(sh.pair[:, :, 0], total[:, :])
                for j in range(2):
                    dve.tensor_tensor(sh.pick[:, j], lane8[:, :, :],
                                      place_f[:, :, j:j + 1].to_broadcast([P, NT, X8]), ALU.is_equal)
                dve.drain()
                dve.tensor_tensor(sh.pair[:, :, 1], second[:, :], sh.pair[:, :, 0], ALU.mult)
                dve.drain()
                for j in range(2):
                    dve.tensor_tensor(part[:, j], sh.pick[:, j],
                                      sh.pair[:, :, j:j + 1].to_broadcast([P, NT, X8]), ALU.mult)
                dve.drain()
                dve.tensor_tensor(sh.gate[:, :, :], part[:, 0], part[:, 1], ALU.add).then_inc(gate_ready, 1)
                for t in range(NT):
                    dve.wait_ge(bias_ready, t + 1)
                    dve.tensor_tensor(sh.x[:, t, :], sh.x[:, t, :], added[:, t % 2, 0:D], ALU.add
                                      ).then_inc(bias_added, 1)


GS = 256
EX = 8
NGS = (2 * NP + EX * (GS - 1)) // GS
assert NGS % 2 == 0


def stage_slots(nc, sh):
    with ExitStack() as ctx:
        def sb(n, shape, dt=F32):
            return ctx.enter_context(nc.sbuf_tensor(f"slot_{n}", shape, dt))

        def sem(n):
            return ctx.enter_context(semaphore(nc, sh, f"slot_{n}"))

        earlier = sb("earlier", [P, P])
        chosen = sb("chosen", [P, NT, EX])
        through = sb("through", [P, EX, NT])
        total = sb("total", [P, EX])
        before = sb("before", [P, EX])
        count = sb("count", [P, 2, EX], I32)
        groups = sb("groups", [P, EX])
        ends = sb("ends", [P, EX])
        base = sb("base", [P, EX])
        at = sb("at", [P, NT, EX])
        part = sb("part", [P, 2, NT, EX])
        slot_f = sb("slot_f", [P, 2, NT])
        passed = sb("passed", [1, NGS, EX])
        expert = sb("expert", [1, NGS])
        bank = ctx.enter_context(nc.psum_tensor("slot_bank", [P, 512], F32))
        made = sem("made")
        total_ready = sem("total_ready")
        summed = sem("summed")
        slots_ready = sem("slots_ready")
        scattered = ctx.enter_context(nc.semaphore("slot_scattered"))

        with nc.Block() as block:
            @block.gpsimd
            def _(pool):
                pool.affine_select(out=earlier[:, :], in_=sh.ones[:, :], compare_op=ALU.is_gt, fill=0.0,
                                   base=0, pattern=[[1, P]], channel_multiplier=-1).then_inc(made, 1)
                pool.wait_ge(sh.xs_zeroed, 16)
                pool.wait_ge(slots_ready, 1)
                for t in range(NT):
                    for j in range(2):
                        pool.indirect_dma_start(sh.xs_d, bass.IndirectOffsetOnAxis(ap=sh.slot[:, j, t:t + 1], axis=0),
                                                sh.xn[:, t, :], None).then_inc(scattered, 16)
                pool.wait_ge(scattered, 16 * 2 * NT)

            @block.tensor
            def _(pe):
                pe.wait_ge(made, 1)
                pe.wait_ge(total_ready, 1)
                pe.matmul(bank[:, 0:EX], earlier[:, :], total[:, :], start=True, stop=True)
                pe.matmul(bank[:, EX:2 * EX], sh.ones[:, :], total[:, :], start=True, stop=True).then_inc(summed, 1)

            @block.vector
            def _(dve):
                dve.tensor_tensor(chosen[:, :, :], sh.pick[:, 0], sh.pick[:, 1], ALU.add)
                dve.memset(part[:, :, :, :], 1.0)
                dve.drain()
                for e in range(EX):
                    dve.tensor_tensor_scan(through[:, e, :], part[:, 0, :, 0], chosen[:, :, e], 0.0, ALU.mult, ALU.add)
                dve.drain()
                dve.tensor_copy(total[:, :], through[:, :, NT - 1]).then_inc(total_ready, 1)
                dve.wait_ge(summed, 1)
                dve.tensor_copy(before[:, :], bank[:, 0:EX])
                dve.tensor_scalar(count[:, 0, :], bank[:, EX:2 * EX], float(GS - 1), None, ALU.add)
                dve.drain()
                dve.tensor_scalar(count[:, 1, :], count[:, 0, :], GS.bit_length() - 1, None, ALU.arith_shift_right)
                dve.drain()
                dve.tensor_copy(groups[:, :], count[:, 1, :])
                dve.drain()
                dve.tensor_tensor_scan(ends[:, :], part[:, 0, 0, :], groups[:, :], 0.0, ALU.mult, ALU.add)
                dve.drain()
                dve.tensor_tensor(base[:, :], ends[:, :], groups[:, :], ALU.subtract)
                dve.drain()
                dve.scalar_tensor_tensor(out=base[:, :], in0=base[:, :], scalar=float(GS), in1=before[:, :],
                                         op0=ALU.mult, op1=ALU.add)
                dve.drain()
                dve.scalar_tensor_tensor(out=at[:, :, :], in0=through[:, :, :].rearrange("p e t -> p t e"), scalar=-1.0,
                                         in1=base[:, :].unsqueeze(1).to_broadcast([P, NT, EX]),
                                         op0=ALU.add, op1=ALU.add)
                dve.drain()
                for j in range(2):
                    dve.tensor_tensor(part[:, j], sh.pick[:, j], at[:, :, :], ALU.mult)
                dve.drain()
                for j in range(2):
                    dve.tensor_reduce(slot_f[:, j, :], part[:, j], AX.X, ALU.add)
                dve.drain()
                dve.tensor_copy(sh.slot[:, :, :], slot_f[:, :, :]).then_inc(slots_ready, 1)
                dve.tensor_tensor(passed[:, :, :], sh.lane[0:1, 0:NGS].unsqueeze(2).to_broadcast([1, NGS, EX]),
                                  ends[0:1, :].unsqueeze(1).to_broadcast([1, NGS, EX]), ALU.is_ge)
                dve.drain()
                dve.tensor_reduce(expert[:, :], passed[:, :, :], AX.X, ALU.add)
                dve.drain()
                dve.tensor_scalar(sh.group_expert[:, :], expert[:, :], float(EX - 1), None, ALU.min)


def stage_experts(nc, sh, w1_of, w2_of, b1_of, function):
    A = GS // P
    with ExitStack() as ctx:
        def sb(n, shape, dt=F32):
            return ctx.enter_context(nc.sbuf_tensor(f"expert_{n}", shape, dt))

        def ps(n, shape, dt=F32):
            return ctx.enter_context(nc.psum_tensor(f"expert_{n}", shape, dt))

        def sem(n):
            return ctx.enter_context(semaphore(nc, sh, f"expert_{n}"))

        w1 = sb("w1", [P, 2, KB, F1])
        w2 = sb("w2", [P, 2, FB, D])
        b1 = sb("b1", [P, 2, FB])
        rows = sb("rows", [P, 2, A, D])
        cols = sb("cols", [P, 2, KB, GS])
        hidden = sb("hidden", [P, FB, GS])
        y = sb("y", [P, 2, A, D])
        turned = ps("turned", [P, 2, 512])
        up = ps("up", [P, 2, 512])
        down = ps("down", [P, 2, A, 512])
        weights_in = [sem(f"weights_in{q}") for q in range(2)]
        rows_in = [sem(f"rows_in{q}") for q in range(2)]
        turn_ready = sem("turn_ready")
        cols_ready = sem("cols_ready")
        up_ready = sem("up_ready")
        hidden_ready = sem("hidden_ready")
        down_ready = sem("down_ready")
        y_ready = sem("y_ready")
        y_free = sem("y_free")
        stored = [ctx.enter_context(nc.semaphore(f"expert_stored{q}")) for q in range(2)]

        with nc.Block() as block:
            @block.sync
            def _(sp):
                with sp.Fori(0, NGS // 2) as i:
                    for q in range(2):
                        sp.wait_ge(turn_ready, 2 * i + (q + 1))
                        sp.dma_start(rows[:, q, :, :], sh.xs_d[bass.ds((2 * i + q) * GS, GS), :]
                                     .rearrange("(a p) f -> p a f", p=P)).then_inc(rows_in[q], 16)
                        e = sp.value_load(sh.group_expert[0:1, bass.ds(2 * i + q, 1)], min_val=0, max_val=EX - 1)
                        sp.wait_ge(down_ready, 2 * i + (q + 1))
                        sp.dma_start(w1[:, q], w1_of(e)).then_inc(weights_in[q], 16)
                        sp.dma_start(w2[:, q], w2_of(e)).then_inc(weights_in[q], 16)
                        sp.dma_start(b1[:, q], b1_of(e)).then_inc(weights_in[q], 16)
                sp.wait_ge(turn_ready, NGS + 1)
                sp.dma_start(rows[:, 0, :, :], sh.xs_d[NGS * GS:(NGS + 1) * GS, :].rearrange("(a p) f -> p a f", p=P)
                             ).then_inc(rows_in[0], 16)

            @block.tensor
            def _(pe):
                def turn(q):
                    for k in range(KB):
                        for a in range(A):
                            last = pe.transpose(turned[:, q, (k * A + a) * P:(k * A + a + 1) * P],
                                                rows[:, q, a, k * P:(k + 1) * P], sh.ident[:, :])
                    last.then_inc(turn_ready, 1)

                pe.sem_inc(turn_ready, 2)
                pe.sem_inc(down_ready, 2)
                pe.wait_ge(rows_in[0], 16)
                turn(0)
                with pe.Fori(0, NGS // 2) as i:
                    for q in range(2):
                        pe.wait_ge(rows_in[1 - q], 16 * i + 16 * (q + 1))
                        pe.wait_ge(cols_ready, 2 * i + (q + 1))
                        turn(1 - q)
                        pe.wait_ge(cols_ready, 2 * i + (q + 2))
                        pe.wait_ge(weights_in[q], 48 * i + 48)
                        for m in range(FB):
                            for k in range(KB):
                                last = pe.matmul(up[:, m // 2, (m % 2) * GS:(m % 2 + 1) * GS],
                                                 w1[:, q, k, m * P:(m + 1) * P], cols[:, q, k, :],
                                                 start=(k == 0), stop=(k == KB - 1))
                            if m % 2 == 1:
                                last.then_inc(up_ready, 1)
                        pe.wait_ge(y_ready, 2 * i + (q + 1))
                        for m in range(FB):
                            if m % 2 == 0:
                                pe.wait_ge(hidden_ready, 4 * i + (2 * q + m // 2 + 1))
                            for a in range(A):
                                last = pe.matmul(down[:, q, a, 0:D], hidden[:, m, a * P:(a + 1) * P], w2[:, q, m, :],
                                                 start=(m == 0), stop=(m == FB - 1))
                        last.then_inc(down_ready, 1)

            @block.scalar
            def _(act):
                def keep(q):
                    act.activation(cols[:, q, :, :].rearrange("p k n -> p (k n)"), turned[:, q, :], ACT.Copy
                                   ).then_inc(cols_ready, 1)

                act.sem_inc(cols_ready, 1)
                act.wait_ge(turn_ready, 3)
                keep(0)
                with act.Fori(0, NGS // 2) as i:
                    for q in range(2):
                        act.wait_ge(turn_ready, 2 * i + (q + 4))
                        keep(1 - q)
                        for b in range(2):
                            act.wait_ge(up_ready, 4 * i + (2 * q + b + 1))
                            for m in (2 * b, 2 * b + 1):
                                last = act.activation(hidden[:, m, :], up[:, b, (m % 2) * GS:(m % 2 + 1) * GS], function,
                                                      bias=b1[:, q, m:m + 1])
                            last.then_inc(hidden_ready, 1)

            @block.vector
            def _(dve):
                dve.sem_inc(y_ready, 2)
                dve.sem_inc(y_free, 2)
                with dve.Fori(0, NGS // 2) as i:
                    for q in range(2):
                        dve.wait_ge(down_ready, 2 * i + (q + 3))
                        dve.wait_ge(y_free, 2 * i + (q + 1))
                        dve.tensor_copy(y[:, q, :, :], down[:, q, :, 0:D]).then_inc(y_ready, 1)

            @block.gpsimd
            def _(pool):
                with pool.Fori(0, NGS // 2) as i:
                    for q in range(2):
                        pool.wait_ge(y_ready, 2 * i + (q + 3))
                        pool.dma_start(sh.y_d[bass.ds((2 * i + q) * GS, GS), :].rearrange("(a p) f -> p a f", p=P),
                                       y[:, q, :, :]).then_inc(stored[q], 16)
                        hold(pool, stored[q], 16 * i + 16, y_free)


def stage_combine(nc, sh):
    B = 16
    with ExitStack() as ctx:
        rows = ctx.enter_context(nc.sbuf_tensor("combine_rows", [P, B, D], F32))
        gathered, past = sh.gathered, list(sh.past)
        used = ctx.enter_context(semaphore(nc, sh, "combine_used"))

        with nc.Block() as block:
            @block.gpsimd
            def _(pool):
                for n in range(2 * NT):
                    if n >= B:
                        pool.wait_ge(used, n - B + 1)
                    pool.indirect_dma_start(rows[:, n % B, :], None, sh.y_d,
                                            bass.IndirectOffsetOnAxis(ap=sh.slot[:, n % 2, n // 2:n // 2 + 1], axis=0)
                                            ).then_inc(gathered[n % B], 16)

            @block.vector
            def _(dve):
                for n in range(2 * NT):
                    t, j = n // 2, n % 2
                    dve.wait_ge(gathered[n % B], past[n % B] + 16 * (n // B + 1))
                    if j == 1:
                        dve.drain()
                    dve.scalar_tensor_tensor(out=sh.x[:, t, :], in0=rows[:, n % B, :], scalar=sh.pair[:, t, j:j + 1],
                                             in1=sh.x[:, t, :], op0=ALU.mult, op1=ALU.add).then_inc(used, 1)
        for n in range(2 * NT):
            sh.past[n % B] += 16


def stage_ffn(nc, sh, name, parts, w1_of, w2_of, b1_of, function, weight_of, into):
    with ExitStack() as ctx:
        def sb(n, shape, dt=F32):
            return ctx.enter_context(nc.sbuf_tensor(f"{name}_{n}", shape, dt))

        def sem(n):
            return ctx.enter_context(semaphore(nc, sh, f"{name}_{n}"))

        w1 = sb("w1", [P, 2, KB, F1])
        w2 = sb("w2", [P, 2, FB, D])
        b1 = sb("b1", [P, 2, FB])
        hidden = sb("hidden", [P, FB, GT * P])
        up = ctx.enter_context(nc.psum_tensor(f"{name}_up", [P, FB, 512], F32))
        down = ctx.enter_context(nc.psum_tensor(f"{name}_down", [P, GT, 512], F32))
        weights_in = [sem(f"weights_in{q}") for q in range(2)]
        pe_ticks = sem("pe_ticks")
        up_ready = sem("up_ready")
        hidden_ready = sem("hidden_ready")
        down_ready = sem("down_ready")
        summed = sem("summed")

        with nc.Block() as block:
            @block.sync
            def _(sp):
                with sp.Fori(0, parts // 2) as pair:
                    for q in range(2):
                        sp.wait_ge(down_ready, 2 * NGR * pair + NGR * (q + 1))
                        sp.dma_start(w1[:, q], w1_of(pair, q)).then_inc(weights_in[q], 16)
                        sp.dma_start(w2[:, q], w2_of(pair, q)).then_inc(weights_in[q], 16)
                        sp.dma_start(b1[:, q], b1_of(pair, q)).then_inc(weights_in[q], 16)

            def groups(eng, pair, q, body):
                before = 2 * NGR * pair + NGR * q
                with eng.Fori(0, NGR - 1) as g:
                    body(before + g, g, GT)
                body(before + (NGR - 1), NGR - 1, NT - GT * (NGR - 1))

            @block.tensor
            def _(pe):
                pe.sem_inc(down_ready, 2 * NGR)
                with pe.Fori(0, parts // 2) as pair:
                    for q in range(2):
                        hold(pe, weights_in[q], 48 * pair + 48, pe_ticks)

                        def body(n, g, tiles, q=q):
                            for m in range(FB):
                                for k in range(KB):
                                    last = pe.matmul(up[:, m, 0:tiles * P], w1[:, q, k, m * P:(m + 1) * P],
                                                     sh.xt[:, k, bass.ds(g * (GT * P), tiles * P)],
                                                     start=(k == 0), stop=(k == KB - 1))
                                last.then_inc(up_ready, 1)
                            pe.wait_ge(summed, n + 1)
                            for m in range(FB):
                                pe.wait_ge(hidden_ready, FB * n + (m + 1))
                                for j in range(tiles):
                                    last = pe.matmul(down[:, j, 0:D], hidden[:, m, j * P:(j + 1) * P], w2[:, q, m, :],
                                                     start=(m == 0), stop=(m == FB - 1))
                            last.then_inc(down_ready, 1)

                        groups(pe, pair, q, body)

            @block.scalar
            def _(act):
                with act.Fori(0, parts // 2) as pair:
                    for q in range(2):
                        def body(n, g, tiles, q=q):
                            for m in range(FB):
                                act.wait_ge(up_ready, FB * n + (m + 1))
                                act.activation(hidden[:, m, 0:tiles * P], up[:, m, 0:tiles * P], function,
                                               bias=b1[:, q, m:m + 1]).then_inc(hidden_ready, 1)

                        groups(act, pair, q, body)

            @block.vector
            def _(dve):
                dve.sem_inc(summed, 1)
                with dve.Fori(0, parts // 2) as pair:
                    for q in range(2):
                        def body(n, g, tiles, q=q):
                            dve.wait_ge(down_ready, n + (1 + 2 * NGR))
                            for j in range(tiles):
                                t = g * GT + j
                                last = dve.scalar_tensor_tensor(out=into[:, bass.ds(t, 1), :].rearrange("p a f -> p (a f)"),
                                                                in0=down[:, j, 0:D], scalar=weight_of(t, pair, q),
                                                                in1=into[:, bass.ds(t, 1), :].rearrange("p a f -> p (a f)"),
                                                                op0=ALU.mult, op1=ALU.add)
                            last.then_inc(summed, 1)

                        groups(dve, pair, q, body)


def stage_rows(nc, sh, name, gain, shift, more=(), into=None, out=None):
    with ExitStack() as ctx:
        def sem(n):
            return ctx.enter_context(semaphore(nc, sh, f"{name}_{n}"))

        vectors = [gain, shift, *more]
        rows = ctx.enter_context(nc.sbuf_tensor(f"{name}_rows", [P, 2 + len(more), D], F32))
        loaded = sem("loaded")
        scaled = sem("scaled")
        shift_ready = sem("shift_ready")
        shifted = sem("shifted")
        added = sem("added")
        stored = sem("stored")

        with nc.Block() as block:
            @block.sync
            def _(sp):
                for n, v in enumerate(vectors):
                    sp.dma_start(rows[:, n, :], v.partition_broadcast(P)).then_inc(loaded, 16)
                if out is not None:
                    for g in range(TG):
                        sp.wait_ge(added, g + 1)
                        a, z = g * TU * P, min(N, (g + 1) * TU * P)
                        full = (z - a) // P
                        sp.dma_start(out[a:a + full * P, :].rearrange("(t p) f -> p t f", p=P),
                                     into[:, g * TU:g * TU + full, :]).then_inc(stored, 16)
                        if z - a > full * P:
                            sp.dma_start(out[a + full * P:z, :], into[0:z - a - full * P, g * TU + full, :]
                                         ).then_inc(stored, 16)
                    sp.wait_ge(stored, 16 * (TG + 1))

            @block.vector
            def _(dve):
                dve.wait_ge(loaded, 16 * len(vectors))
                for n in range(len(more)):
                    dve.tensor_tensor(rows[:, 1, :], rows[:, 1, :], rows[:, 2 + n, :], ALU.add)
                    dve.drain()
                dve.sem_inc(shift_ready, 1)
                for g in range(TG):
                    t = slice(g * TU, (g + 1) * TU)
                    dve.tensor_tensor(sh.work[:, t, :], sh.work[:, t, :],
                                      rows[:, 0, :].unsqueeze(1).to_broadcast([P, TU, D]), ALU.mult).then_inc(scaled, 1)
                if into is not None:
                    for g in range(TG):
                        t = slice(g * TU, (g + 1) * TU)
                        dve.wait_ge(shifted, g + 1)
                        dve.tensor_tensor(into[:, t, :], into[:, t, :], sh.work[:, t, :], ALU.add).then_inc(added, 1)

            @block.gpsimd
            def _(pool):
                pool.wait_ge(shift_ready, 1)
                for g in range(TG):
                    t = slice(g * TU, (g + 1) * TU)
                    pool.wait_ge(scaled, g + 1)
                    pool.tensor_tensor(sh.work[:, t, :], sh.work[:, t, :],
                                       rows[:, 1, :].unsqueeze(1).to_broadcast([P, TU, D]), ALU.add).then_inc(shifted, 1)


def stage_mix1(nc, sh, wq, wk, wv, wo, bq, bk, bv, bo):
    NG = len(COLS)
    with ExitStack() as ctx:
        def sb(n, shape, dt=F32):
            return ctx.enter_context(nc.sbuf_tensor(f"mix1_{n}", shape, dt))

        def ps(n, shape, dt=F32):
            return ctx.enter_context(nc.psum_tensor(f"mix1_{n}", shape, dt))

        def sem(n):
            return ctx.enter_context(semaphore(nc, sh, f"mix1_{n}"))

        w_s = sb("w", [P, 4, KB, D])
        b_s = sb("b", [P, 3, KB])
        bo_s = sb("bo", [P, D])
        phi = [sh.work[:, :, :].rearrange("p t f -> p (t f)").rearrange("p (k n) -> p k n", k=KB),
               sh.acc[:, :, :].rearrange("p t w -> p (t w)")[:, 0:KB * NP].rearrange("p (k n) -> p k n", k=KB)]
        pos = sb("pos", [P, 2, 512])
        neg = sb("neg", [P, 2, 512])
        ksum = sb("ksum", [P, KB])
        kt = sb("kt", [P, 2, D])
        z = sb("z", [P, KB, D])
        zt = sb("zt", [P, KB, KB, P])
        own = sb("own", [P, P])
        kv = sb("kv", [P, KB, P])
        heads = sb("heads", [P, KB, P])
        den = sb("den", [P, KB, P])
        m = sb("m", [P, KB, D])
        rden = sb("rden", [P, 2, 512])
        bank = ps("bank", [P, 4, 512])
        zsum = ps("zsum", [P, KB, 512])
        small = ps("small", [P, 2, 512])

        loaded = sem("loaded")
        prod = sem("prod")
        pos_ready = sem("pos_ready")
        neg_ready = sem("neg_ready")
        exp_ready = sem("exp_ready")
        phi_ready = sem("phi_ready")
        turn_ready = sem("turn_ready")
        turn_kept = sem("turn_kept")
        zsummed = sem("zsummed")
        pe_small = sem("pe_small")
        dve_small = sem("dve_small")
        den_ready = sem("den_ready")
        divided = sem("divided")
        out_ready = sem("out_ready")
        out_added = sem("out_added")
        biased = sem("biased")

        with nc.Block() as block:
            @block.sync
            def _(sp):
                for n, w in enumerate((wk, wq, wv, wo)):
                    sp.dma_start(w_s[:, n], w).then_inc(loaded, 16)
                for n, b in enumerate((bk, bq, bv)):
                    sp.dma_start(b_s[:, n, :], b).then_inc(loaded, 16)
                sp.dma_start(bo_s[:, :], bo.partition_broadcast(P)).then_inc(loaded, 16)

            @block.gpsimd
            def _(pool):
                pool.wait_ge(loaded, 128)
                pool.wait_ge(zsummed, NT)
                pool.wait_ge(dve_small, 2)
                for g in range(TG):
                    t = slice(g * TU, (g + 1) * TU)
                    pool.tensor_tensor(sh.work[:, t, :], sh.xn[:, t, :],
                                       bo_s[:, :].unsqueeze(1).to_broadcast([P, TU, D]), ALU.add).then_inc(biased, 1)

            @block.tensor
            def _(pe):
                pe.wait_ge(loaded, 128)
                for n in range(2):
                    for g, (c, w) in enumerate(COLS):
                        for m_ in range(KB):
                            q = KB * (NG * n + g) + m_
                            if q >= 4:
                                pe.wait_ge(neg_ready, q - 3)
                            for k in range(KB):
                                last = pe.matmul(bank[:, q % 4, 0:w], w_s[:, n, k, m_ * P:(m_ + 1) * P],
                                                 sh.xt[:, k, c:c + w], start=(k == 0), stop=(k == KB - 1))
                            last.then_inc(prod, 1)

                def turn(t):
                    pe.wait_ge(phi_ready, min(KB * NG, KB * (t // 4 + 1)))
                    if t == NT - 1:
                        pe.wait_ge(dve_small, 1)
                    if t >= 2:
                        pe.wait_ge(turn_kept, t - 1)
                    for k in range(KB):
                        last = pe.transpose(small[:, t % 2, k * P:(k + 1) * P], phi[0][:, k, t * P:(t + 1) * P],
                                            sh.ident[:, :])
                    last.then_inc(turn_ready, 1)

                turn(0)
                for t in range(NT):
                    if t + 1 < NT:
                        turn(t + 1)
                    pe.wait_ge(turn_kept, t + 1)
                    for m_ in range(KB):
                        last = pe.matmul(zsum[:, m_, 0:D], kt[:, t % 2, m_ * P:(m_ + 1) * P], sh.xn[:, t, :],
                                         start=(t == 0), stop=(t == NT - 1))
                    last.then_inc(zsummed, 1)
                pe.wait_ge(dve_small, 2)
                for m_ in range(KB):
                    for k in range(KB):
                        last = pe.transpose(small[:, 0, (2 * m_ + k) * P:(2 * m_ + k + 1) * P],
                                            z[:, m_, k * P:(k + 1) * P], sh.ident[:, :])
                last.then_inc(pe_small, 1)
                for m_ in range(KB):
                    last = pe.matmul(small[:, 1, (2 + m_) * P:(3 + m_) * P], ksum[:, m_:m_ + 1].to_broadcast([P, P]),
                                     sh.ident[:, :], start=True, stop=True)
                pe.wait_ge(dve_small, 3)
                for m_ in range(KB):
                    for k in range(KB):
                        last = pe.matmul(small[:, 1, m_ * P:(m_ + 1) * P], w_s[:, 2, k, m_ * P:(m_ + 1) * P],
                                         zt[:, m_, k, :], start=(k == 0), stop=(k == KB - 1))
                last.then_inc(pe_small, 1)
                pe.wait_ge(dve_small, 4)
                for m_ in range(KB):
                    last = pe.matmul(small[:, 0, m_ * D:(m_ + 1) * D], heads[:, m_, :], w_s[:, 3, m_, :],
                                     start=True, stop=True)
                last.then_inc(pe_small, 1)
                for g, (c, w) in enumerate(COLS):
                    for m_ in range(KB):
                        q = KB * g + m_
                        pe.wait_ge(phi_ready, KB * NG + q + 1)
                        if q >= 4:
                            pe.wait_ge(den_ready, q - 3)
                        pe.matmul(bank[:, q % 4, 0:w], den[:, m_, :], phi[1][:, m_, c:c + w],
                                  start=True, stop=True).then_inc(pe_small, 1)
                pe.wait_ge(dve_small, 5)
                for t in range(NT):
                    w = min(P, N - t * P)
                    pe.wait_ge(divided, KB * (t // 4 + 1))
                    if t >= 2:
                        pe.wait_ge(out_added, t - 1)
                    for m_ in range(KB):
                        last = pe.matmul(zsum[0:w, t % 2, 0:D], phi[1][:, m_, t * P:t * P + w], m[:, m_, :],
                                         start=(m_ == 0), stop=(m_ == KB - 1))
                    last.then_inc(out_ready, 1)

            @block.scalar
            def _(act):
                act.wait_ge(loaded, 128)
                for q in range(2 * NG * KB):
                    n, g, m_ = q // (NG * KB), q // KB % NG, q % KB
                    w = COLS[g][1]
                    act.wait_ge(prod, q + 1)
                    if q >= 2:
                        act.wait_ge(phi_ready, q - 1)
                    act.activation(pos[:, q % 2, 0:w], bank[:, q % 4, 0:w], ACT.Relu, bias=b_s[:, n, m_:m_ + 1]
                                   ).then_inc(pos_ready, 1)
                    if q >= 1:
                        w = COLS[(q - 1) // KB % NG][1]
                        act.wait_ge(neg_ready, q)
                        act.activation(neg[:, (q - 1) % 2, 0:w], neg[:, (q - 1) % 2, 0:w], ACT.Exp).then_inc(exp_ready, 1)
                act.wait_ge(neg_ready, 2 * NG * KB)
                w = COLS[-1][1]
                act.activation(neg[:, 1, 0:w], neg[:, 1, 0:w], ACT.Exp).then_inc(exp_ready, 1)
                for t in range(NT):
                    act.wait_ge(turn_ready, t + 1)
                    if t >= 2:
                        act.wait_ge(zsummed, t - 1)
                    act.activation(kt[:, t % 2, :], small[:, t % 2, 0:D], ACT.Copy).then_inc(turn_kept, 1)

            @block.vector
            def _(dve):
                dve.memset(phi[0][:, :, N:NP], 0.0).then_inc(dve_small, 1)
                dve.memset(own[:, :], 0.0)
                dve.drain()
                for h in range(P // DH):
                    r = slice(h * DH, (h + 1) * DH)
                    dve.memset(own[r, r], 1.0)
                dve.wait_ge(loaded, 128)

                def finish(q):
                    n, g, m_ = q // (NG * KB), q // KB % NG, q % KB
                    c, w = COLS[g]
                    dve.wait_ge(exp_ready, q + 1)
                    dve.tensor_tensor(phi[n][:, m_, c:c + w], pos[:, q % 2, 0:w], neg[:, q % 2, 0:w], ALU.add
                                      ).then_inc(phi_ready, 1)

                for q in range(2 * NG * KB):
                    n, g, m_ = q // (NG * KB), q // KB % NG, q % KB
                    w = COLS[g][1]
                    dve.wait_ge(pos_ready, q + 1)
                    if q >= 2:
                        dve.wait_ge(phi_ready, q - 1)
                    dve.tensor_scalar(neg[:, q % 2, 0:w], bank[:, q % 4, 0:w], b_s[:, n, m_:m_ + 1], 0.0,
                                      ALU.add, ALU.min).then_inc(neg_ready, 1)
                    if q >= 1:
                        finish(q - 1)
                finish(2 * NG * KB - 1)
                dve.wait_ge(phi_ready, KB * NG)
                dve.tensor_reduce(ksum[:, :], phi[0][:, :, 0:N], AX.X, ALU.add)
                dve.wait_ge(zsummed, NT)
                for m_ in range(KB):
                    last = dve.tensor_copy(z[:, m_, :], zsum[:, m_, 0:D])
                dve.drain().then_inc(dve_small, 1)
                for m_ in range(KB):
                    dve.tensor_scalar(den[:, m_, :], own[:, :], ksum[:, m_:m_ + 1], None, ALU.mult)
                dve.wait_ge(pe_small, 1)
                dve.tensor_copy(zt[:, :, :, :].rearrange("p m k n -> p (m k n)"), small[:, 0, :])
                dve.drain().then_inc(dve_small, 1)
                dve.wait_ge(pe_small, 2)
                for m_ in range(KB):
                    dve.tensor_scalar(kv[:, m_, :], small[:, 1, (2 + m_) * P:(3 + m_) * P], b_s[:, 2, m_:m_ + 1],
                                      None, ALU.mult)
                dve.drain()
                for m_ in range(KB):
                    dve.tensor_tensor(kv[:, m_, :], kv[:, m_, :], small[:, 1, m_ * P:(m_ + 1) * P], ALU.add)
                dve.drain()
                for m_ in range(KB):
                    last = dve.tensor_tensor(heads[:, m_, :], kv[:, m_, :], own[:, :], ALU.mult)
                last.then_inc(dve_small, 1)
                dve.wait_ge(pe_small, 3)
                dve.tensor_copy(m[:, :, :].rearrange("p m f -> p (m f)"), small[:, 0, :]).then_inc(dve_small, 1)
                for g, (c, w) in enumerate(COLS):
                    for m_ in range(KB):
                        q = KB * g + m_
                        dve.wait_ge(pe_small, 4 + q)
                        dve.tensor_scalar(rden[:, q % 2, 0:w], bank[:, q % 4, 0:w], 1e-6, None, ALU.add
                                          ).then_inc(den_ready, 1)
                        dve.drain()
                        dve.reciprocal(rden[:, q % 2, 0:w], rden[:, q % 2, 0:w])
                        dve.drain()
                        dve.tensor_tensor(phi[1][:, m_, c:c + w], phi[1][:, m_, c:c + w], rden[:, q % 2, 0:w],
                                          ALU.mult).then_inc(divided, 1)
                for t in range(NT):
                    w = min(P, N - t * P)
                    dve.wait_ge(out_ready, t + 1)
                    dve.wait_ge(biased, t // TU + 1)
                    dve.tensor_tensor(sh.work[0:w, t, :], sh.work[0:w, t, :], zsum[0:w, t % 2, 0:D], ALU.add
                                      ).then_inc(out_added, 1)


def stage_project(nc, sh, w, bq, bk, bv):
    with ExitStack() as ctx:
        def sem(n):
            return ctx.enter_context(semaphore(nc, sh, f"proj_{n}"))

        w_s = ctx.enter_context(nc.sbuf_tensor("proj_w", [P, KB, 3 * D], F32))
        b_s = ctx.enter_context(nc.sbuf_tensor("proj_b", [P, 3 * D], F32))
        kv = ctx.enter_context(nc.sbuf_tensor("proj_kv", [P, 4, 2 * D], F32))
        out = ctx.enter_context(nc.psum_tensor("proj_out", [P, 2, 2, 512], F32))
        loaded = sem("loaded")
        prod = sem("prod")
        kept = sem("kept")
        stored = [sem(f"stored{q}") for q in range(4)]

        with nc.Block() as block:
            @block.sync
            def _(sp):
                sp.dma_start(w_s[:, :, :], w).then_inc(loaded, 16)
                for n, v in enumerate((bq, bk, bv)):
                    sp.dma_start(b_s[:, n * D:(n + 1) * D], v.partition_broadcast(P)).then_inc(loaded, 16)
                for t in range(NT):
                    sp.wait_ge(kept, t + 1)
                    for n, table in enumerate((sh.k_d, sh.v_d)):
                        sp.dma_start(table[t * P:(t + 1) * P, :], kv[:, t % 4, n * D:(n + 1) * D]
                                     ).then_inc(stored[t % 4], 16)
                for q in range(4):
                    sp.wait_ge(stored[q], 32 * len(range(q, NT, 4)))

            @block.tensor
            def _(pe):
                pe.wait_ge(loaded, 64)
                for t in range(NT):
                    if t >= 2:
                        pe.wait_ge(kept, t - 1)
                    for a, z in ((0, 2 * D), (2 * D, 3 * D)):
                        for k in range(KB):
                            last = pe.matmul(out[:, t % 2, a // (2 * D), 0:z - a], sh.xt[:, k, t * P:(t + 1) * P],
                                             w_s[:, k, a:z], start=(k == 0), stop=(k == KB - 1))
                    last.then_inc(prod, 1)

            @block.vector
            def _(dve):
                dve.wait_ge(loaded, 64)
                for t in range(NT):
                    dve.wait_ge(prod, t + 1)
                    if t >= 4:
                        dve.wait_ge(stored[t % 4], 32 * (t // 4))
                    dve.tensor_tensor(sh.q[:, t, :], out[:, t % 2, 0, 0:D], b_s[:, 0:D], ALU.add)
                    dve.tensor_tensor(kv[:, t % 4, 0:D], out[:, t % 2, 0, D:2 * D], b_s[:, D:2 * D], ALU.add)
                    dve.tensor_tensor(kv[:, t % 4, D:2 * D], out[:, t % 2, 1, 0:D], b_s[:, 2 * D:3 * D], ALU.add
                                      ).then_inc(kept, 1)


def stage_scores(nc, sh, ef_t, we, be):
    UI = 4
    NB = UI * SUBS
    with ExitStack() as ctx:
        def sb(n, shape, dt=F32):
            return ctx.enter_context(nc.sbuf_tensor(f"score_{n}", shape, dt))

        def ps(n, shape, dt=F32):
            return ctx.enter_context(nc.psum_tensor(f"score_{n}", shape, dt))

        def sem(n):
            return ctx.enter_context(semaphore(nc, sh, f"score_{n}"))

        index = sb("index", [P, NB], I32)
        rows = sb("rows", [P, NB, D])
        goal = sb("goal", [1, UI, EC], BF16)
        off = sb("off", [P, 2, EC])
        member = sb("member", [P, 2, EC])
        feats = sb("feats", [ED + 1, UI, EC])
        we_s = sb("we", [ED + 1, DH])
        summed = sb("summed", [P, 2, SUBS * D])
        dots = sb("dots", [P, 2, SUBS * H])
        wide = ps("wide", [P, 2, 512])
        edge = ps("edge", [P, 2, 512])
        query = ps("query", [P, 2, SUBS * D])

        loaded = sem("loaded")
        index_ready = sem("index_ready")
        gathered, past = sh.gathered, list(sh.past)
        goal_in = [sem(f"goal_in{u}") for u in range(UI)]
        feats_in = [sem(f"feats_in{u}") for u in range(UI)]
        wide_ready = sem("wide_ready")
        off_ready = sem("off_ready")
        member_ready = sem("member_ready")
        edge_ready = sem("edge_ready")
        query_ready = sem("query_ready")
        rows_used = sem("rows_used")
        query_used = sem("query_used")
        pool_ticks = sem("pool_ticks")

        with nc.Block() as block:
            @block.gpsimd
            def _(pool):
                with pool.Fori(0, NI // UI) as i:
                    for u in range(UI):
                        hold(pool, index_ready, UI * i + (u + 1), pool_ticks)
                        for k in range(SUBS):
                            q = u * SUBS + k
                            pool.indirect_dma_start(rows[:, q, :], None, sh.k_d,
                                                    bass.IndirectOffsetOnAxis(ap=index[:, q:q + 1], axis=0)
                                                    ).then_inc(gathered[q], 16)

            @block.sync
            def _(sp):
                sp.dma_start(we_s[0:ED, :], we).then_inc(loaded, 16)
                sp.dma_start(we_s[ED:ED + 1, :], be).then_inc(loaded, 16)
                unsorted = sp.value_load(sh.unsorted[0:1, 0:1], min_val=0, max_val=P)
                with sp.Fori(0, NI // UI) as i:
                    for u in range(UI):
                        c = sp.value_load(sh.chunk_id[0:1, bass.ds(UI * i + u, 1)], min_val=0, max_val=NCH - 1)
                        sp.wait_ge(edge_ready, UI * i + (u + 1))
                        sp.dma_start(goal[:, u, :], sh.goal_d[bass.ds(UI * i + u, 1), :]).then_inc(goal_in[u], 16)
                        with sp.If(unsorted == 0):
                            sp.dma_start(feats[0:ED, u, :], ef_t[:, bass.ds(c * EC, EC)]).then_inc(feats_in[u], 16)
                        with sp.If(unsorted != 0):
                            sp.dma_start(feats[0:ED, u, :], sh.ef_p[:, bass.ds(c * EC, EC)]).then_inc(feats_in[u], 16)

            @block.tensor
            def _(pe):
                pe.wait_ge(loaded, 33)
                pe.sem_inc(edge_ready, UI)
                pe.sem_inc(query_ready, 2)
                with pe.Fori(0, NI // UI) as i:
                    for pair in range(0, UI, 2):
                        for u in (pair, pair + 1):
                            pe.wait_ge(goal_in[u], 16 * i + 16)
                            pe.wait_ge(off_ready, UI * i + (u + 1))
                            pe.matmul(wide[:, u % 2, :], sh.ones_b[0:1, :], goal[:, u, :], start=True, stop=True
                                      ).then_inc(wide_ready, 1)
                        for u in (pair, pair + 1):
                            pe.wait_ge(feats_in[u], 16 * i + 16)
                            pe.wait_ge(rows_used, UI * i + (u + 1 + UI - 2))
                            for k in range(SUBS):
                                last = pe.matmul(edge[:, u % 2, k * DH:(k + 1) * DH], feats[:, u, k * P:(k + 1) * P],
                                                 we_s[:, :], start=True, stop=True)
                            last.then_inc(edge_ready, 1)
                        for u in (pair, pair + 1):
                            t = pe.value_load(sh.tile_id[0:1, bass.ds(UI * i + u, 1)], min_val=0, max_val=NT - 1)
                            pe.wait_ge(member_ready, UI * i + (u + 1))
                            pe.wait_ge(query_used, UI * i + (u + 1))
                            for k in range(SUBS):
                                last = pe.matmul(query[:, u % 2, k * D:(k + 1) * D], member[:, u % 2, k * P:(k + 1) * P],
                                                 sh.q[:, bass.ds(t, 1), :], start=True, stop=True)
                            last.then_inc(query_ready, 1)

            @block.scalar
            def _(act):
                act.sem_inc(off_ready, 2)
                with act.Fori(0, NI // UI) as i:
                    for pair in range(0, UI, 2):
                        for u in (pair, pair + 1):
                            act.wait_ge(wide_ready, UI * i + (u + 1))
                            act.activation(off[:, u % 2, :], wide[:, u % 2, :], ACT.Abs, bias=sh.minus_row[:, 0:1]
                                           ).then_inc(off_ready, 1)
                        for u in (pair, pair + 1):
                            act.wait_ge(off_ready, UI * i + (u + 3))
                            act.wait_ge(query_ready, UI * i + (u + 1))
                            act.activation(member[:, u % 2, :], off[:, u % 2, :], ACT.Relu, bias=sh.ones[:, 0:1],
                                           scale=-1.0).then_inc(member_ready, 1)

            @block.vector
            def _(dve):
                dve.memset(feats[ED:ED + 1, :, :], 1.0).then_inc(loaded, 1)
                dve.tensor_copy(index[:, :], sh.src_of[:, 0:NB])
                dve.drain()
                dve.sem_inc(index_ready, UI)
                dve.sem_inc(rows_used, UI)
                dve.sem_inc(query_used, 2)
                with dve.Fori(0, NI // UI) as i:
                    for pair in range(0, UI, 2):
                        for u in (pair, pair + 1):
                            for k in range(SUBS):
                                dve.wait_ge(gathered[u * SUBS + k], 16 * i + (past[u * SUBS + k] + 16))
                            dve.wait_ge(edge_ready, UI * i + (u + 1 + UI))
                            dve.tensor_tensor(
                                summed[:, u % 2, :].rearrange("p (k h d) -> p k h d", k=SUBS, h=H),
                                rows[:, u * SUBS:(u + 1) * SUBS, :].rearrange("p k (h d) -> p k h d", h=H),
                                edge[:, u % 2, 0:SUBS * DH].rearrange("p (k d) -> p k d", k=SUBS).unsqueeze(2)
                                .to_broadcast([P, SUBS, H, DH]), ALU.add).then_inc(rows_used, 1)
                            dve.tensor_copy(index[:, u * SUBS:(u + 1) * SUBS],
                                            sh.src_of[:, bass.ds((UI * i + (u + UI)) * SUBS, SUBS)]).then_inc(index_ready, 1)
                        dve.drain()
                        for u in (pair, pair + 1):
                            dve.wait_ge(query_ready, UI * i + (u + 3))
                            dve.tensor_tensor(summed[:, u % 2, :], summed[:, u % 2, :], query[:, u % 2, :], ALU.mult
                                              ).then_inc(query_used, 1)
                        dve.drain()
                        for u in (pair, pair + 1):
                            dve.tensor_reduce(dots[:, u % 2, :], summed[:, u % 2, :].rearrange("p (g d) -> p g d", d=DH),
                                              AX.X, ALU.add)
                        dve.drain()
                        u = pair
                        dve.scalar_tensor_tensor(
                            out=sh.scores[:, bass.ds((UI * i + u) * SUBS * H, 2 * SUBS * H)]
                            .rearrange("p (k h) -> p k h", h=H),
                            in0=dots[:, :, :].rearrange("p n (k h) -> p (n k) h", h=H), scalar=float(DH) ** -0.5,
                            in1=sh.weight_of[:, bass.ds((UI * i + u) * SUBS, 2 * SUBS)].unsqueeze(2)
                            .to_broadcast([P, 2 * SUBS, H]), op0=ALU.mult, op1=ALU.mult)
                    dve.drain()
        for q in range(NB):
            sh.past[q] += 16 * (NI // UI)


def stage_softmax(nc, sh):
    SP_ = 8
    PP = NS // SP_
    SL = SP_ * P
    NBL = NS // 16
    BIG = 1.0e30
    assert NS % 16 == 0 and PP <= P
    with ExitStack() as ctx:
        def sb(n, shape, dt=F32):
            return ctx.enter_context(nc.sbuf_tensor(f"max_{n}", shape, dt))

        def ps(n, shape, dt=F32):
            return ctx.enter_context(nc.psum_tensor(f"max_{n}", shape, dt))

        def sem(n):
            return ctx.enter_context(semaphore(nc, sh, f"max_{n}"))

        st = sb("st", [P, NBL, P])
        line = sb("line", [P, H, SL])
        free = sh.acc[:, :, :].rearrange("p t w -> p (t w)")
        key = free[:, 0:SL]
        new = free[:, SL:2 * SL]
        last_ = free[:, 2 * SL:3 * SL]
        edge_key = free[:, 3 * SL:4 * SL]
        side = sb("side", [P, H + 2])
        side_t = sb("side_t", [H + 2, P])
        keys = sb("keys", [1, 2, P])
        same = sb("same", [1, 3, P])
        wide = free[0:H, 4 * SL:4 * SL + 3 * P].rearrange("h (n p) -> h n p", n=3)
        carry = sb("carry", [H, 2, P])
        carried = sb("carried", [P, H])
        turned = ps("turned", [P, 4, 512])
        small = ps("small", [P, 2, 512])

        turn_ready = sem("turn_ready")
        turn_kept = sem("turn_kept")
        lines_out = sem("lines_out")
        lines_in = sem("lines_in")
        key_in = sem("key_in")
        pe_small = sem("pe_small")
        dve_small = sem("dve_small")
        keys_moved = sem("keys_moved")
        maxima = sem("maxima")
        maxima_out = sem("maxima_out")
        maxima_in = sem("maxima_in")
        back_ready = sem("back_ready")
        back_used = sem("back_used")
        keys_kept = sem("keys_kept")

        score_lines = sh.scores_d.rearrange("h (b s) e -> s h b e", s=16)

        def blocks(q):
            return range(4 * q, min(4 * q + 4, NBL))

        NQ = -(-NBL // 4)

        with nc.Block() as block:
            @block.tensor
            def _(pe):
                for q in range(NQ):
                    if q >= 4:
                        pe.wait_ge(turn_kept, q - 3)
                    for b in blocks(q):
                        last = pe.transpose(turned[:, q % 4, (b % 4) * P:(b % 4 + 1) * P],
                                            sh.scores[:, b * P:(b + 1) * P], sh.ident[:, :])
                    last.then_inc(turn_ready, 1)
                for r in range(2):
                    pe.wait_ge(dve_small, 3 * r + 1)
                    pe.transpose(small[0:H + 2, 0, 0:PP], side[0:PP, :], sh.ident[0:PP, 0:PP]).then_inc(pe_small, 1)
                    pe.wait_ge(dve_small, 3 * r + 2)
                    pe.matmul(small[0:H, 1, 0:3 * P], sh.ones[0:1, 0:H], same[:, :, :].rearrange("a n p -> a (n p)"),
                              start=True, stop=True).then_inc(pe_small, 1)
                    pe.wait_ge(dve_small, 3 * r + 3)
                    pe.transpose(small[0:P, 0, 0:H], carry[:, 1, :], sh.ident[0:H, 0:H]).then_inc(pe_small, 1)
                pe.wait_ge(maxima_in, 256)
                for q in range(NQ):
                    if q >= 4:
                        pe.wait_ge(back_used, q - 3)
                    for b in blocks(q):
                        last = pe.transpose(turned[:, q % 4, (b % 4) * P:(b % 4 + 1) * P], st[:, b, :], sh.ident[:, :])
                    last.then_inc(back_ready, 1)

            @block.sync
            def _(sp):
                sp.dma_start(key[0:PP, :], sh.key_d.rearrange("i e -> (i e)").rearrange("(p s) -> p s", s=SL)
                             ).then_inc(key_in, 16)
                sp.wait_ge(turn_kept, NQ)
                for s in range(16):
                    sp.dma_start(score_lines[s], st[s * H:(s + 1) * H, :, :]).then_inc(lines_out, 16)
                sp.wait_ge(lines_out, 256)
                sp.dma_start(line[0:PP, :, :], sh.scores_d.rearrange("h j e -> h (j e)")
                             .rearrange("h (p s) -> p h s", s=SL)).then_inc(lines_in, 16)
                for r in range(2):
                    sp.wait_ge(dve_small, 3 * r + 1)
                    sp.wait_ge(keys_kept, r + 1)
                    for n in range(2):
                        sp.dma_start(keys[:, n, 0:PP], side_t[H + n:H + n + 1, 0:PP]).then_inc(keys_moved, 16)
                sp.wait_ge(maxima, 1)
                sp.dma_start(sh.scores_d.rearrange("h j e -> h (j e)").rearrange("h (p s) -> p h s", s=SL),
                             line[0:PP, :, :]).then_inc(maxima_out, 16)
                sp.wait_ge(maxima_out, 16)
                for s in range(16):
                    sp.dma_start(st[s * H:(s + 1) * H, :, :], score_lines[s]).then_inc(maxima_in, 16)

            @block.scalar
            def _(act):
                for q in range(NQ):
                    n = len(blocks(q))
                    act.wait_ge(turn_ready, q + 1)
                    act.activation(st[:, 4 * q:4 * q + n, :].rearrange("p b e -> p (b e)"), turned[:, q % 4, 0:n * P],
                                   ACT.Copy).then_inc(turn_kept, 1)

            @block.vector
            def _(dve):
                dve.memset(keys[:, :, :], -2.0)
                dve.memset(side_t[:, :], 0.0)
                dve.memset(same[:, :, :], 0.0)
                dve.memset(carry[:, :, :], 0.0)
                dve.wait_ge(key_in, 16)
                dve.memset(new[:, 0:1], 0.0)
                dve.memset(last_[:, SL - 1:SL], 0.0)
                dve.tensor_tensor(new[0:PP, 1:SL], key[0:PP, 1:SL], key[0:PP, 0:SL - 1], ALU.not_equal)
                dve.drain()
                dve.tensor_scalar(new[0:PP, 1:SL], new[0:PP, 1:SL], -BIG, None, ALU.mult)
                dve.drain()
                dve.tensor_copy(last_[0:PP, 0:SL - 1], new[0:PP, 1:SL])
                dve.wait_ge(lines_in, 16)
                for r in range(2):
                    near, far = (0, SL - 1) if r == 0 else (SL - 1, 0)
                    step = new if r == 0 else last_
                    for h in range(H):
                        if r == 0:
                            dve.tensor_tensor_scan(line[0:PP, h, :], step[0:PP, :], line[0:PP, h, :], -BIG,
                                                   ALU.add, ALU.max)
                        else:
                            dve.tensor_tensor_scan(line[0:PP, h, ::-1], step[0:PP, ::-1], line[0:PP, h, ::-1], -BIG,
                                                   ALU.add, ALU.max)
                    dve.tensor_scalar(edge_key[0:PP, :], key[0:PP, :], key[0:PP, near:near + 1], -BIG,
                                      ALU.not_equal, ALU.mult)
                    dve.drain()
                    dve.tensor_copy(side[0:PP, 0:H], line[0:PP, :, far])
                    dve.tensor_copy(side[0:PP, H:H + 1], key[0:PP, near:near + 1])
                    dve.tensor_copy(side[0:PP, H + 1:H + 2], key[0:PP, far:far + 1])
                    dve.drain().then_inc(dve_small, 1)
                    dve.wait_ge(pe_small, 3 * r + 1)
                    dve.tensor_copy(side_t[:, 0:PP], small[0:H + 2, 0, 0:PP]).then_inc(keys_kept, 1)
                    dve.wait_ge(keys_moved, 32 * (r + 1))
                    if r == 0:
                        dve.tensor_tensor(same[:, 0, 1:PP], keys[:, 0, 1:PP], keys[:, 1, 0:PP - 1], ALU.not_equal)
                    else:
                        dve.memset(same[:, 0, PP - 1:PP], 0.0)
                        dve.tensor_tensor(same[:, 0, 0:PP - 1], keys[:, 0, 0:PP - 1], keys[:, 1, 1:PP], ALU.not_equal)
                    end = 0 if r == 0 else PP - 1
                    dve.drain()
                    dve.memset(same[:, 0, end:end + 1], 1.0)
                    dve.tensor_tensor(same[:, 1, 0:PP], keys[:, 0, 0:PP], keys[:, 1, 0:PP], ALU.not_equal)
                    dve.drain()
                    dve.tensor_tensor(same[:, 1, 0:PP], same[:, 1, 0:PP], same[:, 0, 0:PP], ALU.max)
                    dve.drain()
                    dve.tensor_scalar(same[:, 0:2, 0:PP], same[:, 0:2, 0:PP], -BIG, None, ALU.mult)
                    dve.drain().then_inc(dve_small, 1)
                    dve.wait_ge(pe_small, 3 * r + 2)
                    dve.tensor_copy(wide[:, :, :].rearrange("h n p -> h (n p)"), small[0:H, 1, 0:3 * P])
                    dve.drain()
                    if r == 0:
                        dve.tensor_tensor_scan(carry[:, 0, 0:PP], wide[:, 1, 0:PP], side_t[0:H, 0:PP], -BIG,
                                               ALU.add, ALU.max)
                        dve.drain()
                        dve.tensor_tensor(carry[:, 1, 1:PP], carry[:, 0, 0:PP - 1], wide[:, 0, 1:PP], ALU.add)
                    else:
                        dve.tensor_tensor_scan(carry[:, 0, PP - 1::-1], wide[:, 1, PP - 1::-1], side_t[0:H, PP - 1::-1],
                                               -BIG, ALU.add, ALU.max)
                        dve.drain()
                        dve.tensor_tensor(carry[:, 1, 0:PP - 1], carry[:, 0, 1:PP], wide[:, 0, 0:PP - 1], ALU.add)
                    dve.memset(carry[:, 1, end:end + 1], -BIG)
                    dve.drain().then_inc(dve_small, 1)
                    dve.wait_ge(pe_small, 3 * r + 3)
                    dve.tensor_copy(carried[:, :], small[:, 0, 0:H])
                    dve.drain()
                    dve.tensor_scalar(carried[:, :], carried[:, :], -BIG, None, ALU.max)
                    dve.drain()
                    for h in range(H):
                        dve.scalar_tensor_tensor(out=line[0:PP, h, :], in0=edge_key[0:PP, :],
                                                 scalar=carried[0:PP, h:h + 1], in1=line[0:PP, h, :],
                                                 op0=ALU.add, op1=ALU.max)
                    dve.drain()
                dve.sem_inc(maxima, 1)
                for q in range(NQ):
                    a, z = 4 * q * P, 4 * q * P + len(blocks(q)) * P
                    dve.wait_ge(back_ready, q + 1)
                    dve.tensor_tensor(sh.scores[:, a:z], sh.scores[:, a:z], turned[:, q % 4, 0:z - a], ALU.subtract
                                      ).then_inc(back_used, 1)


def stage_attend(nc, sh, w1, w2, b1):
    UI = 4
    NB = UI * SUBS
    W = D + H
    with ExitStack() as ctx:
        def sb(n, shape, dt=F32):
            return ctx.enter_context(nc.sbuf_tensor(f"att_{n}", shape, dt))

        def sem(n):
            return ctx.enter_context(semaphore(nc, sh, f"att_{n}"))

        index = sb("index", [P, NB], I32)
        rows = sb("rows", [P, NB, W])
        member = sb("member", [P, NB, P])
        w1_s = sb("w1", [P, KB, F1])
        w2_s = sb("w2", [P, FB, D])
        b1_s = sb("b1", [P, 2 * FB])
        hidden = sb("hidden", [P, FB, P])
        sums = ctx.enter_context(nc.psum_tensor("att_sums", [P, UI, 512], F32))
        up = ctx.enter_context(nc.psum_tensor("att_up", [P, 512], F32))
        down = ctx.enter_context(nc.psum_tensor("att_down", [P, 512], F32))
        weights_in = sem("weights_in")
        up_ready = sem("up_ready")
        hidden_ready = sem("hidden_ready")
        down_ready = sem("down_ready")
        down_added = sem("down_added")
        index_ready = sem("index_ready")
        gathered, past = sh.gathered, list(sh.past)
        exp_ready = sem("exp_ready")
        ready = sem("ready")
        summed = sem("summed")
        added = sem("added")
        pool_ticks = sem("pool_ticks")
        act_ticks = sem("act_ticks")

        STEPS = 2 * NT
        assert NI // UI > STEPS

        def loops(eng, body):
            for half in range(2):
                with eng.Fori(0, NT) as t:
                    body(t + half * NT, half, t)
            with eng.Fori(STEPS, NI // UI) as i:
                body(i, None, None)

        with nc.Block() as block:
            @block.sync
            def _(sp):
                for half in range(2):
                    if half == 1:
                        sp.wait_ge(down_ready, NT)
                    sp.dma_start(w1_s[:, :, :], w1[:, :, half * F1:(half + 1) * F1]).then_inc(weights_in, 16)
                    sp.dma_start(w2_s[:, :, :], w2[:, half * FB:(half + 1) * FB, :]).then_inc(weights_in, 16)
                    sp.dma_start(b1_s[:, half * FB:(half + 1) * FB], b1[half]).then_inc(weights_in, 16)

            @block.gpsimd
            def _(pool):
                with pool.Fori(0, NI // UI) as i:
                    for u in range(UI):
                        hold(pool, index_ready, UI * i + (u + 1), pool_ticks)
                        for k in range(SUBS):
                            q = u * SUBS + k
                            pool.indirect_dma_start(rows[:, q, 0:D], None, sh.v_d,
                                                    bass.IndirectOffsetOnAxis(ap=index[:, q:q + 1], axis=0)
                                                    ).then_inc(gathered[q], 16)

            @block.scalar
            def _(act):
                def body(i, half, t):
                    for u in range(UI):
                        hold(act, summed, UI * i + (u + 1), act_ticks)
                        act.activation(rows[:, u * SUBS:(u + 1) * SUBS, D:W],
                                       sh.scores[:, bass.ds((UI * i + u) * SUBS * H, SUBS * H)]
                                       .rearrange("p (k h) -> p k h", h=H), ACT.Exp).then_inc(exp_ready, 1)
                        if u == 1 and half is not None:
                            act.wait_ge(up_ready, i + 1)
                            for m in range(FB):
                                last = act.activation(hidden[:, m, :], up[:, m * P:(m + 1) * P], ACT.Relu,
                                                      bias=b1_s[:, half * FB + m:half * FB + m + 1])
                            last.then_inc(hidden_ready, 1)

                loops(act, body)

            @block.vector
            def _(dve):
                dve.memset(sh.acc[:, :, :], 0.0)
                dve.tensor_copy(index[:, :], sh.src_of[:, 0:NB])
                dve.drain()
                dve.sem_inc(index_ready, UI)
                dve.sem_inc(added, UI)
                dve.sem_inc(down_added, 1)

                def body(i, half, t):
                    tile = [dve.value_load(sh.tile_id[0:1, bass.ds(UI * i + u, 1)], min_val=0, max_val=NT - 1)
                            for u in range(UI)]

                    def add(u):
                        dve.wait_ge(summed, UI * i + (u + 1 + UI))
                        a = sh.acc[:, bass.ds(tile[u], 1), :].rearrange("p a w -> p (a w)")
                        dve.tensor_tensor(a, a, sums[:, u, 0:W], ALU.add).then_inc(added, 1)
                        dve.tensor_copy(index[:, u * SUBS:(u + 1) * SUBS],
                                        sh.src_of[:, bass.ds((UI * i + (u + UI)) * SUBS, SUBS)]).then_inc(index_ready, 1)

                    for u in range(UI):
                        dve.wait_ge(summed, UI * i + (u + 1))
                        for k in range(SUBS):
                            dve.tensor_scalar(member[:, u * SUBS + k, :], sh.lane[:, :],
                                              sh.lane_of[:, bass.ds((UI * i + u) * SUBS + k, 1)], None,
                                              ALU.is_equal)
                        for k in range(SUBS):
                            dve.wait_ge(gathered[u * SUBS + k], 16 * i + (past[u * SUBS + k] + 16))
                        dve.wait_ge(exp_ready, UI * i + (u + 1))
                        r = rows[:, u * SUBS:(u + 1) * SUBS, 0:D].rearrange("p k (h d) -> p k h d", h=H)
                        e = rows[:, u * SUBS:(u + 1) * SUBS, D:W]
                        dve.tensor_tensor(r, r, e.unsqueeze(3).to_broadcast([P, SUBS, H, DH]), ALU.mult)
                        dve.drain().then_inc(ready, 1)
                        if u >= 2:
                            add(u - 2)
                    dve.drain()
                    add(UI - 2)
                    if half is not None:
                        dve.wait_ge(down_ready, i + 1)
                        w = sh.work[:, bass.ds(t, 1), :].rearrange("p a f -> p (a f)")
                        dve.tensor_tensor(w, w, down[:, 0:D], ALU.add).then_inc(down_added, 1)
                    dve.drain()
                    add(UI - 1)
                    dve.drain()

                loops(dve, body)

            @block.tensor
            def _(pe):
                pe.sem_inc(summed, UI)

                def body(i, half, t):
                    if half is not None:
                        pe.wait_ge(weights_in, 48 * (half + 1))
                        for m in range(FB):
                            for k in range(KB):
                                last = pe.matmul(up[:, m * P:(m + 1) * P],
                                                 w1_s[:, k, m * P:(m + 1) * P],
                                                 sh.xt[:, k, bass.ds(t * P, P)], start=(k == 0), stop=(k == KB - 1))
                        last.then_inc(up_ready, 1)
                    for u in range(UI):
                        pe.wait_ge(added, UI * i + (u + 1))
                        pe.wait_ge(ready, UI * i + (u + 1))
                        for k in range(SUBS):
                            last = pe.matmul(sums[:, u, 0:W], member[:, u * SUBS + k, :], rows[:, u * SUBS + k, :],
                                             start=(k == 0), stop=(k == SUBS - 1))
                        last.then_inc(summed, 1)
                        if u == 1 and half is not None:
                            pe.wait_ge(hidden_ready, i + 1)
                            pe.wait_ge(down_added, i + 1)
                            for m in range(FB):
                                last = pe.matmul(down[:, 0:D], hidden[:, m, :], w2_s[:, m, :],
                                                 start=(m == 0), stop=(m == FB - 1))
                            last.then_inc(down_ready, 1)

                loops(pe, body)

        for q in range(NB):
            sh.past[q] += 16 * (NI // UI)


def stage_attention_out(nc, sh, wo, bo, alpha, beta, b2):
    with ExitStack() as ctx:
        def sb(n, shape, dt=F32):
            return ctx.enter_context(nc.sbuf_tensor(f"ao_{n}", shape, dt))

        def sem(n):
            return ctx.enter_context(semaphore(nc, sh, f"ao_{n}"))

        wo_s = sb("wo", [P, KB, D])
        bo_s = sb("bo", [P, D])
        b2_s = sb("b2", [P, D])
        ab = sb("ab", [P, 1])
        total = sb("total", [P, NT, H])
        at = sb("at", [P, 2, KB, P])
        out = sb("out", [P, 2, D])
        turned = ctx.enter_context(nc.psum_tensor("ao_turned", [P, 2, 512], F32))
        prod = ctx.enter_context(nc.psum_tensor("ao_prod", [P, 2, 512], F32))
        loaded = sem("loaded")
        divided = sem("divided")
        turn_ready = sem("turn_ready")
        turn_kept = sem("turn_kept")
        prod_ready = sem("prod_ready")
        prod_used = sem("prod_used")
        xn_ready = sem("xn_ready")
        b2_ready = sem("b2_ready")
        pooled = sem("pooled")

        with nc.Block() as block:
            @block.sync
            def _(sp):
                sp.dma_start(wo_s[:, :, :], wo).then_inc(loaded, 16)
                sp.dma_start(bo_s[:, :], bo.partition_broadcast(P)).then_inc(loaded, 16)
                sp.dma_start(b2_s[:, :], b2.partition_broadcast(P)).then_inc(loaded, 16)
                sp.dma_start(ab[:, :], alpha.partition_broadcast(P)).then_inc(loaded, 16)
                sp.dma_start(sh.beta[:, :], beta.partition_broadcast(P)).then_inc(loaded, 16)

            @block.tensor
            def _(pe):
                pe.wait_ge(loaded, 80)

                def turn(t):
                    pe.wait_ge(divided, t // TU + 1)
                    if t >= 2:
                        pe.wait_ge(turn_kept, t - 1)
                    for k in range(KB):
                        last = pe.transpose(turned[:, t % 2, k * P:(k + 1) * P], sh.acc[:, t, k * P:(k + 1) * P],
                                            sh.ident[:, :])
                    last.then_inc(turn_ready, 1)

                turn(0)
                for t in range(NT):
                    if t + 1 < NT:
                        turn(t + 1)
                    pe.wait_ge(turn_kept, t + 1)
                    if t >= 2:
                        pe.wait_ge(prod_used, t - 1)
                    for k in range(KB):
                        last = pe.matmul(prod[:, t % 2, 0:D], at[:, t % 2, k, :], wo_s[:, k, :],
                                         start=(k == 0), stop=(k == KB - 1))
                    last.then_inc(prod_ready, 1)

            @block.scalar
            def _(act):
                for t in range(NT):
                    act.wait_ge(turn_ready, t + 1)
                    if t >= 2:
                        act.wait_ge(prod_ready, t - 1)
                    act.activation(at[:, t % 2, :, :].rearrange("p k n -> p (k n)"), turned[:, t % 2, 0:D], ACT.Copy
                                   ).then_inc(turn_kept, 1)

            @block.gpsimd
            def _(pool):
                pool.wait_ge(b2_ready, 1)
                for g in range(TG):
                    t = slice(g * TU, (g + 1) * TU)
                    pool.wait_ge(xn_ready, TU * (g + 1))
                    pool.tensor_tensor(sh.x[:, t, :], sh.x[:, t, :], sh.xn[:, t, :], ALU.add).then_inc(pooled, 1)
                    pool.wait_ge(pooled, 2 * g + 1)
                    pool.tensor_tensor(sh.x[:, t, :], sh.x[:, t, :],
                                       b2_s[:, :].unsqueeze(1).to_broadcast([P, TU, D]), ALU.add).then_inc(pooled, 1)

            @block.vector
            def _(dve):
                dve.wait_ge(loaded, 80)
                dve.tensor_scalar(b2_s[:, :], b2_s[:, :], sh.beta[:, 0:1], None, ALU.mult).then_inc(b2_ready, 1)
                dve.tensor_scalar(total[:, :, :], sh.acc[:, :, D:D + H], 0.5, None, ALU.max)
                dve.drain()
                dve.reciprocal(total[:, :, :], total[:, :, :])
                dve.drain()
                for g in range(TG):
                    for t in range(g * TU, (g + 1) * TU):
                        a = sh.acc[:, t, 0:D].rearrange("p (h d) -> p h d", h=H)
                        last = dve.tensor_tensor(a, a, total[:, t, :].unsqueeze(2).to_broadcast([P, H, DH]), ALU.mult)
                    last.then_inc(divided, 1)
                for t in range(NT):
                    dve.wait_ge(prod_ready, t + 1)
                    dve.tensor_tensor(out[:, t % 2, :], prod[:, t % 2, 0:D], bo_s[:, :], ALU.add).then_inc(prod_used, 1)
                    dve.drain()
                    dve.scalar_tensor_tensor(out=sh.xn[:, t, :], in0=out[:, t % 2, :], scalar=ab[:, 0:1],
                                             in1=sh.xn[:, t, :], op0=ALU.mult, op1=ALU.add).then_inc(xn_ready, 1)


def stage_route(nc, sh, wr, br, b2):
    X8 = 8
    CAPACITY = float(-(-N * 5 // (4 * X8)))
    with ExitStack() as ctx:
        def sb(n, shape, dt=F32):
            return ctx.enter_context(nc.sbuf_tensor(f"route_{n}", shape, dt))

        def sem(n):
            return ctx.enter_context(semaphore(nc, sh, f"route_{n}"))

        wr_s = sb("wr", [P, KB, X8])
        br_s = sb("br", [P, X8])
        b2_s = sb("b2", [X8, D])
        mean = sb("mean", [P, KB])
        v = sb("v", [P, 8, X8])
        top = sb("top", [P, 2, X8])
        place = sb("place", [P, X8], U32)
        place_f = sb("place_f", [P, 2])
        one = sb("one", [P, 6])
        dense = sb("dense", [P, X8])
        column = sb("column", [X8, 1])
        row = sb("row", [P, D])
        bank = ctx.enter_context(nc.psum_tensor("route_bank", [P, 2, 512], F32))
        loaded = sem("loaded")
        mean_ready = sem("mean_ready")
        prod = sem("prod")
        act_in = sem("act_in")
        act_out = sem("act_out")
        column_ready = sem("column_ready")
        row_ready = sem("row_ready")
        done = sem("done")

        with nc.Block() as block:
            @block.sync
            def _(sp):
                sp.dma_start(wr_s[:, :, :], wr).then_inc(loaded, 16)
                sp.dma_start(br_s[:, :], br.partition_broadcast(P)).then_inc(loaded, 16)
                sp.dma_start(b2_s[:, :], b2).then_inc(loaded, 16)

            @block.tensor
            def _(pe):
                pe.wait_ge(loaded, 48)
                pe.wait_ge(mean_ready, 1)
                for k in range(KB):
                    last = pe.matmul(bank[:, 0, 0:X8], mean[:, k:k + 1].to_broadcast([P, P]), wr_s[:, k, :],
                                     start=(k == 0), stop=(k == KB - 1))
                last.then_inc(prod, 1)
                pe.wait_ge(column_ready, 1)
                pe.matmul(bank[:, 1, 0:D], column[:, 0:1].to_broadcast([X8, P]), b2_s[:, :], start=True, stop=True
                          ).then_inc(prod, 1)

            @block.scalar
            def _(act):
                for n, (a, b) in enumerate(((1, 1), (3, 4))):
                    act.wait_ge(act_in, n + 1)
                    act.activation(v[:, b, :], v[:, a, :], ACT.Exp).then_inc(act_out, 1)
                act.wait_ge(act_in, 3)
                act.activation(one[:, 4:5], one[:, 4:5], ACT.Exp).then_inc(act_out, 1)

            @block.gpsimd
            def _(pool):
                pool.wait_ge(row_ready, 1)
                for g in range(3):
                    t = slice(g * TU, (g + 1) * TU)
                    pool.tensor_tensor(sh.xn[:, t, :], sh.xn[:, t, :], row[:, :].unsqueeze(1).to_broadcast([P, TU, D]),
                                       ALU.add).then_inc(done, 1)

            @block.vector
            def _(dve):
                dve.tensor_reduce(mean[:, :], sh.xt[:, :, 0:N], AX.X, ALU.add)
                dve.drain()
                dve.tensor_scalar(mean[:, :], mean[:, :], 1.0 / N, None, ALU.mult).then_inc(mean_ready, 1)
                dve.wait_ge(prod, 1)
                dve.tensor_tensor(v[:, 0, :], bank[:, 0, 0:X8], br_s[:, :], ALU.add)
                dve.drain()

                def softmax(a, n, out):
                    dve.tensor_reduce(one[:, 0:1], v[:, a, :], AX.X, ALU.max)
                    dve.drain()
                    dve.tensor_scalar(v[:, a + 1, :], v[:, a, :], one[:, 0:1], None, ALU.subtract).then_inc(act_in, 1)
                    dve.wait_ge(act_out, n + 1)
                    dve.tensor_reduce(one[:, 1:2], v[:, out, :], AX.X, ALU.add)
                    dve.drain()
                    dve.reciprocal(one[:, 2:3], one[:, 1:2])
                    dve.drain()
                    dve.tensor_scalar(v[:, out, :], v[:, out, :], one[:, 2:3], None, ALU.mult)
                    dve.drain()

                softmax(0, 0, 1)
                dve.tensor_scalar(v[:, 5, :], v[:, 1, :], float(N), 1e-30, ALU.mult, ALU.max)
                dve.drain()
                dve.reciprocal(v[:, 6, :], v[:, 5, :])
                dve.drain()
                dve.tensor_scalar(v[:, 7, :], v[:, 6, :], CAPACITY, 1.0, ALU.mult, ALU.min)
                dve.drain()
                dve.tensor_tensor(v[:, 2, :], v[:, 1, :], v[:, 7, :], ALU.mult)
                dve.drain()
                softmax(2, 1, 4)
                dve.max(top[:, 0, :], v[:, 4, :])
                dve.drain()
                dve.max_index(place[:, :], top[:, 0, :], v[:, 4, :])
                dve.tensor_tensor(one[:, 4:5], top[:, 0, 1:2], top[:, 0, 0:1], ALU.subtract).then_inc(act_in, 1)
                dve.drain()
                dve.tensor_copy(sh.expert[:, :], place[:, 0:2])
                dve.tensor_copy(place_f[:, :], place[:, 0:2])
                dve.wait_ge(act_out, 3)
                dve.tensor_scalar(one[:, 5:6], one[:, 4:5], 1.0, None, ALU.add)
                dve.drain()
                dve.reciprocal(sh.share[:, 0:1], one[:, 5:6])
                dve.drain()
                dve.tensor_tensor(sh.share[:, 1:2], sh.share[:, 0:1], one[:, 4:5], ALU.mult)
                dve.drain()
                for j in range(2):
                    dve.tensor_scalar(v[:, 5 + j, :], sh.lane[:, 0:X8], place_f[:, j:j + 1], sh.share[:, j:j + 1],
                                      ALU.is_equal, ALU.mult)
                dve.drain()
                dve.tensor_tensor(dense[:, :], v[:, 5, :], v[:, 6, :], ALU.add)
                dve.drain()
                dve.tensor_tensor(v[0:X8, 7, :], dense[0:X8, :], sh.ident[0:X8, 0:X8], ALU.mult)
                dve.drain()
                dve.tensor_reduce(column[:, :], v[0:X8, 7, :], AX.X, ALU.add).then_inc(column_ready, 1)
                dve.wait_ge(prod, 2)
                dve.tensor_copy(row[:, :], bank[:, 1, 0:D]).then_inc(row_ready, 1)
                dve.drain()
                for g in range(3, TG):
                    t = slice(g * TU, (g + 1) * TU)
                    dve.tensor_tensor(sh.xn[:, t, :], sh.xn[:, t, :], row[:, :].unsqueeze(1).to_broadcast([P, TU, D]),
                                      ALU.add)


def build(nc, a, out):
    with ExitStack() as ctx:
        def sb(name, shape, dt=F32):
            return ctx.enter_context(nc.sbuf_tensor(name, shape, dt))

        def dram(name, shape, dt=F32):
            return nc.dram_tensor(name, shape, dt, kind="Internal").ap()

        def blocks(w):
            return w.rearrange("(k p) f -> p k f", p=P)

        sh = Shared()
        sh.first_semaphore, sh.semaphores = 130, 0
        sh.dst_p = dram("dst_p", (EP,), I32)
        sh.src_p = dram("src_p", (EP,), I32)
        sh.ew_p = dram("ew_p", (EP,))
        sh.order_d = dram("order_d", (EP,), I32)
        sh.ef_p = dram("ef_p", (ED, EP))
        sh.tile_d = dram("tile_d", (NI,), I32)
        sh.chunk_d = dram("chunk_d", (NI,), I32)
        sh.key_d = dram("key_d", (NI, EC))
        sh.goal_d = dram("goal_d", (NI, EC), BF16)
        sh.xn_d = dram("xn_d", (NP, D))
        sh.xs_d = dram("xs_d", ((NGS + 1) * GS, D))
        sh.y_d = dram("y_d", (NGS * GS, D))
        sh.k_d = dram("k_d", (NP, D))
        sh.v_d = dram("v_d", (NP, D))
        sh.scores_d = dram("scores_d", (H, NS, P))

        sh.ident = sb("ident", [P, P])
        sh.lane = sb("lane", [P, P])
        sh.unsorted = sb("unsorted", [1, 1], I32)
        sh.ones = sb("ones", [P, P])
        sh.zeros = sb("zeros", [P, D])
        sh.ones_b = sb("ones_b", [1, P], BF16)
        sh.minus_row = sb("minus_row", [P, 1])
        sh.tile_id = sb("tile_id", [1, NI], I32)
        sh.chunk_id = sb("chunk_id", [1, NI], I32)
        sh.src_of = sb("src_of", [P, NS + 4 * SUBS], I32)
        sh.lane_of = sb("lane_of", [P, NS])
        sh.weight_of = sb("weight_of", [P, NS])
        sh.x = sb("x", [P, NT, D])
        sh.xn = sb("xn", [P, NT, D])
        sh.xt = sb("xt", [P, KB, NP])
        sh.acc = sb("acc", [P, NT, D + H])
        sh.work = sh.acc[:, :, 0:D]
        sh.beta = sb("beta", [P, 1])
        sh.expert = sb("expert", [P, 2], I32)
        sh.share = sb("share", [P, 2])
        sh.gathered = [ctx.enter_context(nc.semaphore(f"gathered{q}")) for q in range(4 * SUBS)]
        sh.past = [0] * (4 * SUBS)
        sh.xs_zeroed = ctx.enter_context(nc.semaphore("xs_zeroed"))

        stage_copy_edges(nc, sh, a["dst"], a["src"], a["edge_weight"])
        stage_sort(nc, sh, a["edge_attr_64"])
        stage_edge_tables(nc, sh)

        stage_norm(nc, sh, "n0", load=a["x"], table=sh.xn_d, source=sh.x, to=sh.xn)
        stage_aggregate(nc, sh)
        with nc.sbuf_tensor("c0", [P, KB, D], F32) as sh.c0:
            stage_mix0(nc, sh, blocks(a["L0_mix_Wk"]), blocks(a["L0_mix_Wv"]), a["L0_mix_Wq_t"], a["L0_mix_W_out"])
            stage_gnn0(nc, sh, blocks(a["L0_gnn_w1_t"]), blocks(a["L0_gnn_w2_t"]), a["L0_gnn_gamma1_f"],
                       a["L0_gnn_beta1_f"], a["L0_gnn_gamma_h_f"], a["L0_gnn_beta_h_f"], a["L0_gnn_eps_weight"],
                       a["L0_mix_b_out_f"])
        clear_semaphores(nc, sh)
        stage_norm(nc, sh, "n1", source=sh.x, to=sh.xn)
        with ExitStack() as moe:
            sh.gate = moe.enter_context(nc.sbuf_tensor("gate", [P, NT, EX], F32))
            sh.pick = moe.enter_context(nc.sbuf_tensor("pick", [P, 2, NT, EX], F32))
            sh.pair = moe.enter_context(nc.sbuf_tensor("pair", [P, NT, 2], F32))
            sh.slot = moe.enter_context(nc.sbuf_tensor("slot", [P, 2, NT], I32))
            sh.group_expert = moe.enter_context(nc.sbuf_tensor("group_expert", [1, NGS], I32))
            stage_gate(nc, sh, blocks(a["L0_ffn_Wg"]), a["L0_ffn_bg"], a["L0_ffn_bias"], a["L0_ffn_b2"])
            stage_slots(nc, sh)
            stage_experts(nc, sh, lambda e: a["L0_ffn_W1"][bass.ds(e, 1)].rearrange("e (k p) f -> p (e k) f", p=P),
                          lambda e: a["L0_ffn_W2"][bass.ds(e, 1)].rearrange("e (k p) f -> p (e k) f", p=P),
                          lambda e: a["L0_ffn_b1_f"][bass.ds(e, 1)].rearrange("e p k -> p (e k)"), ACT.Relu)
            stage_combine(nc, sh)

        def halves(pre):
            w1 = blocks(a[pre + "W1"])
            w2 = a[pre + "W2"].rearrange("(e k p) f -> p e k f", p=P, e=2)
            return (lambda pair, q: w1[:, :, q * F1:(q + 1) * F1], lambda pair, q: w2[:, q],
                    lambda pair, q: a[pre + "b1_f"][q])

        stage_norm(nc, sh, "n2", source=sh.x, to=sh.xn, turn=False)
        clear_semaphores(nc, sh)
        stage_norm(nc, sh, "n5", source=sh.xn, to=sh.work, gain=a["L1_gnn_ln1_g_f"], shift=a["L1_gnn_ln1_b_f"])
        with nc.sbuf_tensor("scores", [P, NS * H], F32) as sh.scores:
            sh.q = sh.work
            stage_project(nc, sh, blocks(a["L1_gnn_Wqkv"]), a["L1_gnn_bq"], a["L1_gnn_bk"], a["L1_gnn_bv"])
            stage_scores(nc, sh, a["ef_t"], a["L1_gnn_We"], a["L1_gnn_be"])
            stage_softmax(nc, sh)
            with nc.sbuf_tensor("mixed", [P, NT, D], F32) as sh.work:
                stage_norm(nc, sh, "n2t", to=sh.xn)
                stage_mix1(nc, sh, *[blocks(a["L1_mix_" + w]) for w in ("Wq", "Wk", "Wv", "Wo")],
                           *[a["L1_mix_" + b] for b in ("bq_f", "bk_f", "bv_f", "bo")])
                clear_semaphores(nc, sh)
                stage_norm(nc, sh, "n3", source=sh.work, to=sh.work, gain=a["L1_mix_ln1_g_f"],
                           shift=a["L1_mix_ln1_b_f"])
                stage_rows(nc, sh, "r3", a["L1_mix_ln1_g"], a["L1_mix_ln1_b"], [a["L1_mix_b2"]])
                stage_attend(nc, sh, blocks(a["L1_mix_W1"]), blocks(a["L1_mix_W2"]), a["L1_mix_b1_f"])
                stage_norm(nc, sh, "n4", source=sh.work, to=sh.work, turn=False)
                stage_rows(nc, sh, "r4", a["L1_mix_ln2_g"], a["L1_mix_ln2_b"], into=sh.x)
        clear_semaphores(nc, sh)
        sh.work = sh.acc[:, :, 0:D]
        stage_attention_out(nc, sh, blocks(a["L1_gnn_Wo"]), a["L1_gnn_bo"], a["L1_gnn_alpha"], a["L1_gnn_beta"],
                            a["L1_gnn_b2"])
        stage_norm(nc, sh, "n6", source=sh.xn, to=sh.work, gain=a["L1_gnn_ln2_g_f"], shift=a["L1_gnn_ln2_b_f"])
        stage_ffn(nc, sh, "ffg", 2, *halves("L1_gnn_"), ACT.Gelu, lambda t, pair, q: sh.beta[:, 0:1], sh.x)

        stage_norm(nc, sh, "n7", source=sh.x, to=sh.xn)
        stage_route(nc, sh, blocks(a["L1_ffn_Wr"]), a["L1_ffn_br"], a["L1_ffn_b2"])

        def expert1(array, pattern):
            def part(pair, q):
                e = nc.sync.value_load(sh.expert[0:1, q:q + 1], min_val=0, max_val=7)
                return a[array][bass.ds(e, 1)].rearrange(pattern, p=P)
            return part

        stage_ffn(nc, sh, "ffx", 2, expert1("L1_ffn_W1", "e (k p) f -> p (e k) f"),
                  expert1("L1_ffn_W2", "e (k p) f -> p (e k) f"), expert1("L1_ffn_b1_f", "e p k -> p (e k)"),
                  ACT.Gelu, lambda t, pair, q: sh.share[:, q:q + 1], sh.xn)
        stage_norm(nc, sh, "n8", source=sh.xn, to=sh.work, turn=False)
        stage_rows(nc, sh, "r8", a["L1_ffn_gamma"], a["L1_ffn_beta"], into=sh.x, out=out)


def kernel(**inputs):
    import numpy as np
    import concourse.bacc as bacc
    from concourse.bass_utils import run_bass_kernel_spmd

    given = {name: np.asarray(array) for name, array in inputs.items()}

    def by_feature(v, parts=()):
        v = v.reshape(*parts, -1, P)
        return np.swapaxes(v, -1, -2)

    laid = {name: given[name] for name in (
        "x", "src", "dst", "edge_weight", "edge_attr_64", "L0_gnn_eps_weight", "L0_mix_W_out", "L0_ffn_Wg", "L0_ffn_bg",
        "L0_ffn_bias", "L0_ffn_W1", "L0_ffn_W2", "L0_ffn_b2", "L1_gnn_bq", "L1_gnn_bk", "L1_gnn_bv",
        "L1_gnn_We", "L1_gnn_Wo", "L1_gnn_bo", "L1_gnn_W1", "L1_gnn_W2", "L1_gnn_b2", "L1_gnn_alpha",
        "L1_gnn_beta", "L1_mix_Wq", "L1_mix_Wk", "L1_mix_Wv", "L1_mix_Wo", "L1_mix_bo", "L1_mix_W1", "L1_mix_W2",
        "L1_mix_b2", "L1_mix_ln1_g", "L1_mix_ln1_b", "L1_mix_ln2_g", "L1_mix_ln2_b", "L1_ffn_Wr", "L1_ffn_br",
        "L1_ffn_W1", "L1_ffn_W2", "L1_ffn_b2", "L1_ffn_gamma", "L1_ffn_beta")}
    for name in ("L0_gnn_gamma1", "L0_gnn_beta1", "L0_gnn_gamma_h", "L0_gnn_beta_h", "L0_mix_b_out",
                 "L1_mix_bq", "L1_mix_bk", "L1_mix_bv", "L1_mix_ln1_g", "L1_mix_ln1_b", "L1_gnn_ln1_g",
                 "L1_gnn_ln1_b", "L1_gnn_ln2_g", "L1_gnn_ln2_b"):
        laid[name + "_f"] = by_feature(given[name])
    laid["L0_ffn_b1_f"] = by_feature(given["L0_ffn_b1"], (8,))
    laid["L1_ffn_b1_f"] = by_feature(given["L1_ffn_b1"], (8,))
    laid["L1_mix_b1_f"] = by_feature(given["L1_mix_b1"], (2,))
    laid["L1_gnn_b1_f"] = by_feature(given["L1_gnn_b1"], (2,))
    laid["ef_t"] = np.zeros((ED, EP), np.float32)
    laid["ef_t"][:, 0:E] = given["edge_attr_64"].T
    laid["L1_gnn_be"] = given["L1_gnn_be"].reshape(1, DH)
    laid["L1_gnn_Wqkv"] = np.concatenate([given["L1_gnn_" + w] for w in ("Wq", "Wk", "Wv")], axis=1)
    laid["L0_gnn_w1_t"], laid["L0_gnn_w2_t"] = given["L0_gnn_w1"].T, given["L0_gnn_w2"].T
    qkv = given["L0_mix_W_qkv"]
    laid["L0_mix_Wq_t"], laid["L0_mix_Wk"], laid["L0_mix_Wv"] = qkv[:, 0:P].T, qkv[:, P:2 * P], qkv[:, 2 * P:3 * P]

    nc = bacc.Bacc("TRN2", target_bir_lowering=False, num_devices=1)
    arrays, args = {}, {}
    for name, array in laid.items():
        array = np.ascontiguousarray(array)
        arrays[f"in_{name}_dram"] = array
        args[name] = nc.dram_tensor(f"in_{name}_dram", array.shape, mybir.dt.from_np(array.dtype),
                                    kind="ExternalInput").ap()
    out = nc.dram_tensor("out_0_dram", (N, D), F32, kind="ExternalOutput").ap()
    build(nc, args, out)
    result = run_bass_kernel_spmd(nc, [arrays], core_ids=[0])
    return np.asarray(result.results[0]["out_0_dram"])
```
